# Optimizing a Trainium2 kernel written in Bass

```python
import numpy as np
import jax
import jax.numpy as jnp

def _softmax(x, axis=-1):
    return jax.nn.softmax(x, axis=axis)

def _gelu(x):
    return jax.nn.gelu(x, approximate=True)

def _silu(x):
    return jax.nn.silu(x)

def _sigmoid(x):
    return jax.nn.sigmoid(x)

def _layernorm(x, axis=-1, eps=1e-05):
    m = jnp.mean(x, axis=axis, keepdims=True)
    v = jnp.var(x, axis=axis, keepdims=True)
    return (x - m) / jnp.sqrt(v + eps)

def _scatter_add(tgt, idx, src, axis=0):
    return tgt.at[idx].add(src)

def _segment_sum(src, seg, n):
    return jax.ops.segment_sum(src, seg, n)
kernel_name = 'mk_macaron_d2_jaxref_r4_1ac6cd'

def setup_inputs(seed: int=0):
    np.random.seed(seed)
    _w = jnp.asarray

    def _L0_attn_setup():
        import jax, jax.numpy as jnp
        import numpy as np
        DIM = 256
        HEADS = 16
        HDIM = DIM // HEADS
        CHUNK = 64
        RES_SCALE = float(1.0 / np.sqrt(2.0))
        EPS_FP32 = float(np.finfo(np.float32).eps)

        def _rms(x, eps):
            return x * jax.lax.rsqrt(jnp.mean(x * x, axis=-1, keepdims=True) + eps)

        def _mixer(x, in_proj_w, out_proj_w):
            B, S, D = x.shape
            proj = x @ in_proj_w.T
            q, k, v, a, g = jnp.split(proj, 5, axis=-1)
            rs = lambda t: t.reshape(B, S, HEADS, HDIM)
            q, k, v, a, g = map(rs, (q, k, v, a, g))
            q = _rms(q, EPS_FP32)
            k = jnp.tanh(k)
            a = jnp.clip(jax.nn.sigmoid(a + 2.0), 0.6, 0.9995)
            u = k * v
            nC = S // CHUNK
            a_c = jnp.moveaxis(a.reshape(B, nC, CHUNK, HEADS, HDIM), 1, 0)
            u_c = jnp.moveaxis(u.reshape(B, nC, CHUNK, HEADS, HDIM), 1, 0)

            def step(state, inp):
                ac, uc = inp
                prefix = jnp.cumprod(ac, axis=1)
                acc = jnp.cumsum(uc / jnp.maximum(prefix, 1e-06), axis=1)
                states = prefix * (state[:, None] + acc)
                return (states[:, -1], states)
            state0 = jnp.zeros((B, HEADS, HDIM), jnp.float32)
            _, states = jax.lax.scan(step, state0, (a_c, u_c))
            memory = jnp.moveaxis(states, 0, 1).reshape(B, S, HEADS, HDIM)
            gate = jax.nn.sigmoid(g)
            y = gate * (q * memory) + (1.0 - gate) * v
            return y.reshape(B, S, D) @ out_proj_w.T
        key = jax.random.key(seed)
        ks = jax.random.split(key, 5)
        s = 0.02
        return {'x': jax.random.normal(ks[0], (2, 1024, DIM), jnp.float32), 'norm1_w': jnp.ones((DIM,), jnp.float32), 'norm2_w': jnp.ones((DIM,), jnp.float32), 'in_proj_w': jax.random.normal(ks[1], (5 * DIM, DIM), jnp.float32) * s, 'out_proj_w': jax.random.normal(ks[2], (DIM, DIM), jnp.float32) * s, 'fc_w': jax.random.normal(ks[3], (1024, DIM), jnp.float32) * s, 'proj_w': jax.random.normal(ks[4], (DIM, 1024), jnp.float32) * s}
    _L0_attn_in = _L0_attn_setup()

    def _L0_ffn_setup():
        import jax, jax.numpy as jnp
        import numpy as np
        TOPK = 8
        BN_EPS = 1e-05
        key = jax.random.key(seed)
        ks = jax.random.split(key, 5)
        b, n, d = (2, 256, 256)
        h, nk, kd = (8, 64, 128)
        ne = nk * nk
        scale = 0.02
        return {'inputs': jax.random.normal(ks[0], (b, n, d), jnp.float32), 'gamma': jnp.ones((d,), jnp.float32), 'beta': jnp.zeros((d,), jnp.float32), 'w_q': jax.random.normal(ks[1], (2 * h * kd, d), jnp.float32) * scale, 'keys': jax.random.normal(ks[2], (h, nk, 2, kd), jnp.float32) * scale, 'key_in': jax.random.normal(ks[3], (ne, d), jnp.float32) * scale, 'key_out': jax.random.normal(ks[4], (ne, d), jnp.float32) * scale}
    _L0_ffn_in = _L0_ffn_setup()

    def _L1_attn_setup():
        import jax, jax.numpy as jnp
        import numpy as np
        EMBED = 256
        N_HEAD = 16
        HEAD_DIM = EMBED // N_HEAD
        key = jax.random.key(seed)
        ks = jax.random.split(key, 9)

        def xavier(k, shape, fan_in, fan_out):
            bound = float(np.sqrt(6.0 / (fan_in + fan_out)))
            return jax.random.uniform(k, shape, jnp.float32, -bound, bound)
        x = jax.random.normal(ks[0], (4, 512, EMBED), jnp.float32)
        wq = xavier(ks[1], (N_HEAD, EMBED, HEAD_DIM), EMBED, HEAD_DIM)
        wk = xavier(ks[2], (N_HEAD, EMBED, HEAD_DIM), EMBED, HEAD_DIM)
        wv = xavier(ks[3], (N_HEAD, EMBED, HEAD_DIM), EMBED, HEAD_DIM)
        bq = jnp.zeros((N_HEAD, 1, HEAD_DIM), jnp.float32)
        bk = jnp.zeros((N_HEAD, 1, HEAD_DIM), jnp.float32)
        bv = jnp.zeros((N_HEAD, 1, HEAD_DIM), jnp.float32)
        bnd = 1.0 / float(np.sqrt(EMBED))
        wo = jax.random.uniform(ks[4], (EMBED, EMBED), jnp.float32, -bnd, bnd)
        bo = jax.random.uniform(ks[5], (EMBED,), jnp.float32, -bnd, bnd)
        return {'x': x, 'wq': wq, 'bq': bq, 'wk': wk, 'bk': bk, 'wv': wv, 'bv': bv, 'wo': wo, 'bo': bo}
    _L1_attn_in = _L1_attn_setup()

    def _L1_ffn_setup():
        import jax, jax.numpy as jnp
        import numpy as np
        B, S, D, E, K = (4, 512, 256, 8, 2)
        EPS, W_THRES, TEMP = (0.0001, 0.1, 1.0)
        key = jax.random.key(seed)
        k1, k2, k3, k4, k5 = jax.random.split(key, 5)
        x = jax.random.normal(k1, (B, S, D), dtype=jnp.float32)
        gate_W = jax.random.normal(k2, (D, E), dtype=jnp.float32) * 0.02
        gate_b = jnp.zeros((E,), dtype=jnp.float32)
        expert_W = jax.random.normal(k3, (E, D, D), dtype=jnp.float32) * 0.02
        expert_b = jnp.zeros((E, D), dtype=jnp.float32)
        return {'x': x, 'gate_W': gate_W, 'gate_b': gate_b, 'expert_W': expert_W, 'expert_b': expert_b}
    _L1_ffn_in = _L1_ffn_setup()
    _d = {'L0_attn_x': _L0_attn_in['x'], 'L0_attn_norm1_w': _L0_attn_in['norm1_w'], 'L0_attn_norm2_w': _L0_attn_in['norm2_w'], 'L0_attn_in_proj_w': _L0_attn_in['in_proj_w'], 'L0_attn_out_proj_w': _L0_attn_in['out_proj_w'], 'L0_attn_fc_w': _L0_attn_in['fc_w'], 'L0_attn_proj_w': _L0_attn_in['proj_w'], 'L0_ffn_gamma': _L0_ffn_in['gamma'], 'L0_ffn_beta': _L0_ffn_in['beta'], 'L0_ffn_w_q': _L0_ffn_in['w_q'], 'L0_ffn_keys': _L0_ffn_in['keys'], 'L0_ffn_key_in': _L0_ffn_in['key_in'], 'L0_ffn_key_out': _L0_ffn_in['key_out'], 'L1_attn_wq': _L1_attn_in['wq'], 'L1_attn_bq': _L1_attn_in['bq'], 'L1_attn_wk': _L1_attn_in['wk'], 'L1_attn_bk': _L1_attn_in['bk'], 'L1_attn_wv': _L1_attn_in['wv'], 'L1_attn_bv': _L1_attn_in['bv'], 'L1_attn_wo': _L1_attn_in['wo'], 'L1_attn_bo': _L1_attn_in['bo'], 'L1_ffn_gate_W': _L1_ffn_in['gate_W'], 'L1_ffn_gate_b': _L1_ffn_in['gate_b'], 'L1_ffn_expert_W': _L1_ffn_in['expert_W'], 'L1_ffn_expert_b': _L1_ffn_in['expert_b']}
    _x0 = _d['L0_attn_x']
    _d['L0_attn_x'] = jax.random.normal(jax.random.fold_in(jax.random.key(seed), 1), (2, 2048, 256), dtype=_x0.dtype)
    del _x0
    return _d

def reference(L0_attn_x, L0_attn_norm1_w, L0_attn_norm2_w, L0_attn_in_proj_w, L0_attn_out_proj_w, L0_attn_fc_w, L0_attn_proj_w, L0_ffn_gamma, L0_ffn_beta, L0_ffn_w_q, L0_ffn_keys, L0_ffn_key_in, L0_ffn_key_out, L1_attn_wq, L1_attn_bq, L1_attn_wk, L1_attn_bk, L1_attn_wv, L1_attn_bv, L1_attn_wo, L1_attn_bo, L1_ffn_gate_W, L1_ffn_gate_b, L1_ffn_expert_W, L1_ffn_expert_b):

    def _L0_attn_ref(x, norm1_w, norm2_w, in_proj_w, out_proj_w, fc_w, proj_w):
        import jax, jax.numpy as jnp
        import numpy as np
        DIM = 256
        HEADS = 16
        HDIM = DIM // HEADS
        CHUNK = 64
        RES_SCALE = float(1.0 / np.sqrt(2.0))
        EPS_FP32 = float(np.finfo(np.float32).eps)

        def _rms(x, eps):
            return x * jax.lax.rsqrt(jnp.mean(x * x, axis=-1, keepdims=True) + eps)

        def _mixer(x, in_proj_w, out_proj_w):
            B, S, D = x.shape
            proj = x @ in_proj_w.T
            q, k, v, a, g = jnp.split(proj, 5, axis=-1)
            rs = lambda t: t.reshape(B, S, HEADS, HDIM)
            q, k, v, a, g = map(rs, (q, k, v, a, g))
            q = _rms(q, EPS_FP32)
            k = jnp.tanh(k)
            a = jnp.clip(jax.nn.sigmoid(a + 2.0), 0.6, 0.9995)
            u = k * v
            nC = S // CHUNK
            a_c = jnp.moveaxis(a.reshape(B, nC, CHUNK, HEADS, HDIM), 1, 0)
            u_c = jnp.moveaxis(u.reshape(B, nC, CHUNK, HEADS, HDIM), 1, 0)

            def step(state, inp):
                ac, uc = inp
                prefix = jnp.cumprod(ac, axis=1)
                acc = jnp.cumsum(uc / jnp.maximum(prefix, 1e-06), axis=1)
                states = prefix * (state[:, None] + acc)
                return (states[:, -1], states)
            state0 = jnp.zeros((B, HEADS, HDIM), jnp.float32)
            _, states = jax.lax.scan(step, state0, (a_c, u_c))
            memory = jnp.moveaxis(states, 0, 1).reshape(B, S, HEADS, HDIM)
            gate = jax.nn.sigmoid(g)
            y = gate * (q * memory) + (1.0 - gate) * v
            return y.reshape(B, S, D) @ out_proj_w.T
        h1 = norm1_w * _rms(x, 1e-06)
        x = x + RES_SCALE * _mixer(h1, in_proj_w, out_proj_w)
        h2 = norm2_w * _rms(x, 1e-06)
        mlp = jax.nn.silu(h2 @ fc_w.T) @ proj_w.T
        return x + RES_SCALE * mlp

    def _L0_ffn_ref(inputs, gamma, beta, w_q, keys, key_in, key_out):
        import jax, jax.numpy as jnp
        import numpy as np
        TOPK = 8
        BN_EPS = 1e-05
        b, n, d = inputs.shape
        h, nk, _, kd = keys.shape
        k = TOPK
        x = inputs.reshape(b * n, d)
        mu = jnp.mean(x, axis=0)
        var = jnp.mean(jnp.square(x - mu), axis=0)
        xn = (x - mu) * jax.lax.rsqrt(var + BN_EPS) * gamma + beta
        q = (xn @ w_q.T).reshape(b, n, 2, h, kd).transpose(2, 0, 1, 3, 4)
        sim = jnp.einsum('pbnhd,hkpd->pbnhk', q, keys)
        s, i = jax.lax.top_k(sim, k)
        sx, sy = (s[0], s[1])
        ix, iy = (i[0], i[1])
        all_scores = (sx[..., :, None] + sy[..., None, :]).reshape(b, n, h, k * k)
        all_idx = (ix[..., :, None] * nk + iy[..., None, :]).reshape(b, n, h, k * k)
        scores, pk = jax.lax.top_k(all_scores, k)
        idx = jnp.take_along_axis(all_idx, pk, axis=-1)
        w_down = key_in[idx]
        w_up = key_out[idx]
        o = jnp.einsum('bnd,bnhkd->bnhk', inputs, w_down)
        o = jax.nn.gelu(o, approximate=False) * jax.nn.softmax(scores, axis=-1)
        return jnp.einsum('bnhk,bnhkd->bnd', o, w_up)

    def _L1_attn_ref(x, wq, bq, wk, bk, wv, bv, wo, bo):
        import jax, jax.numpy as jnp
        import numpy as np
        EMBED = 256
        N_HEAD = 16
        HEAD_DIM = EMBED // N_HEAD
        q = jnp.einsum('bsd,hde->bhse', x, wq) + bq
        k = jnp.einsum('bsd,hde->bhse', x, wk) + bk
        v = jnp.einsum('bsd,hde->bhse', x, wv) + bv
        scale = 1.0 / jnp.sqrt(jnp.asarray(q.shape[-1], q.dtype))
        scores = jax.nn.softmax(jnp.einsum('bhse,bhte->bhst', q, k) * scale, axis=-1)
        att = jnp.einsum('bhst,bhte->bhse', scores, v)
        b, h, s, e = att.shape
        att = att.transpose(0, 2, 1, 3).reshape(b, s, h * e)
        return att @ wo.T + bo

    def _L1_ffn_ref(x, gate_W, gate_b, expert_W, expert_b):
        import jax, jax.numpy as jnp
        import numpy as np
        B, S, D, E, K = (4, 512, 256, 8, 2)
        EPS, W_THRES, TEMP = (0.0001, 0.1, 1.0)
        scores = jnp.maximum((x @ gate_W + gate_b) / TEMP, EPS)
        p = jax.nn.softmax(scores, axis=-1)
        _, topk_idx = jax.lax.top_k(p, K)
        topk_mask = jax.nn.one_hot(topk_idx, E, dtype=p.dtype).sum(-2) > 0
        w = jnp.maximum(p, W_THRES)
        w_gather = jnp.take_along_axis(w, topk_idx, axis=-1)
        total = jax.lax.stop_gradient(w_gather.sum(-1, keepdims=True))
        w = w / total
        comb = jnp.where(topk_mask, w, jnp.zeros_like(w))
        y = jnp.einsum('bsd,edf->bsef', x, expert_W) + expert_b
        out = jnp.einsum('bsef,bse->bsf', y, comb) / K
        return out
    x = L0_attn_x
    x = x + 0.5 * _L0_ffn_ref(_layernorm(x, axis=-1), L0_ffn_gamma, L0_ffn_beta, L0_ffn_w_q, L0_ffn_keys, L0_ffn_key_in, L0_ffn_key_out)
    x = x + _L0_attn_ref(_layernorm(x, axis=-1), L0_attn_norm1_w, L0_attn_norm2_w, L0_attn_in_proj_w, L0_attn_out_proj_w, L0_attn_fc_w, L0_attn_proj_w)
    x = x + 0.5 * _L0_ffn_ref(_layernorm(x, axis=-1), L0_ffn_gamma, L0_ffn_beta, L0_ffn_w_q, L0_ffn_keys, L0_ffn_key_in, L0_ffn_key_out)
    x = x + 0.5 * _L1_ffn_ref(_layernorm(x, axis=-1), L1_ffn_gate_W, L1_ffn_gate_b, L1_ffn_expert_W, L1_ffn_expert_b)
    x = x + _L1_attn_ref(_layernorm(x, axis=-1), L1_attn_wq, L1_attn_bq, L1_attn_wk, L1_attn_bk, L1_attn_wv, L1_attn_bv, L1_attn_wo, L1_attn_bo)
    x = x + 0.5 * _L1_ffn_ref(_layernorm(x, axis=-1), L1_ffn_gate_W, L1_ffn_gate_b, L1_ffn_expert_W, L1_ffn_expert_b)
    return x

_drawn_inputs = setup_inputs


def setup_inputs(seed=0):
    import zlib

    import numpy as np

    out = dict(_drawn_inputs(seed))
    spreads = {'L0_attn_norm1_w': (1.0, 0.6),
     'L0_attn_norm2_w': (1.0, 0.6),
     'L0_ffn_gamma': (1.0, 0.6),
     'L0_ffn_beta': (0.0, 0.8),
     'L1_attn_bq': (0.0, 0.8),
     'L1_attn_bk': (0.0, 0.8),
     'L1_attn_bv': (0.0, 0.279),
     'L1_ffn_gate_b': (0.0, 0.324),
     'L1_ffn_expert_b': (0.0, 0.445)}
    factors = {'L0_ffn_w_q': 8.0,
     'L0_ffn_keys': 8.0,
     'L0_ffn_key_in': 8.0,
     'L0_ffn_key_out': 8.0,
     'L1_attn_bo': 3.031}
    for name, (base, spread) in spreads.items():
        noise = np.random.default_rng([zlib.crc32(name.encode()), seed]).standard_normal(out[name].shape)
        drawn = base * np.exp(spread * noise) if base else spread * noise
        out[name] = jnp.asarray(drawn.astype(out[name].dtype))
    for name, factor in factors.items():
        out[name] = (out[name] * factor).astype(out[name].dtype)
    return out
```

```python
from contextlib import ExitStack

import numpy as np

import concourse.bass as bass
from concourse import mybir

F32 = mybir.dt.float32
F16 = mybir.dt.float16
BF16 = mybir.dt.bfloat16
U32 = mybir.dt.uint32
ALU = mybir.AluOpType
ACT = mybir.ActivationFunctionType
AX_X = mybir.AxisListType.X

P = 128
D = 256
DH = D // P
LN_EPS = 1e-5


def static(v):
    return isinstance(v, int)


def wait_count(eng, sem, count):
    if static(count) and count <= 0:
        return
    eng.wait_ge(sem, count)


def one(i):
    return slice(i, i + 1) if static(i) else bass.ds(i, 1)


def tile_of(buf, i):
    if static(i):
        return buf[:, i, :]
    return buf[:, bass.ds(i, 1), :].rearrange("p a n -> p (a n)")


class Chip:

    def __init__(self, nc, name):
        self.nc, self.name, self.stack, self.sems = nc, name, ExitStack(), []

    def __enter__(self):
        self.stack.__enter__()
        return self

    def __exit__(self, *error):
        if error[0] is None and self.sems:
            self.nc.clear_and_free_semaphores(self.sems)
            self.nc.all_engine_barrier()
        return self.stack.__exit__(*error)

    def sb(self, name, shape, dt=F32):
        return self.stack.enter_context(self.nc.sbuf_tensor(f"{self.name}_{name}", shape, dt))

    def ps(self, name, shape, dt=F32):
        return self.stack.enter_context(self.nc.psum_tensor(f"{self.name}_{name}", shape, dt))

    def sem(self, name):
        self.sems.append(self.nc.alloc_semaphore(name=f"{self.name}_{name}"))
        return self.sems[-1]


def make_identities(nc, *idents):
    with Chip(nc, "ident") as c:
        zeroed = c.sem("zeroed")
        with nc.Block() as block:
            @block.gpsimd
            def _(pool):
                for m in idents:
                    pool.memset(m[:], 0.0).then_inc(zeroed, 1)
                pool.wait_ge(zeroed, len(idents))
                for m in idents:
                    pool.affine_select(out=m[:], in_=m[:], compare_op=ALU.not_equal, fill=1.0,
                                       base=0, pattern=[[-1, P]], channel_multiplier=1)


def row_statistics(nc, name, x, NT, mean, rstd, var_eps=None):
    with Chip(nc, name + "_st") as c:
        st = c.sb("st", [P, NT, 6])
        w = [c.sb(f"w{i}", [P, NT]) for i in range(4)]
        var_ready, root_ready = c.sem("var_ready"), c.sem("root_ready")
        with nc.Block() as block:
            @block.vector
            def _(dve):
                with dve.Fori(0, NT // 4) as i:
                    for k in range(4):
                        dve.bn_stats(tile_of(st, 4 * i + k), tile_of(x, 4 * i + k))
                dve.drain()
                m0, v0, m1, v1 = (st[:, :, k] for k in (1, 2, 4, 5))
                dve.tensor_tensor(w[0][:], m0, m1, ALU.add)
                dve.tensor_tensor(w[1][:], m0, m1, ALU.subtract)
                dve.tensor_tensor(w[2][:], v0, v1, ALU.add)
                dve.drain()
                dve.tensor_scalar(mean[:], w[0][:], 0.5, None, ALU.mult)
                dve.tensor_tensor(w[3][:], w[1][:], w[1][:], ALU.mult)
                dve.tensor_scalar(w[2][:], w[2][:], 1.0 / D, LN_EPS, ALU.mult, ALU.add)
                dve.drain()
                dve.scalar_tensor_tensor(out=w[1][:], in0=w[3][:], scalar=0.25, in1=w[2][:],
                                         op0=ALU.mult, op1=ALU.add).then_inc(var_ready, 1)
                dve.wait_ge(root_ready, 1)
                dve.reciprocal(rstd[:], w[0][:])
                if var_eps is not None:
                    dve.tensor_copy(var_eps[:], w[1][:])
                dve.drain()
                newton(dve, rstd[:], w[1][:], w[2][:])

            @block.scalar
            def _(act):
                act.wait_ge(var_ready, 1)
                act.activation(w[0][:], w[1][:], ACT.Sqrt).then_inc(root_ready, 1)


def newton(dve, r, v, tmp):
    dve.tensor_tensor(tmp, r, r, ALU.mult)
    dve.drain()
    dve.tensor_tensor(tmp, tmp, v, ALU.mult)
    dve.drain()
    dve.tensor_scalar(tmp, tmp, -0.5, 1.5, ALU.mult, ALU.add)
    dve.drain()
    dve.tensor_tensor(r, r, tmp, ALU.mult)
    dve.drain()



def peer_ffn(nc, name, x, ident, ident16, NT, w, yT_dram):
    gamma, beta, w_q, keysT, key_inT, key_out = w
    H, K, NK, KD = 8, 8, 64, 128
    NE = NK * NK
    NJ = NE // P
    JG = 4
    NG = NJ // JG
    HK = H * K
    S = 2 * H * NK
    HM = P // 4
    MQ = P // 2 // NG
    WS = 4096.0
    RING = 4
    with Chip(nc, name) as c:
        keyin = c.sb("keyin", [P, DH, NE])
        keyout = c.sb("keyout", [P, NJ, D])
        wc = c.sb("wc", [P, DH, S])
        xscale, xbias = c.sb("xscale", [P, DH]), c.sb("xbias", [P, DH])
        keys_in = c.sem("keys_in")

        if True:
            with Chip(nc, name + "a") as a:
                mean, rstd = a.sb("mean", [P, NT]), a.sb("rstd", [P, NT])
                row_statistics(nc, name, x, NT, mean, rstd)
                wq = a.sb("wq", [P, 2 * H, D])
                kT = a.sb("kT", [P, 2 * H, NK])
                gb = a.sb("gb", [P, 2, DH])
                y = a.sb("y", [P, 2, D])
                yT = a.sb("yT", [P, 2, D])
                bst = a.sb("bst", [P, DH, NT, 6])
                mv = a.sb("mv", [P, DH, 2])
                rt, rv, rtmp = a.sb("rt", [P, DH]), a.sb("rv", [P, DH]), a.sb("rtmp", [P, DH])
                psT = a.ps("psT", [P, 2, 512])
                psW = a.ps("psW", [P, 2, 512])
                w_in, gb_in = a.sem("w_in"), a.sem("gb_in")
                y_ready, yT_ready = a.sem("y_ready"), a.sem("yT_ready")
                transposed, stats_done = a.sem("transposed"), a.sem("stats_done")
                stored = [a.sem("stored0"), a.sem("stored1")]
                var_ready, root_ready = a.sem("bvar_ready"), a.sem("broot_ready")
                folded, fold_copied = a.sem("folded"), a.sem("fold_copied")
                with nc.Block() as block:
                    @block.sync
                    def _(sp):
                        sp.dma_start(wq[:], w_q.rearrange("(r k) d -> k r d", k=KD)).then_inc(w_in, 16)
                        sp.dma_start(kT[:], keysT).then_inc(w_in, 16)
                        sp.dma_start(gb[:, 0, :], gamma).then_inc(gb_in, 16)
                        sp.dma_start(gb[:, 1, :], beta).then_inc(gb_in, 16)
                        sp.dma_start(keyin[:], key_inT).then_inc(keys_in, 16)
                        sp.dma_start(keyout[:], key_out.rearrange("(c j) d -> c j d", j=NJ)).then_inc(keys_in, 16)
                        with sp.Fori(0, NT // 2) as i:
                            for k in range(2):
                                sp.wait_ge(yT_ready, 2 * i + k + 1)
                                sp.dma_start(yT_dram[bass.ds(2 * i + k, 1), :, :].rearrange("a p n -> (a p) n"),
                                             yT[:, k, :]).then_inc(stored[k], 16)
                        for k in range(2):
                            sp.wait_ge(stored[k], 16 * (NT // 2))

                    @block.vector
                    def _(dve):
                        def y_tile(t, k):
                            wait_count(dve, transposed, t - 1)
                            dve.tensor_scalar(y[:, k, :], tile_of(x, t), mean[:, one(t)], rstd[:, one(t)],
                                              ALU.subtract, ALU.mult).then_inc(y_ready, 1)

                        def stats_tile(t, k):
                            dve.wait_ge(yT_ready, t + 1)
                            for h in range(DH):
                                st = bst[:, h, t, :] if static(t) else \
                                    bst[:, h, bass.ds(t, 1), :].rearrange("p a n -> p (a n)")
                                ins = dve.bn_stats(st, yT[:, k, h * P:(h + 1) * P])
                            ins.then_inc(stats_done, 1)

                        y_tile(0, 0)
                        y_tile(1, 1)
                        with dve.Fori(0, NT // 2 - 1) as i:
                            for k in range(2):
                                stats_tile(2 * i + k, k)
                                y_tile(2 * i + k + 2, k)
                        stats_tile(NT - 2, 0)
                        stats_tile(NT - 1, 1)
                        dve.drain()
                        for h in range(DH):
                            dve.bn_aggr(mv[:, h, :], bst[:, h, :, :].rearrange("p t n -> p (t n)"))
                        dve.drain()
                        dve.tensor_scalar(rv[:], mv[:, :, 1], 1e-5, None, ALU.add).then_inc(var_ready, 1)
                        dve.wait_ge(root_ready, 1)
                        dve.reciprocal(xscale[:], rt[:])
                        dve.drain()
                        newton(dve, xscale[:], rv[:], rtmp[:])
                        dve.wait_ge(gb_in, 32)
                        dve.tensor_tensor(xscale[:], xscale[:], gb[:, 0, :], ALU.mult)
                        dve.drain()
                        dve.tensor_tensor(rt[:], mv[:, :, 0], xscale[:], ALU.mult)
                        dve.drain()
                        dve.tensor_tensor(xbias[:], gb[:, 1, :], rt[:], ALU.subtract)

                    @block.tensor
                    def _(pe):
                        pe.wait_ge(w_in, 32)
                        for n in range(2 * DH):
                            hd, half = n // 2, n % 2
                            if n >= 2:
                                pe.wait_ge(fold_copied, n - 1)
                            for r in range(H):
                                mm = pe.matmul(psW[:, n % 2, r * NK:(r + 1) * NK],
                                               wq[:, half * H + r, hd * P:(hd + 1) * P],
                                               kT[:, half * H + r, :], start=True, stop=True)
                            mm.then_inc(folded, 1)
                        with pe.Fori(0, NT // 2) as i:
                            for k in range(2):
                                pe.wait_ge(y_ready, 2 * i + k + 1)
                                if k == 0:
                                    pe.wait_ge(yT_ready, 2 * i)
                                for h in range(DH):
                                    mm = pe.transpose(psT[:, k, h * P:(h + 1) * P],
                                                      y[:, k, h * P:(h + 1) * P], ident[:])
                                mm.then_inc(transposed, 1)

                    @block.scalar
                    def _(act):
                        for n in range(2 * DH):
                            act.wait_ge(folded, n + 1)
                            act.activation(wc[:, n // 2, (n % 2) * 512:(n % 2 + 1) * 512], psW[:, n % 2, :],
                                           ACT.Copy).then_inc(fold_copied, 1)

                        def yT_tile(t, k, i):
                            act.wait_ge(transposed, t + 1)
                            wait_count(act, stats_done, t - 1)
                            wait_count(act, stored[k], 16 * i)
                            act.activation(yT[:, k, :], psT[:, k, 0:D], ACT.Copy).then_inc(yT_ready, 1)

                        yT_tile(0, 0, 0)
                        yT_tile(1, 1, 0)
                        with act.Fori(1, NT // 2) as i:
                            for k in range(2):
                                yT_tile(2 * i + k, k, i)
                        act.wait_ge(var_ready, 1)
                        act.activation(rt[:], rv[:], ACT.Sqrt).then_inc(root_ready, 1)

        with Chip(nc, name + "b") as b:
            yTd = b.sb("yTd", [P, 2, DH, P])
            yTs = b.sb("yTs", [P, 2, DH, P])
            xnT = b.sb("xnT", [P, DH, P])
            sim = b.sb("sim", [P, S])
            top = b.sb("top", [P, 2 * H, K])
            topi = b.sb("topi", [P, 2 * H, K], U32)
            topf = b.sb("topf", [P, 2 * H, K])
            pair = b.sb("pair", [P, H, K, K])
            best = b.sb("best", [P, H, K])
            pick = b.sb("pick", [P, H, K], U32)
            rank = b.sb("rank", [P, 2, HK], U32)
            hot = b.sb("hot", [P, 2, HK, K], F16)
            ixy = b.sb("ixy", [P, 2, HK])
            upper = b.sb("upper", [P, HK])
            hi = b.sb("hi", [P, HK])
            lo = b.sb("lo", [P, HK])
            expo = b.sb("expo", [P, H, K])
            ex = b.sb("ex", [P, H, K])
            total = b.sb("total", [P, H])
            inv = b.sb("inv", [P, H])
            wt = b.sb("wt", [P, HK])
            wrest = b.sb("wrest", [P, HK])
            NC = 5
            cat = b.sb("cat", [P, NC, 2, HK], F16)
            catT = b.sb("catT", [P, 2, NC, P // 2], F16)
            iota8 = b.sb("iota8", [P, K], U32)
            iota64 = b.sb("iota64", [P, NK, HM], F16)
            left = b.sb("left", [P, 2, P, HM], F16)
            right = b.sb("right", [P, 2, 2, 2 * NJ, HM], F16)
            A = b.sb("A", [P, 2, NJ, P])
            G = b.sb("G", [P, RING, JG * P])
            psO = b.ps("psO", [P, 2, 512])
            psA = b.ps("psA", [P, 2, 512])
            psS = b.ps("psS", [P, 2, 512])
            psX = b.ps("psX", [P, 512])
            psI = b.ps("psI", [P, 1024], F16)

            experts_in = [b.sem("experts_in0"), b.sem("experts_in1")]
            simil_in = [b.sem("simil_in0"), b.sem("simil_in1")]
            xn_ready, sims_done, sim_ready, sim_used = (b.sem(n) for n in ("xn_ready", "sims_done", "sim_ready", "sim_used"))
            expo_ready, ex_ready, cat_ready, cat_turned, catT_ready = (
                b.sem(n) for n in ("expo_ready", "ex_ready", "cat_ready", "cat_turned", "catT_ready"))
            factors_ready, built, A_ready = b.sem("factors_ready"), b.sem("built"), b.sem("A_ready")
            o_done, gelu_done, prod_ready, prod_used, x_added = (
                b.sem(n) for n in ("o_done", "gelu_done", "prod_ready", "prod_used", "x_added"))
            consts = b.sem("consts")

            LEAD = 4

            def run(eng, step):
                for t in range(-LEAD, 2):
                    step(t, t // 2)
                with eng.Fori(1, (NT - LEAD) // 2) as i:
                    for k in range(2):
                        step(2 * i + k, i, k)
                for t in range(NT - LEAD, NT):
                    step(t, t // 2)

            def has(t):
                return not static(t) or 0 <= t < NT

            with nc.Block() as block:
                @block.gpsimd
                def _(pool):
                    pool.iota(iota8[:], [[1, K]], base=0, channel_multiplier=0)
                    pool.iota(iota64[:], [[1, NK], [0, HM]], base=0, channel_multiplier=0,
                              allow_small_or_imprecise_dtypes=True).then_inc(consts, 1)

                @block.sync
                def _(sp):
                    sp.wait_ge(keys_in, 32)

                    def step(t, i, k=None):
                        k = t % 2 if k is None else k
                        u = t + LEAD
                        if has(u):
                            wait_count(sp, xn_ready, u - 1)
                            sp.dma_start(yTs[:, k, :, :].rearrange("p h n -> p (h n)"), dram_tile(yT_dram, u)
                                         ).then_inc(simil_in[k], 16)
                        v = t + 1
                        if has(v):
                            wait_count(sp, o_done, NG * (v - 1))
                            sp.dma_start(yTd[:, 1 - k, :, :].rearrange("p h n -> p (h n)"), dram_tile(yT_dram, v)
                                         ).then_inc(experts_in[1 - k], 16)
                    run(sp, step)

                @block.tensor
                def _(pe):
                    def experts(t, g, k, i):
                        if g == 0:
                            pe.wait_ge(experts_in[k], 16 * (i + 1))
                        wait_count(pe, gelu_done, NG * t + g - 1)
                        for j in range(JG):
                            for h in range(DH):
                                jj = g * JG + j
                                mm = pe.matmul(psO[:, g % 2, j * P:(j + 1) * P], keyin[:, h, jj * P:(jj + 1) * P],
                                               yTd[:, k, h, :], start=(h == 0), stop=(h == DH - 1))
                        mm.then_inc(o_done, 1)

                    def combine(t, g):
                        pe.wait_ge(prod_ready, NG * t + g + 1)
                        if g == 0:
                            wait_count(pe, x_added, t)
                        for j in range(JG):
                            jj = g * JG + j
                            mm = pe.matmul(psX[:, 0:D], G[:, g % RING, j * P:(j + 1) * P], keyout[:, jj, :],
                                           start=(jj == 0), stop=(jj == NJ - 1))
                        mm.then_inc(prod_used, 1)

                    def build(u, q):
                        h = q // (NG // 2)
                        pe.wait_ge(factors_ready, 2 * u + h + 1)
                        wait_count(pe, A_ready, NG * u + q - 1)
                        for n in range(MQ):
                            m = (q * MQ + n) % HM
                            for part in range(2):
                                mm = pe.matmul(psA[:, q % 2, n * 2 * NJ:(n + 1) * 2 * NJ], left[:, h, :, m],
                                               right[:, h, part, :, m], start=(part == 0), stop=(part == 1))
                        mm.then_inc(built, 1)

                    def similarities(u):
                        pe.wait_ge(xn_ready, u + 1)
                        wait_count(pe, sim_ready, u)
                        for s in range(2):
                            for h in range(DH):
                                mm = pe.matmul(psS[:, s, :], xnT[:, h, :], wc[:, h, s * 512:(s + 1) * 512],
                                               start=(h == 0), stop=(h == DH - 1))
                        mm.then_inc(sims_done, 1)

                    def turn(u):
                        pe.wait_ge(cat_ready, u + 1)
                        wait_count(pe, catT_ready, u)
                        for n in range(NC):
                            mm = pe.transpose(psI[:, n * P:(n + 1) * P], cat[:, n, :, :].rearrange("p s n -> p (s n)"),
                                              ident16[:])
                        mm.then_inc(cat_turned, 1)

                    def step(t, i, k=None):
                        k = t % 2 if k is None else k
                        for g in range(NG):
                            if has(t):
                                experts(t, g, k, i)
                            if g == 1 and has(t + 2):
                                turn(t + 2)
                            if has(t + 1):
                                build(t + 1, g)
                            if g >= 2 and has(t):
                                combine(t, g - 2)
                            if g < 2 and has(t - 1) and not (static(t) and t == 0):
                                combine(t - 1, NG - 2 + g)
                            if g == 5 and has(t + LEAD):
                                similarities(t + LEAD)
                    run(pe, step)
                    combine(NT - 1, NG - 2)
                    combine(NT - 1, NG - 1)

                @block.scalar
                def _(act):
                    def step(t, i, k=None):
                        k = t % 2 if k is None else k
                        u = t + LEAD
                        for g in range(NG):
                            if g == 0 and has(u):
                                act.wait_ge(simil_in[k], 16 * (i + LEAD // 2 + 1))
                                wait_count(act, sims_done, u)
                                for h in range(DH):
                                    ins = act.activation(xnT[:, h, :], yTs[:, k, h, :], ACT.Identity,
                                                         scale=xscale[:, h:h + 1], bias=xbias[:, h:h + 1])
                                ins.then_inc(xn_ready, 1)
                            if has(t):
                                act.wait_ge(o_done, NG * t + g + 1)
                                wait_count(act, prod_used, NG * t + g - RING + 1)
                                act.activation(G[:, g % RING, :], psO[:, g % 2, :], ACT.Gelu).then_inc(gelu_done, 1)
                            if g == 2 and has(t + 2):
                                v = t + 2
                                act.wait_ge(cat_turned, v + 1)
                                wait_count(act, factors_ready, 2 * v - 2)
                                for s in range(2):
                                    src = psI[64 * s:64 * s + 64, 0:NC * P].rearrange("p (n s m) -> p n s m", n=NC, s=2)
                                    ins = act.activation(catT[64 * s:64 * s + 64, k, :, :], src[:, :, s, :], ACT.Copy)
                                ins.then_inc(catT_ready, 1)
                            if has(t + 1):
                                act.wait_ge(built, NG * (t + 1) + g + 1)
                                wait_count(act, prod_ready, NG * t)
                                dst = A[:, 1 - k, :, :].rearrange("p j (s m) -> p j s m", s=2)[:, :, :, g * MQ:(g + 1) * MQ]
                                src = psA[:, g % 2, :].rearrange("p (m s j) -> p j s m", s=2, j=NJ)
                                act.activation(dst, src, ACT.Copy).then_inc(A_ready, 1)
                            if g == 6 and has(t + 3):
                                act.wait_ge(expo_ready, t + 4)
                                act.activation(ex[:], expo[:], ACT.Exp).then_inc(ex_ready, 1)
                            if g == 7 and has(u):
                                act.wait_ge(sims_done, u + 1)
                                wait_count(act, sim_used, u)
                                act.activation(sim[:], psS[:].rearrange("p a n -> p (a n)"), ACT.Copy
                                               ).then_inc(sim_ready, 1)
                    run(act, step)

                @block.vector
                def _(dve):
                    flat = lambda ap: ap.rearrange("p h k -> p (h k)")

                    def product(t, g, k):
                        dve.wait_ge(gelu_done, NG * t + g + 1)
                        if g == 0:
                            dve.wait_ge(A_ready, NG * t + NG)
                        dve.tensor_tensor(G[:, g % RING, :], G[:, g % RING, :],
                                          A[:, k, g * JG:(g + 1) * JG, :].rearrange("p j n -> p (j n)"),
                                          ALU.mult).then_inc(prod_ready, 1)

                    def factors(u, h, stage, k):
                        ms = slice(h * HM, (h + 1) * HM)
                        def row(n):
                            return catT[:, k, n, ms].unsqueeze(1).broadcast_to([P, NK, HM])
                        if stage == 0:
                            dve.wait_ge(catT_ready, u + 1)
                            wait_count(dve, built, NG * (u - 1) + (NG // 2) * (h + 1))
                            dve.tensor_tensor(left[:, h, 0:NK, :], iota64[:], row(0), ALU.is_equal)
                            dve.tensor_tensor(right[:, h, 0, :, :], iota64[:], row(2), ALU.is_equal)
                        elif stage == 1:
                            dve.tensor_tensor(left[:, h, NK:P, :], iota64[:], row(1), ALU.is_equal)
                        elif stage == 2:
                            dve.drain()
                            dve.tensor_tensor(right[:, h, 1, :, :], right[:, h, 0, :, :], row(4), ALU.mult)
                        else:
                            dve.drain()
                            dve.tensor_tensor(right[:, h, 0, :, :], right[:, h, 0, :, :], row(3), ALU.mult
                                              ).then_inc(factors_ready, 1)

                    def picks(u, g):
                        if g == 0:
                            for r in range(2 * H):
                                dve.max(top[:, r, :], sim[:, r * NK:(r + 1) * NK])
                        elif g == 1:
                            dve.drain()
                            for r in range(2 * H):
                                ins = dve.max_index(topi[:, r, :], top[:, r, :], sim[:, r * NK:(r + 1) * NK])
                            ins.then_inc(sim_used, 1)
                            dve.tensor_tensor(pair[:], top[:, 0:H, :].unsqueeze(3).broadcast_to([P, H, K, K]),
                                              top[:, H:2 * H, :].unsqueeze(2).broadcast_to([P, H, K, K]), ALU.add)
                        elif g == 2:
                            dve.drain()
                            dve.tensor_copy(topf[:], topi[:])
                            for r in range(H):
                                dve.max(best[:, r, :], pair[:, r, :, :].rearrange("p a b -> p (a b)"))
                        elif g == 3:
                            dve.drain()
                            dve.tensor_tensor(expo[:], best[:], best[:, :, 0:1].broadcast_to([P, H, K]),
                                              ALU.subtract).then_inc(expo_ready, 1)
                            for r in range(H):
                                dve.max_index(pick[:, r, :], best[:, r, :], pair[:, r, :, :].rearrange("p a b -> p (a b)"))
                        elif g == 4:
                            dve.drain()
                            dve.tensor_scalar(rank[:, 0, :], flat(pick[:]), 3, None, ALU.logical_shift_right)
                            dve.tensor_scalar(rank[:, 1, :], flat(pick[:]), K - 1, None, ALU.bitwise_and)
                            dve.drain()
                            dve.tensor_tensor(hot[:].rearrange("p a n k -> p (a n) k"),
                                              rank[:].rearrange("p a n -> p (a n)").unsqueeze(2).broadcast_to([P, 2 * HK, K]),
                                              iota8[:].unsqueeze(1).broadcast_to([P, 2 * HK, K]), ALU.is_equal)
                        elif g == 5:
                            dve.drain()
                            hv = hot[:].rearrange("p a (h r) k -> p (a h) r k", h=H)
                            dve.tensor_tensor(hv, hv, topf[:].unsqueeze(2).broadcast_to([P, 2 * H, K, K]), ALU.mult)
                        elif g == 6:
                            dve.drain()
                            dve.tensor_reduce(ixy[:].rearrange("p a n -> p (a n)"),
                                              hot[:].rearrange("p a n k -> p (a n) k"), AX_X, ALU.add)
                            dve.drain()
                            dve.tensor_scalar(upper[:], ixy[:, 1, :], float(NJ), None, ALU.is_ge)
                            dve.drain()
                            dve.scalar_tensor_tensor(out=hi[:], in0=ixy[:, 0, :], scalar=2.0, in1=upper[:],
                                                     op0=ALU.mult, op1=ALU.add)
                            dve.scalar_tensor_tensor(out=lo[:], in0=upper[:], scalar=-float(NJ), in1=ixy[:, 1, :],
                                                     op0=ALU.mult, op1=ALU.add)
                        else:
                            dve.wait_ge(ex_ready, u + 1)
                            dve.tensor_reduce(total[:], ex[:], AX_X, ALU.add)
                            twice = lambda ap: ap.unsqueeze(1).broadcast_to([P, 2, HK])
                            dve.drain()
                            wait_count(dve, cat_turned, u)
                            dve.reciprocal(inv[:], total[:])
                            dve.tensor_scalar(cat[:, 0, :, :], twice(hi[:]), 1.0, None, ALU.mult)
                            dve.tensor_scalar(cat[:, 1, :, :], twice(hi[:]), -float(NK), None, ALU.add)
                            dve.tensor_scalar(cat[:, 2, 0, :], lo[:], 1.0, None, ALU.mult)
                            dve.tensor_scalar(cat[:, 2, 1, :], lo[:], float(NJ), None, ALU.add)
                            dve.drain()
                            dve.scalar_tensor_tensor(out=wt[:].rearrange("p (h k) -> p h k", h=H), in0=ex[:], scalar=WS,
                                                     in1=inv[:].unsqueeze(2).broadcast_to([P, H, K]),
                                                     op0=ALU.mult, op1=ALU.mult)
                            dve.drain()
                            dve.tensor_scalar(cat[:, 3, :, :], twice(wt[:]), 1.0, None, ALU.mult)
                            dve.drain()
                            dve.tensor_tensor(cat[:, 4, :, :], twice(wt[:]), cat[:, 3, :, :], ALU.subtract
                                              ).then_inc(cat_ready, 1)

                    def add_x(t):
                        dve.wait_ge(prod_used, NG * t + NG)
                        xt = tile_of(x, t)
                        dve.scalar_tensor_tensor(out=xt, in0=psX[:, 0:D], scalar=0.5 / WS, in1=xt,
                                                 op0=ALU.mult, op1=ALU.add).then_inc(x_added, 1)

                    def step(t, i, k=None):
                        k = t % 2 if k is None else k
                        for g in range(NG):
                            if g == 2 and has(t - 1) and not (static(t) and t == 0):
                                add_x(t - 1)
                            if has(t):
                                product(t, g, k)
                            if g == 0 and has(t + 3):
                                dve.wait_ge(sim_ready, t + 4)
                            if g < NG // 2 and has(t + 1):
                                factors(t + 1, 1, g, 1 - k)
                            if g >= NG // 2 and has(t + 2):
                                factors(t + 2, 0, g - NG // 2, k)
                            if has(t + 3):
                                picks(t + 3, g)

                    dve.wait_ge(consts, 1)
                    run(dve, step)
                    add_x(NT - 1)



def moe_ffn(nc, name, x, ident, NT, w):
    gate_w, gate_b, expert_w, expert_b = w
    E, KTOP = 8, 2
    SCORE_EPS, W_MIN = 1e-4, 0.1
    GT = 4
    NGR = NT // GT
    DUOS = 2 * E // 2
    with Chip(nc, name) as c:
        mean, rstd = c.sb("mean", [P, NT]), c.sb("rstd", [P, NT])
        row_statistics(nc, name, x, NT, mean, rstd)
        ew = c.sb("ew", [P, DH, E * D])
        eb = c.sb("eb", [E, D])
        gw = c.sb("gw", [P, DH, E])
        gb = c.sb("gb", [1, E])
        ones = c.sb("ones", [1, P])
        iota = c.sb("iota", [P, E], U32)
        y = c.sb("y", [P, GT, D])
        yT = c.sb("yT", [P, 2, GT, DH, P])
        score = c.sb("score", [P, GT, E])
        big = c.sb("big", [P, GT])
        diff = c.sb("diff", [P, GT, E])
        ex = c.sb("ex", [P, GT, E])
        total = c.sb("total", [P, GT])
        prob = c.sb("prob", [P, GT, E])
        best = c.sb("best", [P, GT, 8])
        besti = c.sb("besti", [P, GT, 8], U32)
        chosen = c.sb("chosen", [P, 2, GT, E])
        two = c.sb("two", [P, GT, 2])
        comb = c.sb("comb", [P, 2, GT, E])
        combT = c.sb("combT", [E, GT, P])
        psY = c.ps("psY", [P, 2, 2, 512])
        psT = c.ps("psT", [P, 512])
        psL = c.ps("psL", [P, 512])
        psB = c.ps("psB", [P, 512])
        w_in, consts = c.sem("w_in"), c.sem("consts")
        y_ready, turned, turn_copied = c.sem("y_ready"), c.sem("turned"), c.sem("turn_copied")
        logits_done, diff_ready, ex_ready, comb_ready = (
            c.sem(n) for n in ("logits_done", "diff_ready", "ex_ready", "comb_ready"))
        duo_done, duo_used, bias_done, bias_added = (
            c.sem(n) for n in ("duo_done", "duo_used", "bias_done", "bias_added"))
        TURNS = 3

        def run(eng, step):
            for n in range(-1, min(2, NGR)):
                step(n, n % 2)
            if NGR > 4:
                with eng.Fori(1, (NGR - 2) // 2) as i:
                    for k in range(2):
                        step(2 * i + k, k)
            for n in range(max(NGR - 2, 2), NGR):
                step(n, n % 2)

        def has(n):
            return not static(n) or 0 <= n < NGR

        def turns_before(n):
            if static(n) and n == 0:
                return 0
            return TURNS * n - 1

        def turns_of_comb(n):
            return TURNS * n + (4 if not static(n) or n < NGR - 1 else 2)

        with nc.Block() as block:
            @block.gpsimd
            def _(pool):
                pool.iota(iota[:], [[1, E]], base=0, channel_multiplier=0)
                pool.memset(ones[:], 1.0).then_inc(consts, 1)

            @block.sync
            def _(sp):
                sp.dma_start(gw[:], gate_w.rearrange("(h p) e -> p h e", p=P)).then_inc(w_in, 16)
                sp.dma_start(gb[:], gate_b.rearrange("(a e) -> a e", a=1)).then_inc(w_in, 16)
                sp.dma_start(eb[:], expert_b).then_inc(w_in, 16)
                for h in range(DH):
                    sp.dma_start(ew[:, h, :].rearrange("p (e f) -> p e f", e=E),
                                 expert_w.rearrange("e (h p) f -> h p e f", p=P)[h]).then_inc(w_in, 16)

            @block.tensor
            def _(pe):
                pe.wait_ge(consts, 1)
                pe.wait_ge(w_in, 16 * (3 + DH))

                def turn_tiles(n, half):
                    if half == 0:
                        pe.wait_ge(y_ready, n + 1)
                    wait_count(pe, turn_copied, turns_before(n) + half)
                    for a in range(2):
                        for h in range(DH):
                            mm = pe.transpose(psT[:, (a * DH + h) * P:(a * DH + h + 1) * P],
                                              y[:, 2 * half + a, h * P:(h + 1) * P], ident[:])
                    mm.then_inc(turned, 1)

                def turn_comb(n, k):
                    pe.wait_ge(comb_ready, n + 1)
                    wait_count(pe, turn_copied, turns_of_comb(n))
                    for a in range(GT):
                        mm = pe.transpose(psT[0:E, a * P:(a + 1) * P], comb[:, k, a, :], ident[:])
                    mm.then_inc(turned, 1)

                def bias(n, half):
                    pe.wait_ge(turn_copied, turns_of_comb(n) + 1)
                    wait_count(pe, bias_added, 2 * n + half)
                    for a in range(2):
                        mm = pe.matmul(psB[:, a * D:(a + 1) * D], combT[:, 2 * half + a, :], eb[:],
                                       start=True, stop=True)
                    mm.then_inc(bias_done, 1)

                def logits(n, k):
                    pe.wait_ge(turn_copied, turns_before(n) + 2)
                    wait_count(pe, diff_ready, n)
                    for a in range(GT):
                        for h in range(DH):
                            pe.matmul(psL[:, a * E:(a + 1) * E], yT[:, k, a, h, :], gw[:, h, :],
                                      start=(h == 0), stop=False)
                        mm = pe.matmul(psL[:, a * E:(a + 1) * E], ones[:], gb[:], start=False, stop=True)
                    mm.then_inc(logits_done, 1)

                def duo(n, u, k):
                    ep, tp = u % (E // 2), u // (E // 2)
                    wait_count(pe, duo_used, DUOS * n + u - 1)
                    for a in range(2):
                        for h in range(DH):
                            mm = pe.matmul(psY[:, u % 2, a, :], yT[:, k, 2 * tp + a, h, :],
                                           ew[:, h, ep * 2 * D:(ep + 1) * 2 * D], start=(h == 0), stop=(h == DH - 1))
                    mm.then_inc(duo_done, 1)

                def step(n, k):
                    for u in range(DUOS):
                        if has(n):
                            duo(n, u, k)
                        if u in (0, 1) and has(n + 1):
                            turn_tiles(n + 1, u)
                        if u == 2 and has(n):
                            turn_comb(n, k)
                        if u in (3, 5) and has(n):
                            bias(n, (u - 3) // 2)
                        if u == 4 and has(n + 1):
                            logits(n + 1, 1 - k)
                run(pe, step)

            @block.scalar
            def _(act):
                def copy_tiles(n, half, k):
                    act.wait_ge(turned, turns_before(n) + half + 1)
                    act.activation(yT[:, k, 2 * half:2 * half + 2, :, :].rearrange("p a h n -> p (a h n)"), psT[:],
                                   ACT.Copy).then_inc(turn_copied, 1)

                def copy_comb(n):
                    act.wait_ge(turned, turns_of_comb(n) + 1)
                    wait_count(act, bias_done, 2 * n)
                    act.activation(combT[:].rearrange("e a n -> e (a n)"), psT[0:E, :], ACT.Copy
                                   ).then_inc(turn_copied, 1)

                def step(n, k):
                    if has(n + 1):
                        copy_tiles(n + 1, 0, 1 - k)
                        copy_tiles(n + 1, 1, 1 - k)
                    if has(n):
                        copy_comb(n)
                    if has(n + 1):
                        act.wait_ge(diff_ready, n + 2)
                        act.activation(ex[:], diff[:], ACT.Exp).then_inc(ex_ready, 1)
                run(act, step)

            @block.vector
            def _(dve):
                def normalise(n):
                    wait_count(dve, turned, turns_before(n - 1) + 2 if not static(n) or n > 0 else 0)
                    for a in range(GT):
                        t = GT * n + a
                        ins = dve.tensor_scalar(y[:, a, :], tile_of(x, t), mean[:, one(t)], rstd[:, one(t)],
                                                ALU.subtract, ALU.mult)
                    ins.then_inc(y_ready, 1)

                def route_scores(n):
                    dve.wait_ge(logits_done, n + 1)
                    dve.tensor_scalar(score[:].rearrange("p a e -> p (a e)"), psL[:, 0:GT * E], SCORE_EPS, None, ALU.max)
                    dve.drain()
                    dve.tensor_reduce(big[:], score[:], AX_X, ALU.max)
                    dve.drain()
                    dve.tensor_tensor(diff[:], score[:], big[:].unsqueeze(2).broadcast_to([P, GT, E]), ALU.subtract
                                      ).then_inc(diff_ready, 1)

                def route_weights(n, k):
                    wide = lambda ap: ap.unsqueeze(2).broadcast_to([P, GT, E])
                    dve.wait_ge(ex_ready, n + 1)
                    dve.tensor_reduce(total[:], ex[:], AX_X, ALU.add)
                    dve.drain()
                    dve.reciprocal(total[:], total[:])
                    dve.drain()
                    dve.tensor_tensor(prob[:], ex[:], wide(total[:]), ALU.mult)
                    dve.drain()
                    for a in range(GT):
                        dve.max(best[:, a, :], prob[:, a, :])
                    dve.drain()
                    for a in range(GT):
                        dve.max_index(besti[:, a, :], best[:, a, :], prob[:, a, :])
                    dve.tensor_scalar(two[:], best[:, :, 0:KTOP], W_MIN, None, ALU.max)
                    dve.drain()
                    for q in range(KTOP):
                        dve.tensor_tensor(chosen[:, q, :, :], iota[:].unsqueeze(1).broadcast_to([P, GT, E]),
                                          besti[:, :, q:q + 1].broadcast_to([P, GT, E]), ALU.is_equal)
                    dve.tensor_reduce(total[:], two[:], AX_X, ALU.add)
                    dve.tensor_scalar(prob[:], prob[:], W_MIN, 0.5 / KTOP, ALU.max, ALU.mult)
                    dve.drain()
                    dve.reciprocal(total[:], total[:])
                    dve.tensor_tensor(chosen[:, 0, :, :], chosen[:, 0, :, :], chosen[:, 1, :, :], ALU.add)
                    dve.drain()
                    dve.tensor_tensor(prob[:], prob[:], wide(total[:]), ALU.mult)
                    dve.drain()
                    dve.tensor_tensor(comb[:, k, :, :], prob[:], chosen[:, 0, :, :], ALU.mult).then_inc(comb_ready, 1)

                def combine(n, u, k):
                    ep, tp = u % (E // 2), u // (E // 2)
                    for q in range(2):
                        e = 2 * ep + q
                        dve.drain()
                        if q == 0:
                            dve.wait_ge(duo_done, DUOS * n + u + 1)
                        for a in range(2):
                            ta = 2 * tp + a
                            xt = tile_of(x, GT * n + ta)
                            ins = dve.scalar_tensor_tensor(out=xt, in0=psY[:, u % 2, a, q * D:(q + 1) * D],
                                                           scalar=comb[:, k, ta, e:e + 1], in1=xt,
                                                           op0=ALU.mult, op1=ALU.add)
                    ins.then_inc(duo_used, 1)

                def add_bias(n, half):
                    dve.drain()
                    dve.wait_ge(bias_done, 2 * n + half + 1)
                    t = GT * n + 2 * half
                    xt = (x[:, t:t + 2, :] if static(t) else x[:, bass.ds(t, 2), :]).rearrange("p a n -> p (a n)")
                    dve.tensor_tensor(xt, psB[:], xt, ALU.add).then_inc(bias_added, 1)

                dve.wait_ge(consts, 1)

                def step(n, k):
                    if has(n + 1):
                        normalise(n + 1)
                    for u in range(DUOS):
                        if has(n):
                            combine(n, u, k)
                        if u == 4 and has(n):
                            add_bias(n, 0)
                        if u == 5 and has(n + 1):
                            route_scores(n + 1)
                        if u == 7:
                            if has(n):
                                add_bias(n, 1)
                            if has(n + 1):
                                route_weights(n + 1, 1 - k)
                run(dve, step)



def recurrent_block(nc, name, x, ident, NT, SEQ, w):
    norm1, norm2, in_projT, out_projT, fcT, projT = w
    HD = 16
    CH = 64
    GT = 4
    SEG = GT * P
    NS = NT // GT
    NC = SEG // CH
    PARTS = 5
    F = fcT.shape[2]
    MF = F // P
    RES = float(1.0 / np.sqrt(2.0))
    QEPS = float(np.finfo(np.float32).eps)
    with Chip(nc, name) as c:
        mean, rstd, var_eps = c.sb("mean", [P, NT]), c.sb("rstd", [P, NT]), c.sb("var_eps", [P, NT])
        row_statistics(nc, name, x, NT, mean, rstd, var_eps)
        wi = c.sb("wi", [P, DH, PARTS * D])
        wo = c.sb("wo", [P, DH, D])
        wf = c.sb("wf", [P, DH, F])
        wp = c.sb("wp", [P, MF, D])
        n1, n2 = c.sb("n1", [P, DH]), c.sb("n2", [P, DH])
        scale1 = c.sb("scale1", [P, NT])
        t1, t2, t3 = c.sb("t1", [P, NT]), c.sb("t2", [P, NT]), c.sb("t3", [P, NT])
        heads = c.sb("heads", [P, P])
        goes_on = c.sb("goes_on", [P, NS])
        inside = c.sb("inside", [P, SEG])
        two_bias, q_eps, r_eps = c.sb("two_bias", [P, 1]), c.sb("q_eps", [P, 1]), c.sb("r_eps", [P, 1])
        y = c.sb("y", [P, GT, D])
        h1T = c.sb("h1T", [P, DH, SEG])
        seg = lambda n: c.sb(n, [P, DH, SEG])
        q, k, v, a, g, qq, rq = (seg(n) for n in ("q", "k", "v", "a", "g", "qq", "rq"))
        first, prefix, ratio, acc, mixed = (seg(n) for n in ("first", "prefix", "ratio", "acc", "mixed"))
        chunk_end = c.sb("chunk_end", [P, DH, NC])
        prefix_end = c.sb("prefix_end", [P, DH, NC])
        state = c.sb("state", [P, DH, NC + 1])
        x1 = c.sb("x1", [P, GT, D])
        sq = c.sb("sq", [P, D])
        ms, root2, r2, r2t = (c.sb(n, [P, GT]) for n in ("ms", "root2", "r2", "r2t"))
        h2 = c.sb("h2", [P, GT, D])
        h2T = c.sb("h2T", [P, DH, SEG])
        hid = c.sb("hid", [P, MF, SEG])
        psR = c.ps("psR", [P, 2, 512])
        psT = c.ps("psT", [P, 512])
        psX = c.ps("psX", [P, 2, 512])
        psM = c.ps("psM", [P, 2, 512])
        w_in, consts, sq1_ready, root1_ready, weights_ready = (
            c.sem(n) for n in ("w_in", "consts", "sq1_ready", "root1_ready", "weights_ready"))
        y_ready, turned, turn_copied, filled, emptied = (
            c.sem(n) for n in ("y_ready", "turned", "turn_copied", "filled", "emptied"))
        qq_ready, mixed_ready, attn_done, x1_ready, ms_ready, root2_ready, h2_ready = (
            c.sem(n) for n in ("qq_ready", "mixed_ready", "attn_done", "x1_ready", "ms_ready", "root2_ready", "h2_ready"))
        mlp_done, mlp_added = c.sem("mlp_done"), c.sem("mlp_added")
        TILES_P = PARTS * DH
        USES = TILES_P + MF + DH

        def psr_base(n):
            return 0 if static(n) and n <= 0 else USES * n - MF

        def fc_base(n):
            return psr_base(n) + (TILES_P if not static(n) or n < NS else 0)

        def rms_base(n):
            return psr_base(n) + TILES_P + (MF if not static(n) or n > 0 else 0)

        def turns_h2(n):
            return 4 * n if not static(n) or n < NS else 4 * n - 2

        def turns_h1(n):
            return 0 if static(n) and n < 0 else 4 * n + 2

        def run(eng, step):
            for n in range(-1, min(1, NS)):
                step(n)
            if NS > 2:
                with eng.Fori(1, NS - 1) as n:
                    step(n)
            for n in range(max(1, NS - 1), NS + 1):
                step(n)

        def runs(n):
            return not static(n) or 0 <= n < NS

        with nc.Block() as block:
            @block.gpsimd
            def _(pool):
                pool.memset(heads[:], 1.0 / HD).then_inc(consts, 1)
                pool.memset(goes_on[:], 1.0).then_inc(consts, 1)
                pool.memset(inside[:], 1.0).then_inc(consts, 1)
                pool.memset(first[:], 0.0)
                pool.memset(state[:], 0.0)
                pool.memset(two_bias[:], 2.0)
                pool.memset(q_eps[:], QEPS)
                pool.memset(r_eps[:], 1e-6)
                pool.wait_ge(consts, 3)
                hv = heads[:].rearrange("p (h d) -> p h d", d=HD)
                pool.affine_select(out=hv, in_=hv, compare_op=ALU.is_ge, fill=0.0, base=0,
                                   pattern=[[-HD, P // HD], [0, HD]], channel_multiplier=1).then_inc(consts, 1)
                pool.memset(goes_on[:].rearrange("p (b s) -> p b s", s=SEQ // SEG)[:, :, 0:1], 0.0)
                pool.memset(inside[:].rearrange("p (n c) -> p n c", c=CH)[:, :, 0:1], 0.0)
                pool.wait_ge(consts, 4)
                pool.affine_select(out=hv, in_=hv, compare_op=ALU.is_ge, fill=0.0, base=HD - 1,
                                   pattern=[[HD, P // HD], [0, HD]], channel_multiplier=-1).then_inc(consts, 1)

            @block.sync
            def _(sp):
                sp.dma_start(wi[:], in_projT).then_inc(w_in, 16)
                sp.dma_start(n1[:], norm1).then_inc(w_in, 16)
                sp.dma_start(n2[:], norm2).then_inc(w_in, 16)
                sp.dma_start(wf[:], fcT).then_inc(w_in, 16)
                sp.dma_start(wo[:], out_projT).then_inc(w_in, 16)
                sp.dma_start(wp[:], projT).then_inc(w_in, 16)

            @block.tensor
            def _(pe):
                pe.wait_ge(weights_ready, 1)
                pe.wait_ge(w_in, 96)
                pe.wait_ge(consts, 5)

                def turn(src, base):
                    for half in range(2):
                        wait_count(pe, turn_copied, base + half)
                        for hh in range(DH):
                            for b in range(2):
                                mm = pe.transpose(psT[:, (2 * hh + b) * P:(2 * hh + b + 1) * P],
                                                  src[:, 2 * half + b, hh * P:(hh + 1) * P], ident[:])
                        mm.then_inc(turned, 1)

                def step(n):
                    if runs(n):
                        pe.wait_ge(turn_copied, turns_h1(n - 1) + 2)
                        for m in range(TILES_P):
                            wait_count(pe, emptied, psr_base(n) + m - 1)
                            for hh in range(DH):
                                mm = pe.matmul(psR[:, m % 2, :], wi[:, hh, m * P:(m + 1) * P], h1T[:, hh, :],
                                               start=(hh == 0), stop=(hh == DH - 1))
                            mm.then_inc(filled, 1)
                    if runs(n - 1):
                        pe.wait_ge(h2_ready, n)
                        turn(h2, turns_h2(n))
                        pe.wait_ge(turn_copied, turns_h2(n) + 2)
                        for m in range(MF):
                            wait_count(pe, emptied, fc_base(n) + m - 1)
                            for hh in range(DH):
                                mm = pe.matmul(psR[:, m % 2, :], wf[:, hh, m * P:(m + 1) * P], h2T[:, hh, :],
                                               start=(hh == 0), stop=(hh == DH - 1))
                            mm.then_inc(filled, 1)
                    if runs(n):
                        pe.wait_ge(qq_ready, n + 1)
                        for hh in range(DH):
                            wait_count(pe, emptied, rms_base(n) + hh - 1)
                            pe.matmul(psR[:, hh % 2, :], heads[:], qq[:, hh, :], start=True, stop=True
                                      ).then_inc(filled, 1)
                    if runs(n + 1):
                        pe.wait_ge(y_ready, n + 2)
                        turn(y, turns_h1(n))
                    if runs(n - 1):
                        pe.wait_ge(emptied, fc_base(n) + MF)
                        wait_count(pe, mlp_added, n - 1)
                        for t in range(GT):
                            for m in range(MF):
                                mm = pe.matmul(psM[:, t // 2, (t % 2) * D:(t % 2 + 1) * D], hid[:, m, t * P:(t + 1) * P],
                                               wp[:, m, :], start=(m == 0), stop=(m == MF - 1))
                        mm.then_inc(mlp_done, 1)
                    if runs(n):
                        pe.wait_ge(mixed_ready, n + 1)
                        wait_count(pe, x1_ready, n)
                        for t in range(GT):
                            for hh in range(DH):
                                mm = pe.matmul(psX[:, t // 2, (t % 2) * D:(t % 2 + 1) * D],
                                               mixed[:, hh, t * P:(t + 1) * P], wo[:, hh, :],
                                               start=(hh == 0), stop=(hh == DH - 1))
                        mm.then_inc(attn_done, 1)
                run(pe, step)

            @block.scalar
            def _(act):
                act.wait_ge(sq1_ready, 1)
                act.activation(t2[:], t1[:], ACT.Sqrt).then_inc(root1_ready, 1)
                act.wait_ge(consts, 5)

                def copy_turned(dst, base):
                    for half in range(2):
                        act.wait_ge(turned, base + half + 1)
                        act.activation(dst[:, :, 2 * half * P:2 * (half + 1) * P],
                                       psT[:].rearrange("p (h n) -> p h n", h=DH), ACT.Copy).then_inc(turn_copied, 1)

                def step(n):
                    if runs(n):
                        wait_count(act, mixed_ready, n)
                        for m in range(TILES_P):
                            act.wait_ge(filled, psr_base(n) + m + 1)
                            dst = (q, k, v, a, g)[m // DH][:, m % DH, :]
                            src = psR[:, m % 2, :]
                            part = "qkvag"[m // DH]
                            if part in "qv":
                                ins = act.activation(dst, src, ACT.Copy)
                            elif part == "k":
                                ins = act.activation(dst, src, ACT.Tanh)
                            elif part == "a":
                                ins = act.activation(dst, src, ACT.Sigmoid, bias=two_bias[:])
                            else:
                                ins = act.activation(dst, src, ACT.Sigmoid)
                            ins.then_inc(emptied, 1)
                    if runs(n - 1):
                        copy_turned(h2T, turns_h2(n))
                        wait_count(act, mlp_done, n - 1)
                        for m in range(MF):
                            act.wait_ge(filled, fc_base(n) + m + 1)
                            act.activation(hid[:, m, :], psR[:, m % 2, :], ACT.Silu).then_inc(emptied, 1)
                    if runs(n):
                        for hh in range(DH):
                            act.wait_ge(filled, rms_base(n) + hh + 1)
                            act.activation(rq[:, hh, :], psR[:, hh % 2, :], ACT.Sqrt, bias=q_eps[:]).then_inc(emptied, 1)
                    if runs(n + 1):
                        copy_turned(h1T, turns_h1(n))
                    if runs(n):
                        act.wait_ge(x1_ready, n + 1)
                        for t in range(GT):
                            if t:
                                act.drain()
                            ins = act.activation(sq[:], x1[:, t, :], ACT.Square, accum_out=ms[:, t:t + 1])
                        act.drain()
                        act.activation(root2[:], ms[:], ACT.Sqrt, bias=r_eps[:], scale=1.0 / D).then_inc(root2_ready, 1)
                run(act, step)

            @block.vector
            def _(dve):
                dve.tensor_scalar(t1[:], var_eps[:], -LN_EPS, None, ALU.add)
                dve.tensor_tensor(t2[:], rstd[:], rstd[:], ALU.mult)
                dve.drain()
                dve.tensor_tensor(t3[:], t1[:], t2[:], ALU.mult)
                dve.drain()
                dve.tensor_scalar(t1[:], t3[:], 1e-6, None, ALU.add).then_inc(sq1_ready, 1)
                dve.wait_ge(root1_ready, 1)
                dve.reciprocal(scale1[:], t2[:])
                dve.drain()
                newton(dve, scale1[:], t1[:], t3[:])
                dve.tensor_tensor(scale1[:], scale1[:], rstd[:], ALU.mult)
                dve.wait_ge(w_in, 96)
                for hh in range(DH):
                    dve.tensor_scalar(wi[:, hh, :], wi[:, hh, :], n1[:, hh:hh + 1], None, ALU.mult)
                    dve.tensor_scalar(wf[:, hh, :], wf[:, hh, :], n2[:, hh:hh + 1], None, ALU.mult)
                dve.drain()
                dve.memset(t3[:, 0:1], 0.0).then_inc(weights_ready, 1)
                dve.wait_ge(consts, 5)
                ends = lambda ap: ap.rearrange("p h (n c) -> p h n c", c=CH)[:, :, :, CH - 1]
                starts = lambda ap: ap.rearrange("p h (n c) -> p h n c", c=CH)[:, :, :, 0]

                def normalise(n):
                    wait_count(dve, turned, turns_h1(n - 2) + 2 if not static(n) or n > 0 else 0)
                    for b in range(GT):
                        t = GT * n + b
                        ins = dve.tensor_scalar(y[:, b, :], tile_of(x, t), mean[:, one(t)], scale1[:, one(t)],
                                                ALU.subtract, ALU.mult)
                    ins.then_inc(y_ready, 1)

                def second_norm(n):
                    dve.wait_ge(root2_ready, n + 1)
                    dve.reciprocal(r2[:], root2[:])
                    dve.tensor_scalar(r2t[:], ms[:], 1.0 / D, 1e-6, ALU.mult, ALU.add)
                    dve.drain()
                    newton(dve, r2[:], r2t[:], root2[:])
                    for b in range(GT):
                        ins = dve.tensor_scalar(h2[:, b, :], x1[:, b, :], r2[:, b:b + 1], None, ALU.mult)
                    ins.then_inc(h2_ready, 1)

                def recurrence(n):
                    dve.wait_ge(emptied, psr_base(n) + 2)
                    dve.tensor_tensor(qq[:], q[:], q[:], ALU.mult).then_inc(qq_ready, 1)
                    dve.wait_ge(emptied, psr_base(n) + 8)
                    dve.tensor_tensor(k[:], k[:], v[:], ALU.mult)
                    dve.tensor_scalar(a[:], a[:], 0.6, 0.9995, ALU.max, ALU.min)
                    dve.tensor_scalar(state[:, :, 0], state[:, :, NC], goes_on[:, one(n)], None, ALU.mult)
                    dve.drain()
                    dve.tensor_copy(starts(first[:]), starts(a[:]))
                    dve.drain()
                    dve.memset(starts(a[:]), 0.0)
                    dve.drain()
                    for hh in range(DH):
                        dve.tensor_tensor_scan(prefix[:, hh, :], a[:, hh, :], first[:, hh, :], 0.0, ALU.mult, ALU.add)
                    dve.drain()
                    dve.tensor_scalar(ratio[:], prefix[:], 1e-6, None, ALU.max)
                    dve.drain()
                    dve.reciprocal(ratio[:], ratio[:])
                    dve.drain()
                    dve.tensor_tensor(ratio[:], ratio[:], k[:], ALU.mult)
                    dve.drain()
                    for hh in range(DH):
                        dve.tensor_tensor_scan(acc[:, hh, :], inside[:], ratio[:, hh, :], 0.0, ALU.mult, ALU.add)
                    dve.tensor_copy(prefix_end[:], ends(prefix[:]))
                    dve.drain()
                    dve.tensor_tensor(chunk_end[:], prefix_end[:], ends(acc[:]), ALU.mult)
                    dve.drain()
                    for hh in range(DH):
                        dve.tensor_tensor_scan(state[:, hh, 1:NC + 1], prefix_end[:, hh, :], chunk_end[:, hh, :],
                                               state[:, hh, 0:1], ALU.mult, ALU.add)
                    dve.drain()
                    byc = lambda ap: ap.rearrange("p h (n c) -> p (h n) c", c=CH)
                    for hh in range(DH):
                        av = acc[:, hh, :].rearrange("p (n c) -> p n c", c=CH)
                        dve.tensor_tensor(av, av, state[:, hh, 0:NC].unsqueeze(2).broadcast_to([P, NC, CH]), ALU.add)
                    dve.drain()
                    dve.tensor_tensor(acc[:], acc[:], prefix[:], ALU.mult)
                    dve.drain()
                    dve.tensor_tensor(acc[:], acc[:], q[:], ALU.mult)
                    dve.wait_ge(emptied, rms_base(n) + 2)
                    dve.reciprocal(rq[:], rq[:])
                    dve.drain()
                    dve.tensor_tensor(acc[:], acc[:], rq[:], ALU.mult)
                    dve.drain()
                    dve.tensor_tensor(acc[:], acc[:], v[:], ALU.subtract)
                    dve.drain()
                    dve.tensor_tensor(acc[:], acc[:], g[:], ALU.mult)
                    dve.drain()
                    wait_count(dve, attn_done, n)
                    dve.tensor_tensor(mixed[:], acc[:], v[:], ALU.add).then_inc(mixed_ready, 1)

                def finish(n):
                    t = GT * n
                    xs = (x[:, t:t + GT, :] if static(t) else x[:, bass.ds(t, GT), :]).rearrange("p a n -> p (a n)")
                    dve.tensor_tensor(xs, xs, x1[:].rearrange("p a n -> p (a n)"), ALU.add)
                    dve.drain()
                    dve.wait_ge(mlp_done, n + 1)
                    dve.scalar_tensor_tensor(out=xs, in0=psM[:].rearrange("p a n -> p (a n)"), scalar=RES, in1=xs,
                                             op0=ALU.mult, op1=ALU.add).then_inc(mlp_added, 1)

                def first_residual(n):
                    for b in range(GT):
                        t = GT * n + b
                        dve.tensor_scalar(x1[:, b, :], tile_of(x, t), mean[:, one(t)], rstd[:, one(t)],
                                          ALU.subtract, ALU.mult)
                    dve.drain()
                    dve.wait_ge(attn_done, n + 1)
                    x1f = x1[:].rearrange("p a n -> p (a n)")
                    dve.scalar_tensor_tensor(out=x1f, in0=psX[:].rearrange("p a n -> p (a n)"), scalar=RES, in1=x1f,
                                             op0=ALU.mult, op1=ALU.add).then_inc(x1_ready, 1)

                def step(n):
                    if runs(n - 1):
                        second_norm(n - 1)
                    if runs(n + 1):
                        normalise(n + 1)
                    if runs(n):
                        recurrence(n)
                    if runs(n - 1):
                        finish(n - 1)
                    if runs(n):
                        dve.drain()
                        first_residual(n)
                run(dve, step)



def attention(nc, name, x, ident, identb, NT, SEQ, w, qk_dram, max_dram):
    wqk, bqk, wv, bv, woT, bo = w
    NH, HD = 16, 16
    B = NT * P // SEQ
    ST = SEQ // P
    NU = B * NH
    QPART = (0, 0, 0, 1, 2, 1)
    KPART = (0, 1, 2, 0, 0, 1)
    NP = len(QPART)
    ROWS = NP * HD
    MROW = ROWS
    ALLR = ROWS + 3
    SCALE = float(1.0 / np.sqrt(HD))
    KB = SEQ // 512
    VC = 32
    GT = 4
    GB = SEQ // (GT * P)
    with Chip(nc, name) as c:
        vaug = c.sb("vaug", [P, NU, ST, HD + 1])
        att = c.sb("att", [P, NU, ST, HD])
        with Chip(nc, name + "a") as a:
            mean, rstd = a.sb("mean", [P, NT]), a.sb("rstd", [P, NT])
            row_statistics(nc, name, x, NT, mean, rstd)
            wqk_sb = a.sb("wqk", [P, DH, 2 * D])
            bqk_sb = a.sb("bqk", [P, 2 * DH])
            wv_sb = a.sb("wv", [P, DH, D])
            bv_sb = a.sb("bv", [1, D])
            ones = a.sb("ones", [1, P])
            y = a.sb("y", [P, GT, D])
            yT = a.sb("yT", [P, 2, DH, GT * P])
            qf = a.sb("qf", [P, 2, 512])
            rest = a.sb("rest", [P, 512])
            parts = a.sb("parts", [P, 2, 3, 512], BF16)
            psT, psR, psV = a.ps("psT", [P, 512]), a.ps("psR", [P, 2, 512]), a.ps("psV", [P, 2, 512])
            w_in, consts, y_ready, turned, turn_copied, qk_done, qk_copied, split_ready, v_done, v_copied = (
                a.sem(n) for n in ("w_in", "consts", "y_ready", "turned", "turn_copied", "qk_done", "qk_copied",
                                   "split_ready", "v_done", "v_copied"))
            stored = [a.sem("stored0"), a.sem("stored1")]
            with nc.Block() as block:
                @block.gpsimd
                def _(pool):
                    pool.memset(ones[:], 1.0).then_inc(consts, 1)
                    pool.memset(vaug[:, :, :, HD:HD + 1], 1.0)

                @block.sync
                def _(sp):
                    sp.dma_start(wqk_sb[:], wqk).then_inc(w_in, 16)
                    sp.dma_start(bqk_sb[:], bqk).then_inc(w_in, 16)
                    sp.dma_start(wv_sb[:], wv).then_inc(w_in, 16)
                    sp.dma_start(bv_sb[:], bv).then_inc(w_in, 16)
                    with sp.Fori(0, B) as b:
                        for k in range(GB):
                            for m in range(2 * DH):
                                sp.wait_ge(split_ready, 2 * DH * (GB * b + k) + m + 1)
                                for part in range(3):
                                    sp.dma_start(qk_dram[m // DH, part, bass.ds(b * D + (m % DH) * P, P),
                                                         k * 512:(k + 1) * 512],
                                                 parts[:, m % 2, part, :]).then_inc(stored[m % 2], 16)
                    for m in range(2):
                        sp.wait_ge(stored[m], 16 * 3 * DH * GB * B)

                @block.vector
                def _(dve):
                    with dve.Fori(0, B) as b:
                        for k in range(GB):
                            g = GB * b + k
                            for kk in ([0, 1] if k == 0 else [k + 1] if k + 1 < GB else []):
                                dve.wait_ge(turned, 2 * (GB * b + kk))
                                for q in range(GT):
                                    ins = dve.tensor_scalar(y[:, q, :], tile_of(x, (GB * b + kk) * GT + q),
                                                            mean[:, one((GB * b + kk) * GT + q)],
                                                            rstd[:, one((GB * b + kk) * GT + q)], ALU.subtract, ALU.mult)
                                ins.then_inc(y_ready, 1)
                            for m in range(2 * DH):
                                dve.wait_ge(qk_copied, 2 * DH * g + m + 1)
                                dve.tensor_tensor(rest[:], qf[:, m % 2, :], parts[:, m % 2, 0, :], ALU.subtract)
                                dve.drain()
                                dve.tensor_copy(parts[:, m % 2, 1, :], rest[:])
                                dve.drain()
                                dve.tensor_tensor(parts[:, m % 2, 2, :], rest[:], parts[:, m % 2, 1, :], ALU.subtract
                                                  ).then_inc(split_ready, 1)
                                dve.drain()

                @block.tensor
                def _(pe):
                    pe.wait_ge(w_in, 64)
                    pe.wait_ge(consts, 1)

                    def turn(g):
                        pe.wait_ge(y_ready, g + 1)
                        for half in range(2):
                            pe.wait_ge(turn_copied, 2 * g + half)
                            for hh in range(DH):
                                for q in range(2):
                                    mm = pe.transpose(psT[:, (2 * hh + q) * P:(2 * hh + q + 1) * P],
                                                      y[:, 2 * half + q, hh * P:(hh + 1) * P], ident[:])
                            mm.then_inc(turned, 1)

                    with pe.Fori(0, B) as b:
                        turn(GB * b)
                        for k in range(GB):
                            g = GB * b + k
                            pe.wait_ge(turn_copied, 2 * g + 2)
                            for m in range(2 * DH):
                                pe.wait_ge(qk_copied, 2 * DH * g + max(m - 1, 0))
                                for hh in range(DH):
                                    mm = pe.matmul(psR[:, m % 2, :], wqk_sb[:, hh, m * P:(m + 1) * P], yT[:, k % 2, hh, :],
                                                   start=(hh == 0), stop=(hh == DH - 1))
                                mm.then_inc(qk_done, 1)
                            if k + 1 < GB:
                                turn(g + 1)
                            pe.wait_ge(v_copied, g)
                            for q in range(GT):
                                out = psV[:, q // 2, (q % 2) * D:(q % 2 + 1) * D]
                                for hh in range(DH):
                                    pe.matmul(out, yT[:, k % 2, hh, q * P:(q + 1) * P], wv_sb[:, hh, :],
                                              start=(hh == 0), stop=False)
                                mm = pe.matmul(out, ones[:], bv_sb[:], start=False, stop=True)
                            mm.then_inc(v_done, 1)

                @block.scalar
                def _(act):
                    def copy_turned(g, k):
                        for half in range(2):
                            act.wait_ge(turned, 2 * g + half + 1)
                            act.activation(yT[:, k % 2, :, 2 * half * P:2 * (half + 1) * P],
                                           psT[:].rearrange("p (h n) -> p h n", h=DH), ACT.Copy).then_inc(turn_copied, 1)

                    act.wait_ge(w_in, 64)
                    with act.Fori(0, B) as b:
                        copy_turned(GB * b, 0)
                        for k in range(GB):
                            g = GB * b + k
                            for m in range(2 * DH):
                                act.wait_ge(stored[m % 2], 48 * (DH * g + m // 2))
                                act.wait_ge(qk_done, 2 * DH * g + m + 1)
                                act.activation(qf[:, m % 2, :], psR[:, m % 2, :], ACT.Identity, bias=bqk_sb[:, m:m + 1])
                                act.activation(parts[:, m % 2, 0, :], psR[:, m % 2, :], ACT.Identity,
                                               bias=bqk_sb[:, m:m + 1]).then_inc(qk_copied, 1)
                            if k + 1 < GB:
                                copy_turned(g + 1, k + 1)
                            act.wait_ge(v_done, g + 1)
                            act.activation(vaug[:, bass.ds(NH * b, NH), GT * k:GT * (k + 1), 0:HD].rearrange("p n t e -> p t n e"),
                                           psV[:].rearrange("p a (t n e) -> p (a t) n e", n=NH, e=HD), ACT.Copy
                                           ).then_inc(v_copied, 1)

        RQ = 4
        RP = 4
        with Chip(nc, name + "b") as u_:
            qa = u_.sb("qa", [P, RQ, SEQ], BF16)
            ka = u_.sb("ka", [P, RQ, SEQ], BF16)
            vh = u_.sb("vh", [P, RQ, ST, VC])
            pt = u_.sb("pt", [P, RP, KB, 512])
            mx = u_.sb("mx", [P, ST, KB // 2])
            m = u_.sb("m", [P, ST])
            mr = u_.sb("mr", [P, ST])
            mcat = u_.sb("mcat", [P, P], BF16)
            mT = u_.sb("mT", [3 * ST, P], BF16)
            oS = u_.sb("oS", [P, 512])
            inv = u_.sb("inv", [P, KB, ST // KB])
            psA = u_.ps("psA", [P, 2, 1024])
            psE = u_.ps("psE", [P, 2, 512])
            psO = u_.ps("psO", [P, 512])
            psM = u_.ps("psM", [P, 512])
            rows_in = [u_.sem(f"rows_in{r}") for r in range(RQ)]
            (consts, scores_done, max_taken, m_ready, m_turned, mT_ready, m_stored, m_in, keys_done, exp_ready, pv_done,
             vh_ready, o_ready, o_copied, o_turned, att_ready) = (
                u_.sem(n) for n in ("consts", "scores_done", "max_taken", "m_ready", "m_turned", "mT_ready", "m_stored",
                                    "m_in", "keys_done", "exp_ready", "pv_done", "vh_ready", "o_ready", "o_copied",
                                    "o_turned", "att_ready"))
            LAG = 2
            HC = KB // 2

            def run(eng, step):
                for n in range(-2, RQ):
                    step(n, n // RQ, n % RQ)
                with eng.Fori(1, NU // RQ - 1) as i:
                    for r in range(RQ):
                        step(RQ * i + r, i, r)
                for n in range(NU - RQ, NU + 1):
                    step(n, n // RQ, n % RQ)

            def runs(n):
                return not static(n) or 0 <= n < NU

            with nc.Block() as block:
                @block.gpsimd
                def _(pool):
                    pool.memset(vh[:], 0.0).then_inc(consts, 1)
                    pool.wait_ge(consts, 1)
                    pool.memset(ka[MROW:ALLR, :, :], 1.0).then_inc(consts, 1)
                    pool.wait_ge(consts, 2)
                    pool.memset(mcat[:], 0.0).then_inc(consts, 1)
                    pool.wait_ge(consts, 3)

                    def step(n, i, r):
                        if runs(n + 1):
                            wait_count(pool, o_ready, n - 2)
                            src = vaug[:, n + 1, :, :] if static(n) else \
                                vaug[:, bass.ds(n + 1, 1), :, :].rearrange("p a t e -> p (a t) e")
                            pool.tensor_copy(vh[:, (r + 1) % RQ, :, 0:HD + 1], src).then_inc(vh_ready, 1)
                    run(pool, step)

                @block.sync
                def _(sp):
                    def step(n, i, r):
                        v = n + 3
                        rv = (r + 3) % RQ
                        for v, rv in ([(n + 2, (r + 2) % RQ), (v, rv)] if static(n) and n == -2 else [(v, rv)]):
                            if runs(v):
                                wait_count(sp, keys_done, KB * ST * (v - RQ + 1))
                                for which, dst, pick in ((0, qa, QPART), (1, ka, KPART)):
                                    for j, part in enumerate(pick):
                                        rows = slice(HD * v, HD * (v + 1)) if static(v) else bass.ds(HD * v, HD)
                                        sp.dma_start(dst[HD * j:HD * (j + 1), rv, :], qk_dram[which, part, rows, :]
                                                     ).then_inc(rows_in[rv], 16)
                        if runs(n + 1):
                            sp.wait_ge(mT_ready, n + 2)
                            wait_count(sp, m_in, 16 * (n + 1))
                            sp.dma_start(max_dram, mT[:]).then_inc(m_stored, 16)
                            sp.wait_ge(m_stored, 16 * (n + 2))
                            sp.dma_start(qa[MROW:ALLR, (r + 1) % RQ, :],
                                         max_dram.rearrange("(a t) s -> a (t s)", a=3)).then_inc(m_in, 16)
                    run(sp, step)

                @block.tensor
                def _(pe):
                    pe.wait_ge(consts, 3)

                    def by_query(v, st, r, i):
                        if st == 0:
                            pe.wait_ge(rows_in[r], 16 * 2 * NP * (i + 1))
                        for hc in range(HC):
                            wait_count(pe, max_taken, HC * (ST * v + st) + hc - 1)
                            for q in range(2):
                                kb = 2 * hc + q
                                mm = pe.matmul(psA[:, (HC * st + hc) % 2, q * 512:(q + 1) * 512],
                                               qa[0:ROWS, r, st * P:(st + 1) * P],
                                               ka[0:ROWS, r, kb * 512:(kb + 1) * 512], start=True, stop=True)
                            mm.then_inc(scores_done, 1)

                    def by_key(n, tt, r):
                        if tt == 0:
                            pe.wait_ge(m_in, 16 * (n + 1))
                        for kb in range(KB):
                            wait_count(pe, exp_ready, KB * (ST * n + tt) + kb - 1)
                            pe.matmul(psE[:, kb % 2, :], ka[0:ALLR, r, tt * P:(tt + 1) * P],
                                      qa[0:ALLR, r, kb * 512:(kb + 1) * 512], start=True, stop=True
                                      ).then_inc(keys_done, 1)

                    def values(n, tt, r):
                        if tt == 0:
                            pe.wait_ge(vh_ready, n + 1)
                            wait_count(pe, o_copied, n)
                        pe.wait_ge(exp_ready, KB * (ST * n + tt) + KB)
                        for kb in range(KB):
                            mm = pe.matmul(psO[VC * kb:VC * (kb + 1), :], vh[:, r, tt, :], pt[:, tt % RP, kb, :],
                                           start=(tt == 0), stop=(tt == ST - 1), tile_position=(0, VC * kb))
                        mm.then_inc(pv_done if tt < ST - 1 else o_ready, 1)

                    def turn_max(n):
                        pe.wait_ge(m_ready, n + 1)
                        wait_count(pe, att_ready, n - 2)
                        pe.transpose(psM[:, 0:P // 2].bitcast(BF16), mcat[:], identb[:]
                                     ).then_inc(m_turned, 1)

                    def turn_out(n):
                        pe.wait_ge(o_copied, n + 1)
                        pe.wait_ge(mT_ready, (n + 3) if not static(n) else min(n + 3, NU))
                        wait_count(pe, att_ready, n)
                        for q in range(512 // P):
                            mm = pe.transpose(psM[:, q * P:(q + 1) * P], oS[:, q * P:(q + 1) * P], ident[:])
                        mm.then_inc(o_turned, 1)

                    def step(n, i, r):
                        for t in range(ST):
                            if runs(n):
                                by_key(n, t, r)
                            if runs(n + 2):
                                by_query(n + 2, t, (r + 2) % RQ, i + (r + 2) // RQ)
                            if t == 1 and runs(n + 1):
                                turn_max(n + 1)
                            if t < LAG and runs(n - 1):
                                values(n - 1, ST - LAG + t, (r - 1) % RQ)
                            if t >= LAG and runs(n):
                                values(n, t - LAG, r)
                            if t == 5 and runs(n - 1):
                                turn_out(n - 1)
                    run(pe, step)

                @block.scalar
                def _(act):
                    act.wait_ge(consts, 3)

                    def step(n, i, r):
                        for t in range(ST):
                            if runs(n):
                                if t >= RP:
                                    wait_count(act, pv_done, (ST - 1) * n + t - RP + 1)
                                elif t == RP - 1:
                                    wait_count(act, o_ready, n)
                                else:
                                    wait_count(act, pv_done, (ST - 1) * (n - 1) + ST - RP + t + 1)
                                for kb in range(KB):
                                    act.wait_ge(keys_done, KB * (ST * n + t) + kb + 1)
                                    act.activation(pt[:, t % RP, kb, :], psE[:, kb % 2, :], ACT.Exp, scale=SCALE
                                                   ).then_inc(exp_ready, 1)
                            if t == 1 and runs(n - 1):
                                act.wait_ge(o_ready, n)
                                wait_count(act, o_turned, n - 1)
                                act.activation(oS[:], psO[:], ACT.Copy).then_inc(o_copied, 1)
                            if t == 2 and runs(n + 1):
                                act.wait_ge(m_turned, n + 2)
                                wait_count(act, m_stored, 16 * (n + 1))
                                act.activation(mT[:], psM[0:3 * ST, 0:P // 2].bitcast(BF16), ACT.Copy).then_inc(mT_ready, 1)
                    run(act, step)

                @block.vector
                def _(dve):
                    dve.wait_ge(consts, 3)
                    part_of = lambda j: mcat[:, j * ST:(j + 1) * ST]

                    def step(n, i, r):
                        for t in range(ST):
                            v = n + 2
                            if runs(v):
                                for hc in range(HC):
                                    dve.wait_ge(scores_done, HC * (ST * v + t) + hc + 1)
                                    dve.tensor_reduce(mx[:, t, hc:hc + 1], psA[:, (HC * t + hc) % 2, :], AX_X, ALU.max
                                                      ).then_inc(max_taken, 1)
                            if t == 7 and runs(n - 1):
                                dve.wait_ge(o_turned, n)
                                ov = psM[:].rearrange("p (q j e) -> p j q e", j=KB, e=VC)
                                dve.reciprocal(inv[:], ov[:, :, :, HD])
                                dve.drain()
                                dst = (att[:, n - 1, :, :] if static(n) else
                                       att[:, bass.ds(n - 1, 1), :, :].rearrange("p a t e -> p (a t) e"))
                                dve.tensor_tensor(dst.rearrange("p (j q) e -> p j q e", j=KB), ov[:, :, :, 0:HD],
                                                  inv[:].unsqueeze(3).broadcast_to([P, KB, ST // KB, HD]), ALU.mult
                                                  ).then_inc(att_ready, 1)
                        if runs(n + 2):
                            dve.drain()
                            dve.tensor_reduce(m[:], mx[:], AX_X, ALU.max)
                            dve.drain()
                            wait_count(dve, m_turned, n + 2)
                            dve.tensor_scalar(part_of(0), m[:], -1.0, None, ALU.mult)
                            dve.drain()
                            dve.scalar_tensor_tensor(out=mr[:], in0=m[:], scalar=-1.0, in1=part_of(0),
                                                     op0=ALU.mult, op1=ALU.subtract)
                            dve.drain()
                            dve.tensor_copy(part_of(1), mr[:])
                            dve.drain()
                            dve.tensor_tensor(part_of(2), mr[:], part_of(1), ALU.subtract).then_inc(m_ready, 1)
                    run(dve, step)

        with Chip(nc, name + "c") as o:
            wo_sb = o.sb("wo", [P, DH, D])
            bo_sb = o.sb("bo", [1, D])
            ones = o.sb("ones", [1, P])
            ag = o.sb("ag", [P, 2, D])
            aT = o.sb("aT", [P, 2, DH, P])
            psT, psY = o.ps("psT", [P, 2, 512]), o.ps("psY", [P, 2, 512])
            w_in, consts, gathered, turned, turn_copied, projected, added = (
                o.sem(n) for n in ("w_in", "consts", "gathered", "turned", "turn_copied", "projected", "added"))
            with nc.Block() as block:
                @block.gpsimd
                def _(pool):
                    pool.memset(ones[:], 1.0).then_inc(consts, 1)

                @block.sync
                def _(sp):
                    sp.dma_start(wo_sb[:], woT).then_inc(w_in, 16)
                    sp.dma_start(bo_sb[:], bo).then_inc(w_in, 16)

                def run(eng, step):
                    for b in range(B):
                        for st in range(2 if b == 0 else 0):
                            step(st, st, b, st)
                        with eng.Fori(1 if b == 0 else 0, ST // 2) as i:
                            for k in range(2):
                                step(b * ST + 2 * i + k, k, b, 2 * i + k)

                @block.vector
                def _(dve):
                    def gather(t, k, b, st):
                        src = att[:, b * NH:(b + 1) * NH, one(st), :].rearrange("p n t e -> p n (t e)")
                        wait_count(dve, turned, t - 1)
                        dve.tensor_copy(ag[:, k, :].rearrange("p (n e) -> p n e", n=NH), src).then_inc(gathered, 1)

                    def add(t, k, b, st):
                        dve.wait_ge(projected, t + 1)
                        xt = tile_of(x, t)
                        dve.tensor_tensor(xt, psY[:, k, 0:D], xt, ALU.add).then_inc(added, 1)

                    def both(t, k, b, st):
                        gather(t, k, b, st)
                        if not static(t) or t > 0:
                            add(t - 1, 1 - k, b, st)
                    run(dve, both)
                    add(NT - 1, 1, 0, 0)

                @block.tensor
                def _(pe):
                    pe.wait_ge(w_in, 32)
                    pe.wait_ge(consts, 1)

                    def step(t, k, b, st):
                        pe.wait_ge(gathered, t + 1)
                        wait_count(pe, turn_copied, t - 1)
                        for hh in range(DH):
                            mm = pe.transpose(psT[:, k, hh * P:(hh + 1) * P], ag[:, k, hh * P:(hh + 1) * P], ident[:])
                        mm.then_inc(turned, 1)
                        pe.wait_ge(turn_copied, t + 1)
                        wait_count(pe, added, t - 1)
                        for hh in range(DH):
                            pe.matmul(psY[:, k, 0:D], aT[:, k, hh, :], wo_sb[:, hh, :], start=(hh == 0), stop=False)
                        pe.matmul(psY[:, k, 0:D], ones[:], bo_sb[:], start=False, stop=True).then_inc(projected, 1)
                    run(pe, step)

                @block.scalar
                def _(act):
                    def step(t, k, b, st):
                        act.wait_ge(turned, t + 1)
                        wait_count(act, projected, t - 1)
                        act.activation(aT[:, k, :, :].rearrange("p h n -> p (h n)"), psT[:, k, 0:D], ACT.Copy
                                       ).then_inc(turn_copied, 1)
                    run(act, step)


def dram_tile(d, t):
    return d[t, :, :] if static(t) else d[bass.ds(t, 1), :, :].rearrange("a p n -> (a p) n")


def keys_layout(keys):
    h, nk, p, kd = keys.shape
    return np.ascontiguousarray(keys.transpose(3, 2, 0, 1).reshape(kd, p * h, nk))


def halves_layout(v):
    return np.ascontiguousarray(v.reshape(-1, P).T)


def key_in_layout(key_in):
    ne, d = key_in.shape
    return np.ascontiguousarray(key_in.reshape(P, ne // P, d // P, P).transpose(3, 2, 1, 0).reshape(P, d // P, ne))


def rows_layout(w):
    return np.ascontiguousarray(w.reshape(-1, P, w.shape[1]).transpose(1, 0, 2))


def head_cols(w):
    return w.transpose(1, 0, 2).reshape(w.shape[1], -1)


SEQ = 2048


def build(nc, a, out, qk_dram, max_dram, yT_dram):
    tokens = out.rearrange("b s d -> (b s) d").rearrange("(t p) d -> p t d", p=P)
    x_in = a["x"].rearrange("b s d -> (b s) d").rearrange("(t p) d -> p t d", p=P)
    NT = tokens.shape[1]
    peer = tuple(a[n] for n in ("gamma", "beta", "w_q", "keysT", "key_inT", "key_out"))
    mix = tuple(a[n] for n in ("norm1", "norm2", "in_projT", "out_projT", "fcT", "projT"))
    moe = tuple(a[n] for n in ("gate_W", "gate_b", "expert_W", "expert_b"))
    att = tuple(a[n] for n in ("wqk", "bqk", "wv", "bv", "woT", "bo"))
    with Chip(nc, "all") as c:
        x = c.sb("x", [P, NT, D])
        ident, ident16, identb = c.sb("ident", [P, P]), c.sb("ident16", [P, P], F16), c.sb("identb", [P, P], BF16)
        x_loaded, x_stored = c.sem("x_loaded"), c.sem("x_stored")
        make_identities(nc, ident, ident16, identb)
        with nc.Block() as block:
            @block.sync
            def _(sp):
                sp.dma_start(x[:], x_in).then_inc(x_loaded, 16)
                sp.wait_ge(x_loaded, 16)
        peer_ffn(nc, "peer0", x, ident, ident16, NT, peer, yT_dram)
        recurrent_block(nc, "mix", x, ident, NT, SEQ, mix)
        peer_ffn(nc, "peer1", x, ident, ident16, NT, peer, yT_dram)
        moe_ffn(nc, "moe0", x, ident, NT, moe)
        attention(nc, "att", x, ident, identb, NT, SEQ, att, qk_dram, max_dram)
        moe_ffn(nc, "moe1", x, ident, NT, moe)
        with nc.Block() as block:
            @block.sync
            def _(sp):
                sp.dma_start(tokens, x[:]).then_inc(x_stored, 16)
                sp.wait_ge(x_stored, 16)


def kernel(L0_attn_x, L0_attn_norm1_w, L0_attn_norm2_w, L0_attn_in_proj_w, L0_attn_out_proj_w, L0_attn_fc_w,
           L0_attn_proj_w, L0_ffn_gamma, L0_ffn_beta, L0_ffn_w_q, L0_ffn_keys, L0_ffn_key_in, L0_ffn_key_out,
           L1_attn_wq, L1_attn_bq, L1_attn_wk, L1_attn_bk, L1_attn_wv, L1_attn_bv, L1_attn_wo, L1_attn_bo,
           L1_ffn_gate_W, L1_ffn_gate_b, L1_ffn_expert_W, L1_ffn_expert_b):
    import concourse.bacc as bacc
    from concourse.bass_utils import run_bass_kernel_spmd as run

    arrays = {
        "x": L0_attn_x,
        "gamma": halves_layout(L0_ffn_gamma), "beta": halves_layout(L0_ffn_beta), "w_q": L0_ffn_w_q,
        "keysT": keys_layout(L0_ffn_keys), "key_inT": key_in_layout(L0_ffn_key_in), "key_out": L0_ffn_key_out,
        "norm1": halves_layout(L0_attn_norm1_w), "norm2": halves_layout(L0_attn_norm2_w),
        "in_projT": rows_layout(L0_attn_in_proj_w.T), "out_projT": rows_layout(L0_attn_out_proj_w.T),
        "fcT": rows_layout(L0_attn_fc_w.T), "projT": rows_layout(L0_attn_proj_w.T),
        "gate_W": L1_ffn_gate_W, "gate_b": L1_ffn_gate_b, "expert_W": L1_ffn_expert_W, "expert_b": L1_ffn_expert_b,
        "wqk": rows_layout(np.concatenate([head_cols(L1_attn_wq), head_cols(L1_attn_wk)], axis=1)),
        "bqk": halves_layout(np.concatenate([L1_attn_bq.reshape(-1), L1_attn_bk.reshape(-1)])),
        "wv": rows_layout(head_cols(L1_attn_wv)), "bv": L1_attn_bv.reshape(1, -1),
        "woT": rows_layout(L1_attn_wo.T), "bo": L1_attn_bo.reshape(1, -1),
    }
    arrays = {n: np.ascontiguousarray(v) for n, v in arrays.items()}
    nc = bacc.Bacc("TRN2", target_bir_lowering=False, num_devices=1)
    aps = {n: nc.dram_tensor(f"in_{n}", v.shape, mybir.dt.from_np(v.dtype), kind="ExternalInput").ap()
           for n, v in arrays.items()}
    shape = L0_attn_x.shape
    out = nc.dram_tensor("out", shape, F32, kind="ExternalOutput").ap()
    tokens = shape[0] * shape[1]
    qk_dram = nc.dram_tensor("qk_scratch", (2, 3, tokens // SEQ * D, SEQ), BF16, kind="Internal").ap()
    max_dram = nc.dram_tensor("max_scratch", (3 * SEQ // P, P), BF16, kind="Internal").ap()
    yT_dram = nc.dram_tensor("yT_scratch", (tokens // P, P, D), F32, kind="Internal").ap()
    build(nc, aps, out, qk_dram, max_dram, yT_dram)
    r = run(nc, [{f"in_{n}": v for n, v in arrays.items()}], core_ids=[0])
    return r.results[0]["out"]
```

```python
from contextlib import ExitStack

import numpy as np

import concourse.bass as bass
from concourse import mybir

F32 = mybir.dt.float32
F16 = mybir.dt.float16
BF16 = mybir.dt.bfloat16
U32 = mybir.dt.uint32
ALU = mybir.AluOpType
ACT = mybir.ActivationFunctionType
AX_X = mybir.AxisListType.X

P = 128
D = 256
DH = D // P
LN_EPS = 1e-5


def static(v):
    return isinstance(v, int)


def wait_count(eng, sem, count):
    if static(count) and count <= 0:
        return
    eng.wait_ge(sem, count)


def one(i):
    return slice(i, i + 1) if static(i) else bass.ds(i, 1)


def tile_of(buf, i):
    if static(i):
        return buf[:, i, :]
    return buf[:, bass.ds(i, 1), :].rearrange("p a n -> p (a n)")


class Chip:

    def __init__(self, nc, name):
        self.nc, self.name, self.stack, self.sems = nc, name, ExitStack(), []

    def __enter__(self):
        self.stack.__enter__()
        return self

    def __exit__(self, *error):
        if error[0] is None and self.sems:
            self.nc.clear_and_free_semaphores(self.sems)
            self.nc.all_engine_barrier()
        return self.stack.__exit__(*error)

    def sb(self, name, shape, dt=F32):
        return self.stack.enter_context(self.nc.sbuf_tensor(f"{self.name}_{name}", shape, dt))

    def ps(self, name, shape, dt=F32):
        return self.stack.enter_context(self.nc.psum_tensor(f"{self.name}_{name}", shape, dt))

    def sem(self, name):
        self.sems.append(self.nc.alloc_semaphore(name=f"{self.name}_{name}"))
        return self.sems[-1]


def make_identities(nc, *idents):
    with Chip(nc, "ident") as c:
        zeroed = c.sem("zeroed")
        with nc.Block() as block:
            @block.gpsimd
            def _(pool):
                for m in idents:
                    pool.memset(m[:], 0.0).then_inc(zeroed, 1)
                pool.wait_ge(zeroed, len(idents))
                for m in idents:
                    pool.affine_select(out=m[:], in_=m[:], compare_op=ALU.not_equal, fill=1.0,
                                       base=0, pattern=[[-1, P]], channel_multiplier=1)


def row_statistics(nc, name, x, NT, mean, rstd, var_eps=None):
    with Chip(nc, name + "_st") as c:
        st = c.sb("st", [P, NT, 6])
        w = [c.sb(f"w{i}", [P, NT]) for i in range(4)]
        var_ready, root_ready = c.sem("var_ready"), c.sem("root_ready")
        with nc.Block() as block:
            @block.vector
            def _(dve):
                with dve.Fori(0, NT // 4) as i:
                    for k in range(4):
                        dve.bn_stats(tile_of(st, 4 * i + k), tile_of(x, 4 * i + k))
                dve.drain()
                m0, v0, m1, v1 = (st[:, :, k] for k in (1, 2, 4, 5))
                dve.tensor_tensor(w[0][:], m0, m1, ALU.add)
                dve.tensor_tensor(w[1][:], m0, m1, ALU.subtract)
                dve.tensor_tensor(w[2][:], v0, v1, ALU.add)
                dve.drain()
                dve.tensor_scalar(mean[:], w[0][:], 0.5, None, ALU.mult)
                dve.tensor_tensor(w[3][:], w[1][:], w[1][:], ALU.mult)
                dve.tensor_scalar(w[2][:], w[2][:], 1.0 / D, LN_EPS, ALU.mult, ALU.add)
                dve.drain()
                dve.scalar_tensor_tensor(out=w[1][:], in0=w[3][:], scalar=0.25, in1=w[2][:],
                                         op0=ALU.mult, op1=ALU.add).then_inc(var_ready, 1)
                dve.wait_ge(root_ready, 1)
                dve.reciprocal(rstd[:], w[0][:])
                if var_eps is not None:
                    dve.tensor_copy(var_eps[:], w[1][:])
                dve.drain()
                newton(dve, rstd[:], w[1][:], w[2][:])

            @block.scalar
            def _(act):
                act.wait_ge(var_ready, 1)
                act.activation(w[0][:], w[1][:], ACT.Sqrt).then_inc(root_ready, 1)


def newton(dve, r, v, tmp):
    dve.tensor_tensor(tmp, r, r, ALU.mult)
    dve.drain()
    dve.tensor_tensor(tmp, tmp, v, ALU.mult)
    dve.drain()
    dve.tensor_scalar(tmp, tmp, -0.5, 1.5, ALU.mult, ALU.add)
    dve.drain()
    dve.tensor_tensor(r, r, tmp, ALU.mult)
    dve.drain()



def peer_ffn(nc, name, x, ident, ident16, NT, w, yT_dram):
    gamma, beta, w_q, keysT, key_inT, key_out = w
    H, K, NK, KD = 8, 8, 64, 128
    NE = NK * NK
    NJ = NE // P
    JG = 4
    NG = NJ // JG
    HK = H * K
    S = 2 * H * NK
    HM = P // 4
    MQ = P // 2 // NG
    WS = 4096.0
    KS = 64.0
    PS = 16.0
    RING = 4
    LAG = 3
    with Chip(nc, name) as c:
        keyin = c.sb("keyin", [P, 2, DH * NE], F16)
        keyout = c.sb("keyout", [P, 2, NJ * D], F16)
        wc = c.sb("wc", [P, DH, S])
        xscale, xbias = c.sb("xscale", [P, DH]), c.sb("xbias", [P, DH])

        with Chip(nc, name + "a") as a:
            mean, rstd = a.sb("mean", [P, NT]), a.sb("rstd", [P, NT])
            row_statistics(nc, name, x, NT, mean, rstd)
            wq = a.sb("wq", [P, 2 * H, D])
            kT = a.sb("kT", [P, 2 * H, NK])
            gb = a.sb("gb", [P, 2, DH])
            y = a.sb("y", [P, 2, 2, D])
            yT = a.sb("yT", [P, 2, DH, 2, P])
            bst = a.sb("bst", [P, DH, NT // 2, 6])
            mv = a.sb("mv", [P, DH, 2])
            rt, rv, rtmp = a.sb("rt", [P, DH]), a.sb("rv", [P, DH]), a.sb("rtmp", [P, DH])
            raw = a.sb("raw", [P, 2, 2, NJ * D // (NT // 2)])
            psT = a.ps("psT", [P, 2, 512])
            psW = a.ps("psW", [P, 2, 512])
            w_in, gb_in = a.sem("w_in"), a.sem("gb_in")
            keys_in = [a.sem("keys_in0"), a.sem("keys_in1")]
            key_high, key_low = a.sem("key_high"), a.sem("key_low")
            y_ready, yT_ready = a.sem("y_ready"), a.sem("yT_ready")
            transposed, stats_done = a.sem("transposed"), a.sem("stats_done")
            stored = [a.sem("stored0"), a.sem("stored1")]
            var_ready, root_ready = a.sem("bvar_ready"), a.sem("broot_ready")
            folded, fold_copied = a.sem("folded"), a.sem("fold_copied")
            PAIRS = NT // 2
            QUARTER = PAIRS // (2 * DH)
            PIECE = NJ * D // PAIRS
            assert DH * NE == NJ * D and PAIRS % (2 * DH) == 0 and QUARTER % 2 == 0

            def pairs_of(eng, lo, hi, step):
                if lo < hi:
                    with eng.Fori(lo // 2, hi // 2) as j:
                        for k in range(2):
                            step(2 * j + k, k)

            def piece_of(buf, n, i):
                return buf[:, n, i * PIECE:(i + 1) * PIECE] if static(i) else buf[:, n, bass.ds(i * PIECE, PIECE)]

            with nc.Block() as block:
                @block.sync
                def _(sp):
                    def load_keys(i, k):
                        wait_count(sp, key_low, 2 * (i - 1))
                        for which, src in ((0, key_inT.rearrange("p h e -> p (h e)")),
                                           (1, key_out.rearrange("(c j) d -> c (j d)", j=NJ))):
                            cols = slice(i * PIECE, (i + 1) * PIECE) if static(i) else bass.ds(i * PIECE, PIECE)
                            sp.dma_start(raw[:, k, which, :], src[:, cols]).then_inc(keys_in[k], 16)

                    load_keys(0, 0)
                    load_keys(1, 1)
                    sp.dma_start(wq[:], w_q.rearrange("(r k) d -> k r d", k=KD)).then_inc(w_in, 16)
                    sp.dma_start(kT[:], keysT).then_inc(w_in, 16)
                    sp.dma_start(gb[:, 0, :], gamma).then_inc(gb_in, 16)
                    sp.dma_start(gb[:, 1, :], beta).then_inc(gb_in, 16)
                    pairs_of(sp, 2, PAIRS, load_keys)

                @block.gpsimd
                def _(pool):
                    def store(i, k):
                        pool.wait_ge(yT_ready, i + 1)
                        pool.dma_start(yT_dram[bass.ds(2 * i, 2), :, :].rearrange("a p (h n) -> p h a n", h=DH),
                                     yT[:, k, :, :, :]).then_inc(stored[k], 16)
                    pairs_of(pool, 0, PAIRS, store)
                    for k in range(2):
                        pool.wait_ge(stored[k], 16 * (PAIRS // 2))

                @block.vector
                def _(dve):
                    def y_pair(i, k):
                        wait_count(dve, transposed, i - 1)
                        for a in range(2):
                            t = 2 * i + a
                            ins = dve.tensor_scalar(y[:, k, a, :], tile_of(x, t), mean[:, one(t)], rstd[:, one(t)],
                                                    ALU.subtract, ALU.mult)
                        ins.then_inc(y_ready, 1)

                    def stats_pair(i, k):
                        dve.wait_ge(yT_ready, i + 1)
                        for h in range(DH):
                            st = bst[:, h, i, :] if static(i) else bst[:, h, bass.ds(i, 1), :].rearrange("p a n -> p (a n)")
                            ins = dve.bn_stats(st, yT[:, k, h, :, :].rearrange("p a n -> p (a n)"))
                        ins.then_inc(stats_done, 1)

                    def key_rest(i, k):
                        for which, keys in ((0, keyin), (1, keyout)):
                            dve.wait_ge(key_high, 2 * i + which + 1)
                            dve.scalar_tensor_tensor(out=piece_of(keys, 1, i), in0=raw[:, k, which, :],
                                                     scalar=KS, in1=piece_of(keys, 0, i),
                                                     op0=ALU.mult, op1=ALU.subtract).then_inc(key_low, 1)

                    def step(i, k):
                        stats_pair(i, k)
                        if not static(i) or i + 2 < PAIRS:
                            y_pair(i + 2, k)
                        key_rest(i, k)

                    y_pair(0, 0)
                    y_pair(1, 1)
                    pairs_of(dve, 0, PAIRS - 2, step)
                    step(PAIRS - 2, 0)
                    step(PAIRS - 1, 1)
                    dve.drain()
                    for h in range(DH):
                        dve.bn_aggr(mv[:, h, :], bst[:, h, :, :].rearrange("p t n -> p (t n)"))
                    dve.drain()
                    dve.tensor_scalar(rv[:], mv[:, :, 1], 1e-5, None, ALU.add).then_inc(var_ready, 1)
                    dve.wait_ge(root_ready, 1)
                    dve.reciprocal(xscale[:], rt[:])
                    dve.drain()
                    newton(dve, xscale[:], rv[:], rtmp[:])
                    dve.wait_ge(gb_in, 32)
                    dve.tensor_tensor(xscale[:], xscale[:], gb[:, 0, :], ALU.mult)
                    dve.drain()
                    dve.tensor_tensor(rt[:], mv[:, :, 0], xscale[:], ALU.mult)
                    dve.drain()
                    dve.tensor_tensor(xbias[:], gb[:, 1, :], rt[:], ALU.subtract)

                @block.tensor
                def _(pe):
                    def turn(i, k):
                        pe.wait_ge(y_ready, i + 1)
                        wait_count(pe, yT_ready, i - 1)
                        for a in range(2):
                            for h in range(DH):
                                mm = pe.transpose(psT[:, k, (h * 2 + a) * P:(h * 2 + a + 1) * P],
                                                  y[:, k, a, h * P:(h + 1) * P], ident[:])
                        mm.then_inc(transposed, 1)

                    def fold(n):
                        hd, half = n // 2, n % 2
                        if n == 0:
                            pe.wait_ge(w_in, 32)
                        if n >= 2:
                            pe.wait_ge(fold_copied, n - 1)
                        for r in range(H):
                            mm = pe.matmul(psW[:, n % 2, r * NK:(r + 1) * NK], wq[:, half * H + r, hd * P:(hd + 1) * P],
                                           kT[:, half * H + r, :], start=True, stop=True)
                        mm.then_inc(folded, 1)

                    turn(0, 0)
                    turn(1, 1)
                    for n in range(2 * DH):
                        pairs_of(pe, max(2, n * QUARTER), (n + 1) * QUARTER, turn)
                        fold(n)

                @block.scalar
                def _(act):
                    def yT_pair(i, k):
                        act.wait_ge(transposed, i + 1)
                        wait_count(act, stats_done, i - 1)
                        wait_count(act, stored[k], 16 * ((i - k) // 2) if static(i) else 8 * (i - k))
                        act.activation(yT[:, k, :, :, :].rearrange("p h a n -> p (h a n)"), psT[:, k, :], ACT.Copy
                                       ).then_inc(yT_ready, 1)

                        act.wait_ge(keys_in[k], 32 * ((i - k) // 2 + 1) if static(i) else 16 * (i - k) + 32)
                        for which, keys in ((0, keyin), (1, keyout)):
                            act.activation(piece_of(keys, 0, i), raw[:, k, which, :], ACT.Copy, scale=KS
                                           ).then_inc(key_high, 1)

                    yT_pair(0, 0)
                    yT_pair(1, 1)
                    for n in range(2 * DH):
                        pairs_of(act, max(2, n * QUARTER), (n + 1) * QUARTER, yT_pair)
                        act.wait_ge(folded, n + 1)
                        act.activation(wc[:, n // 2, (n % 2) * 512:(n % 2 + 1) * 512], psW[:, n % 2, :],
                                       ACT.Copy).then_inc(fold_copied, 1)
                    act.wait_ge(var_ready, 1)
                    act.activation(rt[:], rv[:], ACT.Sqrt).then_inc(root_ready, 1)

        with Chip(nc, name + "b") as b:
            yTd = b.sb("yTd", [P, DH, P])
            yTs = b.sb("yTs", [P, DH, P])
            xnT = b.sb("xnT", [P, DH, P])
            sim = b.sb("sim", [P, S])
            top = b.sb("top", [P, 2 * H, K])
            topi = b.sb("topi", [P, 2 * H, K], U32)
            topf = b.sb("topf", [P, 2 * H, K])
            pairs = b.sb("pairs", [P, H * K * K])
            pair = pairs[:].rearrange("p (h a b) -> p h a b", h=H, a=K)
            hot = pairs[:].bitcast(F16).rearrange("p (a n k) -> p a n k", a=2, k=K)
            best = b.sb("best", [P, H, K])
            pick = b.sb("pick", [P, H, K], U32)
            rank = b.sb("rank", [P, 2, HK], U32)
            ixy = b.sb("ixy", [P, 2, HK])
            upper = b.sb("upper", [P, HK])
            hi = b.sb("hi", [P, HK])
            lo = b.sb("lo", [P, HK])
            expo = b.sb("expo", [P, H, K])
            ex = b.sb("ex", [P, H, K])
            total = b.sb("total", [P, H])
            inv = b.sb("inv", [P, H])
            wt = b.sb("wt", [P, HK])
            NC = 5
            cat = b.sb("cat", [P, NC, 2, HK], F16)
            catT = b.sb("catT", [P, 2, NC, P // 2], F16)
            iota8 = b.sb("iota8", [P, K], U32)
            iota64 = b.sb("iota64", [P, NK, HM], F16)
            left = b.sb("left", [P, 2, P, HM], F16)
            right = b.sb("right", [P, 2, 2, 2 * NJ, HM], F16)
            A = b.sb("A", [P, 2, NJ, P])
            G = b.sb("G", [P, RING, JG * P])
            GP = b.sb("GP", [P, RING, 2, JG * P], F16)
            yTp = b.sb("yTp", [P, 2, 2, DH, P], F16)
            psO = b.ps("psO", [P, 2, 512])
            psA = b.ps("psA", [P, 2, 512])
            psS = b.ps("psS", [P, 512])
            psX = b.ps("psX", [P, 2, 512])
            psI = b.ps("psI", [P, 1024], F16)

            experts_in = [b.sem("experts_in0"), b.sem("experts_in1")]
            simil_in = [b.sem("simil_in0"), b.sem("simil_in1")]
            xn_ready, sims_done, sim_ready, sim_used = (b.sem(n) for n in ("xn_ready", "sims_done", "sim_ready", "sim_used"))
            expo_ready, ex_ready, cat_ready, cat_turned, catT_ready = (
                b.sem(n) for n in ("expo_ready", "ex_ready", "cat_ready", "cat_turned", "catT_ready"))
            factors_ready, built, A_ready = b.sem("factors_ready"), b.sem("built"), b.sem("A_ready")
            hot_ready, rest_ready = b.sem("hot_ready"), b.sem("rest_ready")
            o_done, gelu_done, prod_ready, prod_used, x_added = (
                b.sem(n) for n in ("o_done", "gelu_done", "prod_ready", "prod_used", "x_added"))
            y_high, y_split, high_ready, parts_ready = (
                b.sem(n) for n in ("y_high", "y_split", "high_ready", "parts_ready"))
            consts = b.sem("consts")

            LEAD = 4

            def run(eng, step):
                for t in range(-LEAD, 2):
                    step(t, t // 2)
                with eng.Fori(1, (NT - LEAD) // 2) as i:
                    for k in range(2):
                        step(2 * i + k, i, k)
                for t in range(NT - LEAD, NT):
                    step(t, t // 2)

            def has(t):
                return not static(t) or 0 <= t < NT

            with nc.Block() as block:
                @block.gpsimd
                def _(pool):
                    pool.iota(iota8[:], [[1, K]], base=0, channel_multiplier=0)
                    pool.iota(iota64[:], [[1, NK], [0, HM]], base=0, channel_multiplier=0,
                              allow_small_or_imprecise_dtypes=True).then_inc(consts, 1)

                    def rest(u, h, n, k):
                        cols = slice(n * NJ, (n + 1) * NJ)
                        pool.wait_ge(hot_ready, 2 * u + h + 1)
                        pool.tensor_tensor(right[:, h, 1, cols, :], right[:, h, 0, cols, :],
                                           catT[:, k, 4, h * HM:(h + 1) * HM].unsqueeze(1).broadcast_to([P, NJ, HM]),
                                           ALU.mult).then_inc(rest_ready, 1)

                    def low(t, g):
                        pool.wait_ge(high_ready, NG * t + g + 1)
                        pool.tensor_tensor(GP[:, g % RING, 1, :], G[:, g % RING, :], GP[:, g % RING, 0, :], ALU.subtract
                                           ).then_inc(parts_ready, 1)

                    def step(t, i, k=None):
                        k = t % 2 if k is None else k
                        for g in range(NG):
                            for n in range(2):
                                if g == 0 and has(t + 1):
                                    rest(t + 1, 1, n, 1 - k)
                                if g == 4 and has(t + 2):
                                    rest(t + 2, 0, n, k)
                            if has(t):
                                low(t, g)
                            if g == 4 and has(t + 1):
                                pool.wait_ge(y_high, t + 2)
                                pool.tensor_tensor(yTp[:, 1 - k, 1, :, :], yTd[:], yTp[:, 1 - k, 0, :, :],
                                                   ALU.subtract).then_inc(y_split, 1)
                    run(pool, step)

                @block.sync
                def _(sp):
                    def step(t, i, k=None):
                        k = t % 2 if k is None else k
                        u = t + LEAD
                        if has(u):
                            wait_count(sp, xn_ready, u)
                            sp.dma_start(yTs[:].rearrange("p h n -> p (h n)"), dram_tile(yT_dram, u)
                                         ).then_inc(simil_in[k], 16)
                        v = t + 1
                        if has(v):
                            wait_count(sp, y_split, v)
                            sp.dma_start(yTd[:].rearrange("p h n -> p (h n)"), dram_tile(yT_dram, v)
                                         ).then_inc(experts_in[1 - k], 16)
                    run(sp, step)

                @block.tensor
                def _(pe):
                    PASSES = ((0, 0), (0, 1), (1, 0))

                    def experts(t, g, k, i):
                        if g == 0:
                            pe.wait_ge(y_split, t + 1)
                        wait_count(pe, gelu_done, NG * t + g - 1)
                        for j in range(JG):
                            for h in range(DH):
                                at = h * NE + (g * JG + j) * P
                                for n, (kp, yp) in enumerate(PASSES):
                                    mm = pe.matmul(psO[:, g % 2, j * P:(j + 1) * P], keyin[:, kp, at:at + P],
                                                   yTp[:, k, yp, h, :], start=(h == 0 and n == 0),
                                                   stop=(h == DH - 1 and n == 2))
                        mm.then_inc(o_done, 1)

                    def combine(t, g, k):
                        pe.wait_ge(parts_ready, NG * t + g + 1)
                        if g == 0:
                            wait_count(pe, x_added, t - 1)
                        for j in range(JG):
                            jj = g * JG + j
                            for n, (gp, kp) in enumerate(PASSES):
                                mm = pe.matmul(psX[:, k, 0:D], GP[:, g % RING, gp, j * P:(j + 1) * P],
                                               keyout[:, kp, jj * D:(jj + 1) * D],
                                               start=(jj == 0 and n == 0), stop=(jj == NJ - 1 and n == 2))
                        mm.then_inc(prod_used, 1)

                    def build(u, q):
                        h = q // (NG // 2)
                        pe.wait_ge(factors_ready, 2 * u + h + 1)
                        wait_count(pe, A_ready, NG * u + q - 1)
                        for n in range(MQ):
                            m = (q * MQ + n) % HM
                            for part in range(2):
                                mm = pe.matmul(psA[:, q % 2, n * 2 * NJ:(n + 1) * 2 * NJ], left[:, h, :, m],
                                               right[:, h, part, :, m], start=(part == 0), stop=(part == 1))
                        mm.then_inc(built, 1)

                    def similarities(u, s):
                        pe.wait_ge(xn_ready, u + 1)
                        wait_count(pe, sim_ready, 2 * u + s)
                        for h in range(DH):
                            mm = pe.matmul(psS[:], xnT[:, h, :], wc[:, h, s * 512:(s + 1) * 512],
                                           start=(h == 0), stop=(h == DH - 1))
                        mm.then_inc(sims_done, 1)

                    def turn(u):
                        pe.wait_ge(cat_ready, u + 1)
                        wait_count(pe, catT_ready, u)
                        for n in range(NC):
                            mm = pe.transpose(psI[:, n * P:(n + 1) * P], cat[:, n, :, :].rearrange("p s n -> p (s n)"),
                                              ident16[:])
                        mm.then_inc(cat_turned, 1)

                    def step(t, i, k=None):
                        k = t % 2 if k is None else k
                        for g in range(NG):
                            if has(t):
                                experts(t, g, k, i)
                            if g == 1 and has(t + 2):
                                turn(t + 2)
                            if has(t + 1):
                                build(t + 1, g)
                            if g >= LAG and has(t):
                                combine(t, g - LAG, k)
                            if g < LAG and has(t - 1) and not (static(t) and t == 0):
                                combine(t - 1, NG - LAG + g, 1 - k)
                            if g in (3, 5) and has(t + LEAD):
                                similarities(t + LEAD, g // 5)
                    run(pe, step)
                    for g in range(NG - LAG, NG):
                        combine(NT - 1, g, 1)

                @block.scalar
                def _(act):
                    def high(t, g):
                        act.wait_ge(prod_ready, NG * t + g + 1)
                        wait_count(act, prod_used, NG * t + g - RING + 1)
                        act.activation(GP[:, g % RING, 0, :], G[:, g % RING, :], ACT.Copy).then_inc(high_ready, 1)

                    def step(t, i, k=None):
                        k = t % 2 if k is None else k
                        u = t + LEAD
                        for g in range(NG):
                            if g == 0 and has(u):
                                act.wait_ge(simil_in[k], 16 * (i + LEAD // 2 + 1))
                                wait_count(act, sims_done, 2 * u)
                                for h in range(DH):
                                    ins = act.activation(xnT[:, h, :], yTs[:, h, :], ACT.Identity,
                                                         scale=xscale[:, h:h + 1], bias=xbias[:, h:h + 1])
                                ins.then_inc(xn_ready, 1)
                            if has(t):
                                act.wait_ge(o_done, NG * t + g + 1)
                                wait_count(act, parts_ready, NG * t + g - RING + 1)
                                act.activation(G[:, g % RING, :], psO[:, g % 2, :], ACT.Gelu, scale=1 / KS
                                               ).then_inc(gelu_done, 1)
                            if g == 2 and has(t + 2):
                                v = t + 2
                                act.wait_ge(cat_turned, v + 1)
                                wait_count(act, factors_ready, 2 * v - 2)
                                for s in range(2):
                                    src = psI[64 * s:64 * s + 64, 0:NC * P].rearrange("p (n s m) -> p n s m", n=NC, s=2)
                                    ins = act.activation(catT[64 * s:64 * s + 64, k, :, :], src[:, :, s, :], ACT.Copy)
                                ins.then_inc(catT_ready, 1)
                            if has(t + 1):
                                act.wait_ge(built, NG * (t + 1) + g + 1)
                                wait_count(act, prod_ready, NG * t)
                                dst = A[:, 1 - k, :, :].rearrange("p j (s m) -> p j s m", s=2)[:, :, :, g * MQ:(g + 1) * MQ]
                                src = psA[:, g % 2, :].rearrange("p (m s j) -> p j s m", s=2, j=NJ)
                                act.activation(dst, src, ACT.Copy, scale=PS / WS).then_inc(A_ready, 1)
                            if g > 0 and has(t):
                                high(t, g - 1)
                            if g == 0 and has(t - 1) and not (static(t) and t == 0):
                                high(t - 1, NG - 1)
                            if g == 6 and has(t + 3):
                                act.wait_ge(expo_ready, t + 4)
                                act.activation(ex[:], expo[:], ACT.Exp).then_inc(ex_ready, 1)
                            if g in (4, 6) and has(u):
                                half = g // 6
                                act.wait_ge(sims_done, 2 * u + half + 1)
                                wait_count(act, sim_used, u)
                                act.activation(sim[:, half * 512:(half + 1) * 512], psS[:], ACT.Copy).then_inc(sim_ready, 1)
                            if g == 3 and has(t + 1):
                                act.wait_ge(experts_in[1 - k], 16 * ((t + 1) // 2 + 1 if static(t) else i + k + 1))
                                wait_count(act, o_done, NG * t)
                                act.activation(yTp[:, 1 - k, 0, :, :], yTd[:], ACT.Copy).then_inc(y_high, 1)
                    run(act, step)
                    high(NT - 1, NG - 1)

                @block.vector
                def _(dve):
                    flat = lambda ap: ap.rearrange("p h k -> p (h k)")

                    def product(t, g, k):
                        dve.wait_ge(gelu_done, NG * t + g + 1)
                        if g == 0:
                            dve.wait_ge(A_ready, NG * t + NG)
                        dve.tensor_tensor(G[:, g % RING, :], G[:, g % RING, :],
                                          A[:, k, g * JG:(g + 1) * JG, :].rearrange("p j n -> p (j n)"),
                                          ALU.mult).then_inc(prod_ready, 1)

                    def factors(u, h, stage, k):
                        ms = slice(h * HM, (h + 1) * HM)
                        def row(n):
                            return catT[:, k, n, ms].unsqueeze(1).broadcast_to([P, NK, HM])
                        if stage == 0:
                            dve.wait_ge(catT_ready, u + 1)
                            wait_count(dve, built, NG * (u - 1) + (NG // 2) * (h + 1))
                            dve.tensor_tensor(left[:, h, 0:NK, :], iota64[:], row(0), ALU.is_equal)
                            dve.tensor_tensor(right[:, h, 0, :, :], iota64[:], row(2), ALU.is_equal).then_inc(hot_ready, 1)
                        elif stage == 1:
                            dve.tensor_tensor(left[:, h, NK:P, :], iota64[:], row(1), ALU.is_equal)
                        elif stage == 3:
                            dve.drain()
                            dve.wait_ge(rest_ready, 4 * u + 2 * h + 2)
                            dve.tensor_tensor(right[:, h, 0, :, :], right[:, h, 0, :, :], row(3), ALU.mult
                                              ).then_inc(factors_ready, 1)

                    def picks(u, g):
                        if g == 0:
                            for r in range(2 * H):
                                dve.max(top[:, r, :], sim[:, r * NK:(r + 1) * NK])
                        elif g == 1:
                            dve.drain()
                            for r in range(2 * H):
                                ins = dve.max_index(topi[:, r, :], top[:, r, :], sim[:, r * NK:(r + 1) * NK])
                            ins.then_inc(sim_used, 1)
                            dve.tensor_tensor(pair, top[:, 0:H, :].unsqueeze(3).broadcast_to([P, H, K, K]),
                                              top[:, H:2 * H, :].unsqueeze(2).broadcast_to([P, H, K, K]), ALU.add)
                        elif g == 2:
                            dve.drain()
                            dve.tensor_copy(topf[:], topi[:])
                            for r in range(H):
                                dve.max(best[:, r, :], pair[:, r, :, :].rearrange("p a b -> p (a b)"))
                        elif g == 3:
                            dve.drain()
                            dve.tensor_tensor(expo[:], best[:], best[:, :, 0:1].broadcast_to([P, H, K]),
                                              ALU.subtract).then_inc(expo_ready, 1)
                            for r in range(H):
                                dve.max_index(pick[:, r, :], best[:, r, :], pair[:, r, :, :].rearrange("p a b -> p (a b)"))
                        elif g == 4:
                            dve.drain()
                            dve.tensor_scalar(rank[:, 0, :], flat(pick[:]), 3, None, ALU.logical_shift_right)
                            dve.tensor_scalar(rank[:, 1, :], flat(pick[:]), K - 1, None, ALU.bitwise_and)
                            dve.drain()
                            dve.tensor_tensor(hot.rearrange("p a n k -> p (a n) k"),
                                              rank[:].rearrange("p a n -> p (a n)").unsqueeze(2).broadcast_to([P, 2 * HK, K]),
                                              iota8[:].unsqueeze(1).broadcast_to([P, 2 * HK, K]), ALU.is_equal)
                        elif g == 5:
                            dve.drain()
                            hv = hot.rearrange("p a (h r) k -> p (a h) r k", h=H)
                            dve.tensor_tensor(hv, hv, topf[:].unsqueeze(2).broadcast_to([P, 2 * H, K, K]), ALU.mult)
                        elif g == 6:
                            dve.drain()
                            dve.tensor_reduce(ixy[:].rearrange("p a n -> p (a n)"),
                                              hot.rearrange("p a n k -> p (a n) k"), AX_X, ALU.add)
                            dve.drain()
                            dve.tensor_scalar(upper[:], ixy[:, 1, :], float(NJ), None, ALU.is_ge)
                            dve.drain()
                            dve.scalar_tensor_tensor(out=hi[:], in0=ixy[:, 0, :], scalar=2.0, in1=upper[:],
                                                     op0=ALU.mult, op1=ALU.add)
                            dve.scalar_tensor_tensor(out=lo[:], in0=upper[:], scalar=-float(NJ), in1=ixy[:, 1, :],
                                                     op0=ALU.mult, op1=ALU.add)
                        else:
                            dve.wait_ge(ex_ready, u + 1)
                            dve.tensor_reduce(total[:], ex[:], AX_X, ALU.add)
                            twice = lambda ap: ap.unsqueeze(1).broadcast_to([P, 2, HK])
                            dve.drain()
                            wait_count(dve, cat_turned, u)
                            dve.reciprocal(inv[:], total[:])
                            dve.tensor_scalar(cat[:, 0, :, :], twice(hi[:]), 1.0, None, ALU.mult)
                            dve.tensor_scalar(cat[:, 1, :, :], twice(hi[:]), -float(NK), None, ALU.add)
                            dve.tensor_scalar(cat[:, 2, 0, :], lo[:], 1.0, None, ALU.mult)
                            dve.tensor_scalar(cat[:, 2, 1, :], lo[:], float(NJ), None, ALU.add)
                            dve.drain()
                            dve.scalar_tensor_tensor(out=wt[:].rearrange("p (h k) -> p h k", h=H), in0=ex[:], scalar=WS,
                                                     in1=inv[:].unsqueeze(2).broadcast_to([P, H, K]),
                                                     op0=ALU.mult, op1=ALU.mult)
                            dve.drain()
                            dve.tensor_scalar(cat[:, 3, :, :], twice(wt[:]), 1.0, None, ALU.mult)
                            dve.drain()
                            dve.tensor_tensor(cat[:, 4, :, :], twice(wt[:]), cat[:, 3, :, :], ALU.subtract
                                              ).then_inc(cat_ready, 1)

                    def add_x(t, k):
                        dve.wait_ge(prod_used, NG * t + NG)
                        xt = tile_of(x, t)
                        dve.scalar_tensor_tensor(out=xt, in0=psX[:, k, 0:D], scalar=0.5 / (PS * KS), in1=xt,
                                                 op0=ALU.mult, op1=ALU.add).then_inc(x_added, 1)

                    def step(t, i, k=None):
                        k = t % 2 if k is None else k
                        for g in range(NG):
                            if g == LAG + 1 and has(t - 1) and not (static(t) and t == 0):
                                add_x(t - 1, 1 - k)
                            if g == 3 and has(t + 1):
                                factors(t + 1, 1, 3, 1 - k)
                            if g == 7 and has(t + 2):
                                factors(t + 2, 0, 3, k)
                            if has(t):
                                product(t, g, k)
                            if g == 0 and has(t + 3):
                                dve.wait_ge(sim_ready, 2 * (t + 4))
                            if g < 3 and has(t + 1):
                                factors(t + 1, 1, g, 1 - k)
                            if 4 <= g < 7 and has(t + 2):
                                factors(t + 2, 0, g - 4, k)
                            if has(t + 3):
                                picks(t + 3, g)

                    dve.wait_ge(consts, 1)
                    run(dve, step)
                    add_x(NT - 1, 1)



def moe_ffn(nc, name, x, ident, NT, w):
    gate_w, gate_b, expert_w, expert_b = w
    E, KTOP = 8, 2
    SCORE_EPS, W_MIN = 1e-4, 0.1
    GT = 4
    NGR = NT // GT
    DUOS = 2 * E // 2
    with Chip(nc, name) as c:
        mean, rstd = c.sb("mean", [P, NT]), c.sb("rstd", [P, NT])
        row_statistics(nc, name, x, NT, mean, rstd)
        ew = c.sb("ew", [P, DH, E * D])
        eb = c.sb("eb", [E, D])
        gw = c.sb("gw", [P, DH, E])
        gb = c.sb("gb", [1, E])
        ones = c.sb("ones", [1, P])
        iota = c.sb("iota", [P, E], U32)
        y = c.sb("y", [P, GT, D])
        yT = c.sb("yT", [P, 2, GT, DH, P])
        score = c.sb("score", [P, GT, E])
        big = c.sb("big", [P, GT])
        diff = c.sb("diff", [P, GT, E])
        ex = c.sb("ex", [P, GT, E])
        total = c.sb("total", [P, GT])
        prob = c.sb("prob", [P, GT, E])
        best = c.sb("best", [P, GT, 8])
        besti = c.sb("besti", [P, GT, 8], U32)
        chosen = c.sb("chosen", [P, 2, GT, E])
        two = c.sb("two", [P, GT, 2])
        comb = c.sb("comb", [P, 2, GT, E])
        combT = c.sb("combT", [E, GT, P])
        psY = c.ps("psY", [P, 2, 2, 512])
        psT = c.ps("psT", [P, 512])
        psL = c.ps("psL", [P, 512])
        psB = c.ps("psB", [P, 512])
        w_in, consts = c.sem("w_in"), c.sem("consts")
        y_ready, turned, turn_copied = c.sem("y_ready"), c.sem("turned"), c.sem("turn_copied")
        logits_done, diff_ready, ex_ready, comb_ready = (
            c.sem(n) for n in ("logits_done", "diff_ready", "ex_ready", "comb_ready"))
        duo_done, duo_used, bias_done, bias_added = (
            c.sem(n) for n in ("duo_done", "duo_used", "bias_done", "bias_added"))
        TURNS = 3

        def run(eng, step):
            for n in range(-1, min(2, NGR)):
                step(n, n % 2)
            if NGR > 4:
                with eng.Fori(1, (NGR - 2) // 2) as i:
                    for k in range(2):
                        step(2 * i + k, k)
            for n in range(max(NGR - 2, 2), NGR):
                step(n, n % 2)

        def has(n):
            return not static(n) or 0 <= n < NGR

        def turns_before(n):
            if static(n) and n == 0:
                return 0
            return TURNS * n - 1

        def turns_of_comb(n):
            return TURNS * n + (4 if not static(n) or n < NGR - 1 else 2)

        with nc.Block() as block:
            @block.gpsimd
            def _(pool):
                pool.iota(iota[:], [[1, E]], base=0, channel_multiplier=0)
                pool.memset(ones[:], 1.0).then_inc(consts, 1)

            @block.sync
            def _(sp):
                sp.dma_start(gw[:], gate_w.rearrange("(h p) e -> p h e", p=P)).then_inc(w_in, 16)
                sp.dma_start(gb[:], gate_b.rearrange("(a e) -> a e", a=1)).then_inc(w_in, 16)
                sp.dma_start(eb[:], expert_b).then_inc(w_in, 16)
                for h in range(DH):
                    sp.dma_start(ew[:, h, :].rearrange("p (e f) -> p e f", e=E),
                                 expert_w.rearrange("e (h p) f -> h p e f", p=P)[h]).then_inc(w_in, 16)

            @block.tensor
            def _(pe):
                pe.wait_ge(consts, 1)
                pe.wait_ge(w_in, 16 * (3 + DH))

                def turn_tiles(n, half):
                    if half == 0:
                        pe.wait_ge(y_ready, n + 1)
                    wait_count(pe, turn_copied, turns_before(n) + half)
                    for a in range(2):
                        for h in range(DH):
                            mm = pe.transpose(psT[:, (a * DH + h) * P:(a * DH + h + 1) * P],
                                              y[:, 2 * half + a, h * P:(h + 1) * P], ident[:])
                    mm.then_inc(turned, 1)

                def turn_comb(n, k):
                    pe.wait_ge(comb_ready, n + 1)
                    wait_count(pe, turn_copied, turns_of_comb(n))
                    for a in range(GT):
                        mm = pe.transpose(psT[0:E, a * P:(a + 1) * P], comb[:, k, a, :], ident[:])
                    mm.then_inc(turned, 1)

                def bias(n, half):
                    pe.wait_ge(turn_copied, turns_of_comb(n) + 1)
                    wait_count(pe, bias_added, 2 * n + half)
                    for a in range(2):
                        mm = pe.matmul(psB[:, a * D:(a + 1) * D], combT[:, 2 * half + a, :], eb[:],
                                       start=True, stop=True)
                    mm.then_inc(bias_done, 1)

                def logits(n, k):
                    pe.wait_ge(turn_copied, turns_before(n) + 2)
                    wait_count(pe, diff_ready, n)
                    for a in range(GT):
                        for h in range(DH):
                            pe.matmul(psL[:, a * E:(a + 1) * E], yT[:, k, a, h, :], gw[:, h, :],
                                      start=(h == 0), stop=False)
                        mm = pe.matmul(psL[:, a * E:(a + 1) * E], ones[:], gb[:], start=False, stop=True)
                    mm.then_inc(logits_done, 1)

                def duo(n, u, k):
                    ep, tp = u % (E // 2), u // (E // 2)
                    wait_count(pe, duo_used, DUOS * n + u - 1)
                    for a in range(2):
                        for h in range(DH):
                            mm = pe.matmul(psY[:, u % 2, a, :], yT[:, k, 2 * tp + a, h, :],
                                           ew[:, h, ep * 2 * D:(ep + 1) * 2 * D], start=(h == 0), stop=(h == DH - 1))
                    mm.then_inc(duo_done, 1)

                def step(n, k):
                    for u in range(DUOS):
                        if has(n):
                            duo(n, u, k)
                        if u in (0, 1) and has(n + 1):
                            turn_tiles(n + 1, u)
                        if u == 2 and has(n):
                            turn_comb(n, k)
                        if u in (3, 5) and has(n):
                            bias(n, (u - 3) // 2)
                        if u == 4 and has(n + 1):
                            logits(n + 1, 1 - k)
                run(pe, step)

            @block.scalar
            def _(act):
                def copy_tiles(n, half, k):
                    act.wait_ge(turned, turns_before(n) + half + 1)
                    act.activation(yT[:, k, 2 * half:2 * half + 2, :, :].rearrange("p a h n -> p (a h n)"), psT[:],
                                   ACT.Copy).then_inc(turn_copied, 1)

                def copy_comb(n):
                    act.wait_ge(turned, turns_of_comb(n) + 1)
                    wait_count(act, bias_done, 2 * n)
                    act.activation(combT[:].rearrange("e a n -> e (a n)"), psT[0:E, :], ACT.Copy
                                   ).then_inc(turn_copied, 1)

                def step(n, k):
                    if has(n + 1):
                        copy_tiles(n + 1, 0, 1 - k)
                        copy_tiles(n + 1, 1, 1 - k)
                    if has(n):
                        copy_comb(n)
                    if has(n + 1):
                        act.wait_ge(diff_ready, n + 2)
                        act.activation(ex[:], diff[:], ACT.Exp).then_inc(ex_ready, 1)
                run(act, step)

            @block.vector
            def _(dve):
                def normalise(n):
                    wait_count(dve, turned, turns_before(n - 1) + 2 if not static(n) or n > 0 else 0)
                    for a in range(GT):
                        t = GT * n + a
                        ins = dve.tensor_scalar(y[:, a, :], tile_of(x, t), mean[:, one(t)], rstd[:, one(t)],
                                                ALU.subtract, ALU.mult)
                    ins.then_inc(y_ready, 1)

                def route_scores(n):
                    dve.wait_ge(logits_done, n + 1)
                    dve.tensor_scalar(score[:].rearrange("p a e -> p (a e)"), psL[:, 0:GT * E], SCORE_EPS, None, ALU.max)
                    dve.drain()
                    dve.tensor_reduce(big[:], score[:], AX_X, ALU.max)
                    dve.drain()
                    dve.tensor_tensor(diff[:], score[:], big[:].unsqueeze(2).broadcast_to([P, GT, E]), ALU.subtract
                                      ).then_inc(diff_ready, 1)

                def route_weights(n, k):
                    wide = lambda ap: ap.unsqueeze(2).broadcast_to([P, GT, E])
                    dve.wait_ge(ex_ready, n + 1)
                    dve.tensor_reduce(total[:], ex[:], AX_X, ALU.add)
                    dve.drain()
                    dve.reciprocal(total[:], total[:])
                    dve.drain()
                    dve.tensor_tensor(prob[:], ex[:], wide(total[:]), ALU.mult)
                    dve.drain()
                    for a in range(GT):
                        dve.max(best[:, a, :], prob[:, a, :])
                    dve.drain()
                    for a in range(GT):
                        dve.max_index(besti[:, a, :], best[:, a, :], prob[:, a, :])
                    dve.tensor_scalar(two[:], best[:, :, 0:KTOP], W_MIN, None, ALU.max)
                    dve.drain()
                    for q in range(KTOP):
                        dve.tensor_tensor(chosen[:, q, :, :], iota[:].unsqueeze(1).broadcast_to([P, GT, E]),
                                          besti[:, :, q:q + 1].broadcast_to([P, GT, E]), ALU.is_equal)
                    dve.tensor_reduce(total[:], two[:], AX_X, ALU.add)
                    dve.tensor_scalar(prob[:], prob[:], W_MIN, 0.5 / KTOP, ALU.max, ALU.mult)
                    dve.drain()
                    dve.reciprocal(total[:], total[:])
                    dve.tensor_tensor(chosen[:, 0, :, :], chosen[:, 0, :, :], chosen[:, 1, :, :], ALU.add)
                    dve.drain()
                    dve.tensor_tensor(prob[:], prob[:], wide(total[:]), ALU.mult)
                    dve.drain()
                    dve.tensor_tensor(comb[:, k, :, :], prob[:], chosen[:, 0, :, :], ALU.mult).then_inc(comb_ready, 1)

                def combine(n, u, k):
                    ep, tp = u % (E // 2), u // (E // 2)
                    for q in range(2):
                        e = 2 * ep + q
                        dve.drain()
                        if q == 0:
                            dve.wait_ge(duo_done, DUOS * n + u + 1)
                        for a in range(2):
                            ta = 2 * tp + a
                            xt = tile_of(x, GT * n + ta)
                            ins = dve.scalar_tensor_tensor(out=xt, in0=psY[:, u % 2, a, q * D:(q + 1) * D],
                                                           scalar=comb[:, k, ta, e:e + 1], in1=xt,
                                                           op0=ALU.mult, op1=ALU.add)
                    ins.then_inc(duo_used, 1)

                def add_bias(n, half):
                    dve.drain()
                    dve.wait_ge(bias_done, 2 * n + half + 1)
                    t = GT * n + 2 * half
                    xt = (x[:, t:t + 2, :] if static(t) else x[:, bass.ds(t, 2), :]).rearrange("p a n -> p (a n)")
                    dve.tensor_tensor(xt, psB[:], xt, ALU.add).then_inc(bias_added, 1)

                dve.wait_ge(consts, 1)

                def step(n, k):
                    if has(n + 1):
                        normalise(n + 1)
                    for u in range(DUOS):
                        if has(n):
                            combine(n, u, k)
                        if u == 4 and has(n):
                            add_bias(n, 0)
                        if u == 5 and has(n + 1):
                            route_scores(n + 1)
                        if u == 7:
                            if has(n):
                                add_bias(n, 1)
                            if has(n + 1):
                                route_weights(n + 1, 1 - k)
                run(dve, step)



def recurrent_block(nc, name, x, ident, NT, SEQ, w):
    norm1, norm2, in_projT, out_projT, fcT, projT = w
    HD = 16
    CH = 64
    GT = 4
    SEG = GT * P
    NS = NT // GT
    NC = SEG // CH
    PARTS = 5
    F = fcT.shape[2]
    MF = F // P
    RES = float(1.0 / np.sqrt(2.0))
    QEPS = float(np.finfo(np.float32).eps)
    with Chip(nc, name) as c:
        mean, rstd, var_eps = c.sb("mean", [P, NT]), c.sb("rstd", [P, NT]), c.sb("var_eps", [P, NT])
        row_statistics(nc, name, x, NT, mean, rstd, var_eps)
        wi = c.sb("wi", [P, DH, PARTS * D])
        wo = c.sb("wo", [P, DH, D])
        wf = c.sb("wf", [P, DH, F])
        wp = c.sb("wp", [P, MF, D])
        n1, n2 = c.sb("n1", [P, DH]), c.sb("n2", [P, DH])
        scale1 = c.sb("scale1", [P, NT])
        t1, t2, t3 = c.sb("t1", [P, NT]), c.sb("t2", [P, NT]), c.sb("t3", [P, NT])
        heads = c.sb("heads", [P, P])
        goes_on = c.sb("goes_on", [P, NS])
        inside = c.sb("inside", [P, SEG])
        two_bias, q_eps, r_eps = c.sb("two_bias", [P, 1]), c.sb("q_eps", [P, 1]), c.sb("r_eps", [P, 1])
        y = c.sb("y", [P, GT, D])
        h1T = c.sb("h1T", [P, DH, SEG])
        seg = lambda n: c.sb(n, [P, DH, SEG])
        q, k, v, a, g, qq, rq = (seg(n) for n in ("q", "k", "v", "a", "g", "qq", "rq"))
        first, prefix, ratio, acc, mixed = (seg(n) for n in ("first", "prefix", "ratio", "acc", "mixed"))
        chunk_end = c.sb("chunk_end", [P, DH, NC])
        prefix_end = c.sb("prefix_end", [P, DH, NC])
        state = c.sb("state", [P, DH, NC + 1])
        x1 = c.sb("x1", [P, GT, D])
        sq = c.sb("sq", [P, D])
        ms, root2, r2, r2t = (c.sb(n, [P, GT]) for n in ("ms", "root2", "r2", "r2t"))
        h2 = c.sb("h2", [P, GT, D])
        h2T = c.sb("h2T", [P, DH, SEG])
        hid = c.sb("hid", [P, MF, SEG])
        psR = c.ps("psR", [P, 2, 512])
        psT = c.ps("psT", [P, 512])
        psX = c.ps("psX", [P, 2, 512])
        psM = c.ps("psM", [P, 2, 512])
        w_in, consts, sq1_ready, root1_ready, weights_ready = (
            c.sem(n) for n in ("w_in", "consts", "sq1_ready", "root1_ready", "weights_ready"))
        y_ready, turned, turn_copied, filled, emptied = (
            c.sem(n) for n in ("y_ready", "turned", "turn_copied", "filled", "emptied"))
        qq_ready, mixed_ready, attn_done, x1_ready, ms_ready, root2_ready, h2_ready = (
            c.sem(n) for n in ("qq_ready", "mixed_ready", "attn_done", "x1_ready", "ms_ready", "root2_ready", "h2_ready"))
        mlp_done, mlp_added = c.sem("mlp_done"), c.sem("mlp_added")
        TILES_P = PARTS * DH
        USES = TILES_P + MF + DH

        def psr_base(n):
            return 0 if static(n) and n <= 0 else USES * n - MF

        def fc_base(n):
            return psr_base(n) + (TILES_P if not static(n) or n < NS else 0)

        def rms_base(n):
            return psr_base(n) + TILES_P + (MF if not static(n) or n > 0 else 0)

        def turns_h2(n):
            return 4 * n if not static(n) or n < NS else 4 * n - 2

        def turns_h1(n):
            return 0 if static(n) and n < 0 else 4 * n + 2

        def run(eng, step):
            for n in range(-1, min(1, NS)):
                step(n)
            if NS > 2:
                with eng.Fori(1, NS - 1) as n:
                    step(n)
            for n in range(max(1, NS - 1), NS + 1):
                step(n)

        def runs(n):
            return not static(n) or 0 <= n < NS

        with nc.Block() as block:
            @block.gpsimd
            def _(pool):
                pool.memset(heads[:], 1.0 / HD).then_inc(consts, 1)
                pool.memset(goes_on[:], 1.0).then_inc(consts, 1)
                pool.memset(inside[:], 1.0).then_inc(consts, 1)
                pool.memset(first[:], 0.0)
                pool.memset(state[:], 0.0)
                pool.memset(two_bias[:], 2.0)
                pool.memset(q_eps[:], QEPS)
                pool.memset(r_eps[:], 1e-6)
                pool.wait_ge(consts, 3)
                hv = heads[:].rearrange("p (h d) -> p h d", d=HD)
                pool.affine_select(out=hv, in_=hv, compare_op=ALU.is_ge, fill=0.0, base=0,
                                   pattern=[[-HD, P // HD], [0, HD]], channel_multiplier=1).then_inc(consts, 1)
                pool.memset(goes_on[:].rearrange("p (b s) -> p b s", s=SEQ // SEG)[:, :, 0:1], 0.0)
                pool.memset(inside[:].rearrange("p (n c) -> p n c", c=CH)[:, :, 0:1], 0.0)
                pool.wait_ge(consts, 4)
                pool.affine_select(out=hv, in_=hv, compare_op=ALU.is_ge, fill=0.0, base=HD - 1,
                                   pattern=[[HD, P // HD], [0, HD]], channel_multiplier=-1).then_inc(consts, 1)

            @block.sync
            def _(sp):
                sp.dma_start(wi[:], in_projT).then_inc(w_in, 16)
                sp.dma_start(n1[:], norm1).then_inc(w_in, 16)
                sp.dma_start(n2[:], norm2).then_inc(w_in, 16)
                sp.dma_start(wf[:], fcT).then_inc(w_in, 16)
                sp.dma_start(wo[:], out_projT).then_inc(w_in, 16)
                sp.dma_start(wp[:], projT).then_inc(w_in, 16)

            @block.tensor
            def _(pe):
                pe.wait_ge(weights_ready, 1)
                pe.wait_ge(w_in, 96)
                pe.wait_ge(consts, 5)

                def turn(src, base):
                    for half in range(2):
                        wait_count(pe, turn_copied, base + half)
                        for hh in range(DH):
                            for b in range(2):
                                mm = pe.transpose(psT[:, (2 * hh + b) * P:(2 * hh + b + 1) * P],
                                                  src[:, 2 * half + b, hh * P:(hh + 1) * P], ident[:])
                        mm.then_inc(turned, 1)

                def step(n):
                    if runs(n):
                        pe.wait_ge(turn_copied, turns_h1(n - 1) + 2)
                        for m in range(TILES_P):
                            wait_count(pe, emptied, psr_base(n) + m - 1)
                            for hh in range(DH):
                                mm = pe.matmul(psR[:, m % 2, :], wi[:, hh, m * P:(m + 1) * P], h1T[:, hh, :],
                                               start=(hh == 0), stop=(hh == DH - 1))
                            mm.then_inc(filled, 1)
                    if runs(n - 1):
                        pe.wait_ge(h2_ready, n)
                        turn(h2, turns_h2(n))
                        pe.wait_ge(turn_copied, turns_h2(n) + 2)
                        for m in range(MF):
                            wait_count(pe, emptied, fc_base(n) + m - 1)
                            for hh in range(DH):
                                mm = pe.matmul(psR[:, m % 2, :], wf[:, hh, m * P:(m + 1) * P], h2T[:, hh, :],
                                               start=(hh == 0), stop=(hh == DH - 1))
                            mm.then_inc(filled, 1)
                    if runs(n):
                        pe.wait_ge(qq_ready, n + 1)
                        for hh in range(DH):
                            wait_count(pe, emptied, rms_base(n) + hh - 1)
                            pe.matmul(psR[:, hh % 2, :], heads[:], qq[:, hh, :], start=True, stop=True
                                      ).then_inc(filled, 1)
                    if runs(n + 1):
                        pe.wait_ge(y_ready, n + 2)
                        turn(y, turns_h1(n))
                    if runs(n - 1):
                        pe.wait_ge(emptied, fc_base(n) + MF)
                        wait_count(pe, mlp_added, n - 1)
                        for t in range(GT):
                            for m in range(MF):
                                mm = pe.matmul(psM[:, t // 2, (t % 2) * D:(t % 2 + 1) * D], hid[:, m, t * P:(t + 1) * P],
                                               wp[:, m, :], start=(m == 0), stop=(m == MF - 1))
                        mm.then_inc(mlp_done, 1)
                    if runs(n):
                        pe.wait_ge(mixed_ready, n + 1)
                        wait_count(pe, x1_ready, n)
                        for t in range(GT):
                            for hh in range(DH):
                                mm = pe.matmul(psX[:, t // 2, (t % 2) * D:(t % 2 + 1) * D],
                                               mixed[:, hh, t * P:(t + 1) * P], wo[:, hh, :],
                                               start=(hh == 0), stop=(hh == DH - 1))
                        mm.then_inc(attn_done, 1)
                run(pe, step)

            @block.scalar
            def _(act):
                act.wait_ge(sq1_ready, 1)
                act.activation(t2[:], t1[:], ACT.Sqrt).then_inc(root1_ready, 1)
                act.wait_ge(consts, 5)

                def copy_turned(dst, base):
                    for half in range(2):
                        act.wait_ge(turned, base + half + 1)
                        act.activation(dst[:, :, 2 * half * P:2 * (half + 1) * P],
                                       psT[:].rearrange("p (h n) -> p h n", h=DH), ACT.Copy).then_inc(turn_copied, 1)

                def step(n):
                    if runs(n):
                        wait_count(act, mixed_ready, n)
                        for m in range(TILES_P):
                            act.wait_ge(filled, psr_base(n) + m + 1)
                            dst = (q, k, v, a, g)[m // DH][:, m % DH, :]
                            src = psR[:, m % 2, :]
                            part = "qkvag"[m // DH]
                            if part in "qv":
                                ins = act.activation(dst, src, ACT.Copy)
                            elif part == "k":
                                ins = act.activation(dst, src, ACT.Tanh)
                            elif part == "a":
                                ins = act.activation(dst, src, ACT.Sigmoid, bias=two_bias[:])
                            else:
                                ins = act.activation(dst, src, ACT.Sigmoid)
                            ins.then_inc(emptied, 1)
                    if runs(n - 1):
                        copy_turned(h2T, turns_h2(n))
                        wait_count(act, mlp_done, n - 1)
                        for m in range(MF):
                            act.wait_ge(filled, fc_base(n) + m + 1)
                            act.activation(hid[:, m, :], psR[:, m % 2, :], ACT.Silu).then_inc(emptied, 1)
                    if runs(n):
                        for hh in range(DH):
                            act.wait_ge(filled, rms_base(n) + hh + 1)
                            act.activation(rq[:, hh, :], psR[:, hh % 2, :], ACT.Sqrt, bias=q_eps[:]).then_inc(emptied, 1)
                    if runs(n + 1):
                        copy_turned(h1T, turns_h1(n))
                    if runs(n):
                        act.wait_ge(x1_ready, n + 1)
                        for t in range(GT):
                            if t:
                                act.drain()
                            ins = act.activation(sq[:], x1[:, t, :], ACT.Square, accum_out=ms[:, t:t + 1])
                        act.drain()
                        act.activation(root2[:], ms[:], ACT.Sqrt, bias=r_eps[:], scale=1.0 / D).then_inc(root2_ready, 1)
                run(act, step)

            @block.vector
            def _(dve):
                dve.tensor_scalar(t1[:], var_eps[:], -LN_EPS, None, ALU.add)
                dve.tensor_tensor(t2[:], rstd[:], rstd[:], ALU.mult)
                dve.drain()
                dve.tensor_tensor(t3[:], t1[:], t2[:], ALU.mult)
                dve.drain()
                dve.tensor_scalar(t1[:], t3[:], 1e-6, None, ALU.add).then_inc(sq1_ready, 1)
                dve.wait_ge(root1_ready, 1)
                dve.reciprocal(scale1[:], t2[:])
                dve.drain()
                newton(dve, scale1[:], t1[:], t3[:])
                dve.tensor_tensor(scale1[:], scale1[:], rstd[:], ALU.mult)
                dve.wait_ge(w_in, 96)
                for hh in range(DH):
                    dve.tensor_scalar(wi[:, hh, :], wi[:, hh, :], n1[:, hh:hh + 1], None, ALU.mult)
                    dve.tensor_scalar(wf[:, hh, :], wf[:, hh, :], n2[:, hh:hh + 1], None, ALU.mult)
                dve.drain()
                dve.memset(t3[:, 0:1], 0.0).then_inc(weights_ready, 1)
                dve.wait_ge(consts, 5)
                ends = lambda ap: ap.rearrange("p h (n c) -> p h n c", c=CH)[:, :, :, CH - 1]
                starts = lambda ap: ap.rearrange("p h (n c) -> p h n c", c=CH)[:, :, :, 0]

                def normalise(n):
                    wait_count(dve, turned, turns_h1(n - 2) + 2 if not static(n) or n > 0 else 0)
                    for b in range(GT):
                        t = GT * n + b
                        ins = dve.tensor_scalar(y[:, b, :], tile_of(x, t), mean[:, one(t)], scale1[:, one(t)],
                                                ALU.subtract, ALU.mult)
                    ins.then_inc(y_ready, 1)

                def second_norm(n):
                    dve.wait_ge(root2_ready, n + 1)
                    dve.reciprocal(r2[:], root2[:])
                    dve.tensor_scalar(r2t[:], ms[:], 1.0 / D, 1e-6, ALU.mult, ALU.add)
                    dve.drain()
                    newton(dve, r2[:], r2t[:], root2[:])
                    for b in range(GT):
                        ins = dve.tensor_scalar(h2[:, b, :], x1[:, b, :], r2[:, b:b + 1], None, ALU.mult)
                    ins.then_inc(h2_ready, 1)

                def recurrence(n):
                    dve.wait_ge(emptied, psr_base(n) + 2)
                    dve.tensor_tensor(qq[:], q[:], q[:], ALU.mult).then_inc(qq_ready, 1)
                    dve.wait_ge(emptied, psr_base(n) + 8)
                    dve.tensor_tensor(k[:], k[:], v[:], ALU.mult)
                    dve.tensor_scalar(a[:], a[:], 0.6, 0.9995, ALU.max, ALU.min)
                    dve.tensor_scalar(state[:, :, 0], state[:, :, NC], goes_on[:, one(n)], None, ALU.mult)
                    dve.drain()
                    dve.tensor_copy(starts(first[:]), starts(a[:]))
                    dve.drain()
                    dve.memset(starts(a[:]), 0.0)
                    dve.drain()
                    for hh in range(DH):
                        dve.tensor_tensor_scan(prefix[:, hh, :], a[:, hh, :], first[:, hh, :], 0.0, ALU.mult, ALU.add)
                    dve.drain()
                    dve.tensor_scalar(ratio[:], prefix[:], 1e-6, None, ALU.max)
                    dve.drain()
                    dve.reciprocal(ratio[:], ratio[:])
                    dve.drain()
                    dve.tensor_tensor(ratio[:], ratio[:], k[:], ALU.mult)
                    dve.drain()
                    for hh in range(DH):
                        dve.tensor_tensor_scan(acc[:, hh, :], inside[:], ratio[:, hh, :], 0.0, ALU.mult, ALU.add)
                    dve.tensor_copy(prefix_end[:], ends(prefix[:]))
                    dve.drain()
                    dve.tensor_tensor(chunk_end[:], prefix_end[:], ends(acc[:]), ALU.mult)
                    dve.drain()
                    for hh in range(DH):
                        dve.tensor_tensor_scan(state[:, hh, 1:NC + 1], prefix_end[:, hh, :], chunk_end[:, hh, :],
                                               state[:, hh, 0:1], ALU.mult, ALU.add)
                    dve.drain()
                    byc = lambda ap: ap.rearrange("p h (n c) -> p (h n) c", c=CH)
                    for hh in range(DH):
                        av = acc[:, hh, :].rearrange("p (n c) -> p n c", c=CH)
                        dve.tensor_tensor(av, av, state[:, hh, 0:NC].unsqueeze(2).broadcast_to([P, NC, CH]), ALU.add)
                    dve.drain()
                    dve.tensor_tensor(acc[:], acc[:], prefix[:], ALU.mult)
                    dve.drain()
                    dve.tensor_tensor(acc[:], acc[:], q[:], ALU.mult)
                    dve.wait_ge(emptied, rms_base(n) + 2)
                    dve.reciprocal(rq[:], rq[:])
                    dve.drain()
                    dve.tensor_tensor(acc[:], acc[:], rq[:], ALU.mult)
                    dve.drain()
                    dve.tensor_tensor(acc[:], acc[:], v[:], ALU.subtract)
                    dve.drain()
                    dve.tensor_tensor(acc[:], acc[:], g[:], ALU.mult)
                    dve.drain()
                    wait_count(dve, attn_done, n)
                    dve.tensor_tensor(mixed[:], acc[:], v[:], ALU.add).then_inc(mixed_ready, 1)

                def finish(n):
                    t = GT * n
                    xs = (x[:, t:t + GT, :] if static(t) else x[:, bass.ds(t, GT), :]).rearrange("p a n -> p (a n)")
                    dve.tensor_tensor(xs, xs, x1[:].rearrange("p a n -> p (a n)"), ALU.add)
                    dve.drain()
                    dve.wait_ge(mlp_done, n + 1)
                    dve.scalar_tensor_tensor(out=xs, in0=psM[:].rearrange("p a n -> p (a n)"), scalar=RES, in1=xs,
                                             op0=ALU.mult, op1=ALU.add).then_inc(mlp_added, 1)

                def first_residual(n):
                    for b in range(GT):
                        t = GT * n + b
                        dve.tensor_scalar(x1[:, b, :], tile_of(x, t), mean[:, one(t)], rstd[:, one(t)],
                                          ALU.subtract, ALU.mult)
                    dve.drain()
                    dve.wait_ge(attn_done, n + 1)
                    x1f = x1[:].rearrange("p a n -> p (a n)")
                    dve.scalar_tensor_tensor(out=x1f, in0=psX[:].rearrange("p a n -> p (a n)"), scalar=RES, in1=x1f,
                                             op0=ALU.mult, op1=ALU.add).then_inc(x1_ready, 1)

                def step(n):
                    if runs(n - 1):
                        second_norm(n - 1)
                    if runs(n + 1):
                        normalise(n + 1)
                    if runs(n):
                        recurrence(n)
                    if runs(n - 1):
                        finish(n - 1)
                    if runs(n):
                        dve.drain()
                        first_residual(n)
                run(dve, step)



def attention(nc, name, x, ident, identb, NT, SEQ, w, qk_dram, max_dram):
    wqk, bqk, wv, bv, woT, bo = w
    NH, HD = 16, 16
    B = NT * P // SEQ
    ST = SEQ // P
    NU = B * NH
    QPART = (0, 0, 0, 1, 2, 1)
    KPART = (0, 1, 2, 0, 0, 1)
    NP = len(QPART)
    ROWS = NP * HD
    MROW = ROWS
    ALLR = ROWS + 3
    SCALE = float(1.0 / np.sqrt(HD))
    KB = SEQ // 512
    VC = 32
    GT = 4
    GB = SEQ // (GT * P)
    with Chip(nc, name) as c:
        vaug = c.sb("vaug", [P, NU, ST, HD + 1])
        att = c.sb("att", [P, NU, ST, HD])
        with Chip(nc, name + "a") as a:
            mean, rstd = a.sb("mean", [P, NT]), a.sb("rstd", [P, NT])
            row_statistics(nc, name, x, NT, mean, rstd)
            wqk_sb = a.sb("wqk", [P, DH, 2 * D])
            bqk_sb = a.sb("bqk", [P, 2 * DH])
            wv_sb = a.sb("wv", [P, DH, D])
            bv_sb = a.sb("bv", [1, D])
            ones = a.sb("ones", [1, P])
            y = a.sb("y", [P, GT, D])
            yT = a.sb("yT", [P, 2, DH, GT * P])
            qf = a.sb("qf", [P, 2 * DH, 512])
            rest = a.sb("rest", [P, 2, 512])
            parts = a.sb("parts", [P, 2 * DH, 3, 512], BF16)
            psT, psR, psV = a.ps("psT", [P, 512]), a.ps("psR", [P, 2 * DH, 512]), a.ps("psV", [P, 2, 512])
            w_in, consts, y_ready, turned, turn_copied, qk_done, qk_copied, split_ready, v_done, v_copied = (
                a.sem(n) for n in ("w_in", "consts", "y_ready", "turned", "turn_copied", "qk_done", "qk_copied",
                                   "split_ready", "v_done", "v_copied"))
            stored = [a.sem(f"stored{m}") for m in range(2 * DH)]
            with nc.Block() as block:
                @block.gpsimd
                def _(pool):
                    pool.memset(ones[:], 1.0).then_inc(consts, 1)
                    pool.memset(vaug[:, :, :, HD:HD + 1], 1.0)

                @block.sync
                def _(sp):
                    sp.dma_start(wqk_sb[:], wqk).then_inc(w_in, 16)
                    sp.dma_start(bqk_sb[:], bqk).then_inc(w_in, 16)
                    sp.dma_start(wv_sb[:], wv).then_inc(w_in, 16)
                    sp.dma_start(bv_sb[:], bv).then_inc(w_in, 16)
                    with sp.Fori(0, B) as b:
                        for k in range(GB):
                            for m in range(2 * DH):
                                sp.wait_ge(split_ready, 2 * DH * (GB * b + k) + m + 1)
                                for part in range(3):
                                    sp.dma_start(qk_dram[m // DH, part, bass.ds(b * D + (m % DH) * P, P),
                                                         k * 512:(k + 1) * 512],
                                                 parts[:, m, part, :]).then_inc(stored[m], 16)
                    for m in range(2 * DH):
                        sp.wait_ge(stored[m], 16 * 3 * GB * B)

                @block.vector
                def _(dve):
                    with dve.Fori(0, B) as b:
                        for k in range(GB):
                            g = GB * b + k
                            for kk in ([0, 1] if k == 0 else [k + 1] if k + 1 < GB else []):
                                dve.wait_ge(turned, 2 * (GB * b + kk))
                                for q in range(GT):
                                    ins = dve.tensor_scalar(y[:, q, :], tile_of(x, (GB * b + kk) * GT + q),
                                                            mean[:, one((GB * b + kk) * GT + q)],
                                                            rstd[:, one((GB * b + kk) * GT + q)], ALU.subtract, ALU.mult)
                                ins.then_inc(y_ready, 1)
                            for m in range(0, 2 * DH, 2):
                                pair = slice(m, m + 2)
                                dve.wait_ge(qk_copied, 2 * DH * g + m + 2)
                                dve.tensor_tensor(rest[:], qf[:, pair, :], parts[:, pair, 0, :], ALU.subtract)
                                dve.drain()
                                dve.tensor_copy(parts[:, pair, 1, :], rest[:])
                                dve.drain()
                                dve.tensor_tensor(parts[:, pair, 2, :], rest[:], parts[:, pair, 1, :], ALU.subtract
                                                  ).then_inc(split_ready, 2)
                                dve.drain()

                @block.tensor
                def _(pe):
                    pe.wait_ge(w_in, 64)
                    pe.wait_ge(consts, 1)

                    def turn(g):
                        pe.wait_ge(y_ready, g + 1)
                        for half in range(2):
                            pe.wait_ge(turn_copied, 2 * g + half)
                            for hh in range(DH):
                                for q in range(2):
                                    mm = pe.transpose(psT[:, (2 * hh + q) * P:(2 * hh + q + 1) * P],
                                                      y[:, 2 * half + q, hh * P:(hh + 1) * P], ident[:])
                            mm.then_inc(turned, 1)

                    with pe.Fori(0, B) as b:
                        turn(GB * b)
                        for k in range(GB):
                            g = GB * b + k
                            pe.wait_ge(turn_copied, 2 * g + 2)
                            pe.wait_ge(qk_copied, 2 * DH * g)
                            for m in range(2 * DH):
                                for hh in range(DH):
                                    mm = pe.matmul(psR[:, m, :], wqk_sb[:, hh, m * P:(m + 1) * P], yT[:, k % 2, hh, :],
                                                   start=(hh == 0), stop=(hh == DH - 1))
                                mm.then_inc(qk_done, 1)
                            if k + 1 < GB:
                                turn(g + 1)
                            pe.wait_ge(v_copied, g)
                            for q in range(GT):
                                out = psV[:, q // 2, (q % 2) * D:(q % 2 + 1) * D]
                                for hh in range(DH):
                                    pe.matmul(out, yT[:, k % 2, hh, q * P:(q + 1) * P], wv_sb[:, hh, :],
                                              start=(hh == 0), stop=False)
                                mm = pe.matmul(out, ones[:], bv_sb[:], start=False, stop=True)
                            mm.then_inc(v_done, 1)

                @block.scalar
                def _(act):
                    def copy_turned(g, k):
                        for half in range(2):
                            act.wait_ge(turned, 2 * g + half + 1)
                            act.activation(yT[:, k % 2, :, 2 * half * P:2 * (half + 1) * P],
                                           psT[:].rearrange("p (h n) -> p h n", h=DH), ACT.Copy).then_inc(turn_copied, 1)

                    act.wait_ge(w_in, 64)
                    with act.Fori(0, B) as b:
                        copy_turned(GB * b, 0)
                        for k in range(GB):
                            g = GB * b + k
                            for m in range(2 * DH):
                                act.wait_ge(stored[m], 48 * g)
                                act.wait_ge(qk_done, 2 * DH * g + m + 1)
                                act.activation(qf[:, m, :], psR[:, m, :], ACT.Identity, bias=bqk_sb[:, m:m + 1])
                                act.activation(parts[:, m, 0, :], psR[:, m, :], ACT.Identity,
                                               bias=bqk_sb[:, m:m + 1]).then_inc(qk_copied, 1)
                            if k + 1 < GB:
                                copy_turned(g + 1, k + 1)
                            act.wait_ge(v_done, g + 1)
                            act.activation(vaug[:, bass.ds(NH * b, NH), GT * k:GT * (k + 1), 0:HD].rearrange("p n t e -> p t n e"),
                                           psV[:].rearrange("p a (t n e) -> p (a t) n e", n=NH, e=HD), ACT.Copy
                                           ).then_inc(v_copied, 1)

        RQ = 4
        RP = 4
        with Chip(nc, name + "b") as u_:
            qa = u_.sb("qa", [P, RQ, SEQ], BF16)
            ka = u_.sb("ka", [P, RQ, SEQ], BF16)
            vh = u_.sb("vh", [P, RQ, ST, VC])
            pt = u_.sb("pt", [P, RP, KB, 512])
            mx = u_.sb("mx", [P, ST, KB // 2])
            m = u_.sb("m", [P, ST])
            mr = u_.sb("mr", [P, ST])
            mcat = u_.sb("mcat", [P, P], BF16)
            mT = u_.sb("mT", [3 * ST, P], BF16)
            oS = u_.sb("oS", [P, 512])
            inv = u_.sb("inv", [P, KB, ST // KB])
            psA = u_.ps("psA", [P, 2, 1024])
            psE = u_.ps("psE", [P, 3, 512])
            psO = u_.ps("psO", [P, 512])
            rows_in = [u_.sem(f"rows_in{r}") for r in range(RQ)]
            (consts, scores_done, slot_read, m_ready, m_turned, m_stored, m_in, keys_done, exp_ready, pv_done,
             vh_ready, o_ready, o_copied, o_turned) = (
                u_.sem(n) for n in ("consts", "scores_done", "slot_read", "m_ready", "m_turned", "m_stored",
                                    "m_in", "keys_done", "exp_ready", "pv_done", "vh_ready", "o_ready", "o_copied",
                                    "o_turned"))
            LAG = 2
            HC = KB // 2

            T_MAX, T_OUT = 1, 5

            def run(eng, step):
                for n in range(-2, RQ):
                    step(n, n // RQ, n % RQ)
                with eng.Fori(1, NU // RQ - 1) as i:
                    for r in range(RQ):
                        step(RQ * i + r, i, r)
                for n in range(NU - RQ, NU + 1):
                    step(n, n // RQ, n % RQ)

            def runs(n):
                return not static(n) or 0 <= n < NU

            PER_STEP = HC * ST + 2

            def uses_before(n):
                if not static(n):
                    return PER_STEP * n + uses_before(RQ) - PER_STEP * RQ
                return sum(HC * ST * runs(e + 2) + runs(e + 1) + runs(e - 1) for e in range(-2, n))

            def use(n, t, k):
                inside = k + HC * t * runs(n + 2) + (runs(n + 1) if t > T_MAX else 0) + (runs(n - 1) if t > T_OUT else 0)
                slot = (uses_before(n if static(n) else RQ) + inside) % 2
                return uses_before(n) + inside, slot

            def turn_use(n, t):
                return use(n, t, HC if runs(n + 2) else 0)

            def exp_slot(t, kb):
                return 1 if KB * t + kb == KB * ST - 1 else (KB * t + kb) % 3

            def exp_before(t, kb):
                j = KB * t + kb
                return {0: -3, 1: 0, 2: -1, KB * ST - 1: j - 1}.get(j, j - 2)

            assert KB * ST % 3 == 1

            with nc.Block() as block:
                @block.gpsimd
                def _(pool):
                    pool.memset(vh[:], 0.0).then_inc(consts, 1)
                    pool.wait_ge(consts, 1)
                    pool.memset(ka[MROW:ALLR, :, :], 1.0).then_inc(consts, 1)
                    pool.wait_ge(consts, 2)
                    pool.memset(mcat[:], 0.0).then_inc(consts, 1)
                    pool.wait_ge(consts, 3)

                    def step(n, i, r):
                        if runs(n + 1):
                            wait_count(pool, o_ready, n - 2)
                            src = vaug[:, n + 1, :, :] if static(n) else \
                                vaug[:, bass.ds(n + 1, 1), :, :].rearrange("p a t e -> p (a t) e")
                            pool.tensor_copy(vh[:, (r + 1) % RQ, :, 0:HD + 1], src).then_inc(vh_ready, 1)
                    run(pool, step)

                @block.sync
                def _(sp):
                    def step(n, i, r):
                        v = n + 3
                        rv = (r + 3) % RQ
                        for v, rv in ([(n + 2, (r + 2) % RQ), (v, rv)] if static(n) and n == -2 else [(v, rv)]):
                            if runs(v):
                                wait_count(sp, keys_done, KB * ST * (v - RQ + 1))
                                for which, dst, pick in ((0, qa, QPART), (1, ka, KPART)):
                                    for j, part in enumerate(pick):
                                        rows = slice(HD * v, HD * (v + 1)) if static(v) else bass.ds(HD * v, HD)
                                        sp.dma_start(dst[HD * j:HD * (j + 1), rv, :], qk_dram[which, part, rows, :]
                                                     ).then_inc(rows_in[rv], 16)
                        if runs(n + 1):
                            sp.wait_ge(slot_read, turn_use(n, T_MAX)[0] + 1)
                            wait_count(sp, m_in, 16 * (n + 1))
                            sp.dma_start(max_dram, mT[:]).then_inc(m_stored, 16)
                            sp.wait_ge(m_stored, 16 * (n + 2))
                            sp.dma_start(qa[MROW:ALLR, (r + 1) % RQ, :],
                                         max_dram.rearrange("(a t) s -> a (t s)", a=3)).then_inc(m_in, 16)
                    run(sp, step)

                @block.tensor
                def _(pe):
                    pe.wait_ge(consts, 3)

                    def by_query(n, st, r, i, hc):
                        if st == 0 and hc == 0:
                            pe.wait_ge(rows_in[r], 16 * 2 * NP * (i + 1))
                        before, slot = use(n, st, hc)
                        wait_count(pe, slot_read, before - 1)
                        for q in range(2):
                            kb = 2 * hc + q
                            mm = pe.matmul(psA[:, slot, q * 512:(q + 1) * 512],
                                           qa[0:ROWS, r, st * P:(st + 1) * P],
                                           ka[0:ROWS, r, kb * 512:(kb + 1) * 512], start=True, stop=True)
                        mm.then_inc(scores_done, 1)

                    def by_key(n, tt, r, kb):
                        if tt == 0 and kb == 0:
                            pe.wait_ge(m_in, 16 * (n + 1))
                        wait_count(pe, exp_ready, KB * ST * n + exp_before(tt, kb))
                        pe.matmul(psE[:, exp_slot(tt, kb), :], ka[0:ALLR, r, tt * P:(tt + 1) * P],
                                  qa[0:ALLR, r, kb * 512:(kb + 1) * 512], start=True, stop=True
                                  ).then_inc(keys_done, 1)

                    def values(n, tt, r):
                        if tt == 0:
                            pe.wait_ge(vh_ready, n + 1)
                            wait_count(pe, o_copied, n)
                        pe.wait_ge(exp_ready, KB * (ST * n + tt) + KB)
                        for kb in range(KB):
                            mm = pe.matmul(psO[VC * kb:VC * (kb + 1), :], vh[:, r, tt, :], pt[:, tt % RP, kb, :],
                                           start=(tt == 0), stop=(tt == ST - 1), tile_position=(0, VC * kb))
                        mm.then_inc(pv_done if tt < ST - 1 else o_ready, 1)

                    def turn_max(n):
                        pe.wait_ge(m_ready, n + 2)
                        before, slot = turn_use(n, T_MAX)
                        wait_count(pe, slot_read, before - 1)
                        pe.transpose(psA[:, slot, 0:P // 2].bitcast(BF16), mcat[:], identb[:]).then_inc(m_turned, 1)

                    def turn_out(n):
                        pe.wait_ge(o_copied, n)
                        before, slot = turn_use(n, T_OUT)
                        wait_count(pe, slot_read, before - 1)
                        for q in range(512 // P):
                            mm = pe.transpose(psA[:, slot, q * P:(q + 1) * P], oS[:, q * P:(q + 1) * P], ident[:])
                        mm.then_inc(o_turned, 1)

                    def step(n, i, r):
                        def keys(t, blocks):
                            if runs(n):
                                for kb in blocks:
                                    by_key(n, t, r, kb)

                        def queries(t, hc):
                            if runs(n + 2):
                                by_query(n, t, (r + 2) % RQ, i + (r + 2) // RQ, hc)

                        for t in range(ST):
                            keys(t, (0, 1))
                            queries(t, 0)
                            keys(t, range(2, KB - 1))
                            if t < LAG and runs(n - 1):
                                values(n - 1, ST - LAG + t, (r - 1) % RQ)
                            if t >= LAG and runs(n):
                                values(n, t - LAG, r)
                            keys(t, (KB - 1,))
                            queries(t, 1)
                            if t == T_MAX and runs(n + 1):
                                turn_max(n)
                            if t == T_OUT and runs(n - 1):
                                turn_out(n)
                    run(pe, step)

                @block.scalar
                def _(act):
                    act.wait_ge(consts, 3)

                    def step(n, i, r):
                        for t in range(ST):
                            if runs(n):
                                if t >= RP:
                                    wait_count(act, pv_done, (ST - 1) * n + t - RP + 1)
                                elif t == RP - 1:
                                    wait_count(act, o_ready, n)
                                else:
                                    wait_count(act, pv_done, (ST - 1) * (n - 1) + ST - RP + t + 1)
                                for kb in range(KB):
                                    act.wait_ge(keys_done, KB * (ST * n + t) + kb + 1)
                                    act.activation(pt[:, t % RP, kb, :], psE[:, exp_slot(t, kb), :], ACT.Exp, scale=SCALE
                                                   ).then_inc(exp_ready, 1)
                            if t == 1 and runs(n - 1):
                                act.wait_ge(o_ready, n)
                                wait_count(act, o_turned, n - 1)
                                act.activation(oS[:], psO[:], ACT.Copy).then_inc(o_copied, 1)
                    run(act, step)

                @block.vector
                def _(dve):
                    dve.wait_ge(consts, 3)
                    part_of = lambda j: mcat[:, j * ST:(j + 1) * ST]

                    def step(n, i, r):
                        for t in range(ST):
                            if runs(n + 2):
                                for hc in range(HC):
                                    dve.wait_ge(scores_done, HC * (ST * (n + 2) + t) + hc + 1)
                                    dve.tensor_reduce(mx[:, t, hc:hc + 1], psA[:, use(n, t, hc)[1], :], AX_X, ALU.max
                                                      ).then_inc(slot_read, 1)
                            if t == T_MAX and runs(n + 1):
                                wait_count(dve, m_stored, 16 * (n + 1))
                                dve.wait_ge(m_turned, n + 2)
                                dve.tensor_copy(mT[:], psA[0:3 * ST, turn_use(n, t)[1], 0:P // 2].bitcast(BF16)
                                                ).then_inc(slot_read, 1)
                            if t == T_OUT and runs(n - 1):
                                dve.drain()
                                dve.wait_ge(o_turned, n)
                                ov = psA[:, turn_use(n, t)[1], 0:512].rearrange(
                                    "p (q j e) -> p j q e", j=KB, e=VC)
                                dve.reciprocal(inv[:], ov[:, :, :, HD])
                                dve.drain()
                                dst = (att[:, n - 1, :, :] if static(n) else
                                       att[:, bass.ds(n - 1, 1), :, :].rearrange("p a t e -> p (a t) e"))
                                dve.tensor_tensor(dst.rearrange("p (j q) e -> p j q e", j=KB), ov[:, :, :, 0:HD],
                                                  inv[:].unsqueeze(3).broadcast_to([P, KB, ST // KB, HD]), ALU.mult
                                                  ).then_inc(slot_read, 1)
                        if runs(n + 2):
                            dve.drain()
                            dve.tensor_reduce(m[:], mx[:], AX_X, ALU.max)
                            dve.drain()
                            wait_count(dve, m_turned, n + 2)
                            dve.tensor_scalar(part_of(0), m[:], -1.0, None, ALU.mult)
                            dve.drain()
                            dve.scalar_tensor_tensor(out=mr[:], in0=m[:], scalar=-1.0, in1=part_of(0),
                                                     op0=ALU.mult, op1=ALU.subtract)
                            dve.drain()
                            dve.tensor_copy(part_of(1), mr[:])
                            dve.drain()
                            dve.tensor_tensor(part_of(2), mr[:], part_of(1), ALU.subtract).then_inc(m_ready, 1)
                    run(dve, step)

        with Chip(nc, name + "c") as o:
            wo_sb = o.sb("wo", [P, DH, D])
            bo_sb = o.sb("bo", [1, D])
            ones = o.sb("ones", [1, P])
            ag = o.sb("ag", [P, 2, D])
            aT = o.sb("aT", [P, 2, DH, P])
            psT, psY = o.ps("psT", [P, 2, 512]), o.ps("psY", [P, 2, 512])
            w_in, consts, gathered, turned, turn_copied, projected, added = (
                o.sem(n) for n in ("w_in", "consts", "gathered", "turned", "turn_copied", "projected", "added"))
            with nc.Block() as block:
                @block.gpsimd
                def _(pool):
                    pool.memset(ones[:], 1.0).then_inc(consts, 1)

                @block.sync
                def _(sp):
                    sp.dma_start(wo_sb[:], woT).then_inc(w_in, 16)
                    sp.dma_start(bo_sb[:], bo).then_inc(w_in, 16)

                def run(eng, step):
                    for b in range(B):
                        if b == 0:
                            step(0, 0, 0, 0)
                            step(1, 1, 0, 1)
                        with eng.Fori(1 if b == 0 else 0, ST // 2) as i:
                            for k in range(2):
                                step(b * ST + 2 * i + k, k, b, 2 * i + k)

                @block.vector
                def _(dve):
                    def gather(t, k, b, st):
                        src = att[:, b * NH:(b + 1) * NH, one(st), :].rearrange("p n t e -> p n (t e)")
                        wait_count(dve, turned, t - 1)
                        dve.tensor_copy(ag[:, k, :].rearrange("p (n e) -> p n e", n=NH), src).then_inc(gathered, 1)

                    def add(t, k, b, st):
                        dve.wait_ge(projected, t + 1)
                        xt = tile_of(x, t)
                        dve.tensor_tensor(xt, psY[:, k, 0:D], xt, ALU.add).then_inc(added, 1)

                    def both(t, k, b, st):
                        gather(t, k, b, st)
                        if not static(t) or t > 1:
                            add(t - 2, k, b, st)
                    run(dve, both)
                    add(NT - 2, 0, 0, 0)
                    add(NT - 1, 1, 0, 0)

                @block.tensor
                def _(pe):
                    pe.wait_ge(w_in, 32)
                    pe.wait_ge(consts, 1)

                    def turn(t, k, b, st):
                        pe.wait_ge(gathered, t + 1)
                        wait_count(pe, turn_copied, t - 1)
                        for hh in range(DH):
                            mm = pe.transpose(psT[:, k, hh * P:(hh + 1) * P], ag[:, k, hh * P:(hh + 1) * P], ident[:])
                        mm.then_inc(turned, 1)

                    def project(t, k, b, st):
                        pe.wait_ge(turn_copied, t + 1)
                        wait_count(pe, added, t - 1)
                        for hh in range(DH):
                            pe.matmul(psY[:, k, 0:D], aT[:, k, hh, :], wo_sb[:, hh, :], start=(hh == 0), stop=False)
                        pe.matmul(psY[:, k, 0:D], ones[:], bo_sb[:], start=False, stop=True).then_inc(projected, 1)

                    def step(t, k, b, st):
                        turn(t, k, b, st)
                        if not static(t) or t > 0:
                            project(t - 1, 1 - k, b, st)
                    run(pe, step)
                    project(NT - 1, 1, 0, 0)

                @block.scalar
                def _(act):
                    def step(t, k, b, st):
                        act.wait_ge(turned, t + 1)
                        wait_count(act, projected, t - 1)
                        act.activation(aT[:, k, :, :].rearrange("p h n -> p (h n)"), psT[:, k, 0:D], ACT.Copy
                                       ).then_inc(turn_copied, 1)
                    run(act, step)


def dram_tile(d, t):
    return d[t, :, :] if static(t) else d[bass.ds(t, 1), :, :].rearrange("a p n -> (a p) n")


def keys_layout(keys):
    h, nk, p, kd = keys.shape
    return np.ascontiguousarray(keys.transpose(3, 2, 0, 1).reshape(kd, p * h, nk))


def halves_layout(v):
    return np.ascontiguousarray(v.reshape(-1, P).T)


def key_in_layout(key_in):
    ne, d = key_in.shape
    return np.ascontiguousarray(key_in.reshape(P, ne // P, d // P, P).transpose(3, 2, 1, 0).reshape(P, d // P, ne))


def rows_layout(w):
    return np.ascontiguousarray(w.reshape(-1, P, w.shape[1]).transpose(1, 0, 2))


def head_cols(w):
    return w.transpose(1, 0, 2).reshape(w.shape[1], -1)


SEQ = 2048


def build(nc, a, out, qk_dram, max_dram, yT_dram):
    tokens = out.rearrange("b s d -> (b s) d").rearrange("(t p) d -> p t d", p=P)
    x_in = a["x"].rearrange("b s d -> (b s) d").rearrange("(t p) d -> p t d", p=P)
    NT = tokens.shape[1]
    peer = tuple(a[n] for n in ("gamma", "beta", "w_q", "keysT", "key_inT", "key_out"))
    mix = tuple(a[n] for n in ("norm1", "norm2", "in_projT", "out_projT", "fcT", "projT"))
    moe = tuple(a[n] for n in ("gate_W", "gate_b", "expert_W", "expert_b"))
    att = tuple(a[n] for n in ("wqk", "bqk", "wv", "bv", "woT", "bo"))
    with Chip(nc, "all") as c:
        x = c.sb("x", [P, NT, D])
        ident, ident16, identb = c.sb("ident", [P, P]), c.sb("ident16", [P, P], F16), c.sb("identb", [P, P], BF16)
        x_loaded, x_stored = c.sem("x_loaded"), c.sem("x_stored")
        make_identities(nc, ident, ident16, identb)
        with nc.Block() as block:
            @block.sync
            def _(sp):
                sp.dma_start(x[:], x_in).then_inc(x_loaded, 16)
                sp.wait_ge(x_loaded, 16)
        peer_ffn(nc, "peer0", x, ident, ident16, NT, peer, yT_dram)
        recurrent_block(nc, "mix", x, ident, NT, SEQ, mix)
        peer_ffn(nc, "peer1", x, ident, ident16, NT, peer, yT_dram)
        moe_ffn(nc, "moe0", x, ident, NT, moe)
        attention(nc, "att", x, ident, identb, NT, SEQ, att, qk_dram, max_dram)
        moe_ffn(nc, "moe1", x, ident, NT, moe)
        with nc.Block() as block:
            @block.sync
            def _(sp):
                sp.dma_start(tokens, x[:]).then_inc(x_stored, 16)
                sp.wait_ge(x_stored, 16)


def kernel(L0_attn_x, L0_attn_norm1_w, L0_attn_norm2_w, L0_attn_in_proj_w, L0_attn_out_proj_w, L0_attn_fc_w,
           L0_attn_proj_w, L0_ffn_gamma, L0_ffn_beta, L0_ffn_w_q, L0_ffn_keys, L0_ffn_key_in, L0_ffn_key_out,
           L1_attn_wq, L1_attn_bq, L1_attn_wk, L1_attn_bk, L1_attn_wv, L1_attn_bv, L1_attn_wo, L1_attn_bo,
           L1_ffn_gate_W, L1_ffn_gate_b, L1_ffn_expert_W, L1_ffn_expert_b):
    import concourse.bacc as bacc
    from concourse.bass_utils import run_bass_kernel_spmd as run

    arrays = {
        "x": L0_attn_x,
        "gamma": halves_layout(L0_ffn_gamma), "beta": halves_layout(L0_ffn_beta), "w_q": L0_ffn_w_q,
        "keysT": keys_layout(L0_ffn_keys), "key_inT": key_in_layout(L0_ffn_key_in), "key_out": L0_ffn_key_out,
        "norm1": halves_layout(L0_attn_norm1_w), "norm2": halves_layout(L0_attn_norm2_w),
        "in_projT": rows_layout(L0_attn_in_proj_w.T), "out_projT": rows_layout(L0_attn_out_proj_w.T),
        "fcT": rows_layout(L0_attn_fc_w.T), "projT": rows_layout(L0_attn_proj_w.T),
        "gate_W": L1_ffn_gate_W, "gate_b": L1_ffn_gate_b, "expert_W": L1_ffn_expert_W, "expert_b": L1_ffn_expert_b,
        "wqk": rows_layout(np.concatenate([head_cols(L1_attn_wq), head_cols(L1_attn_wk)], axis=1)),
        "bqk": halves_layout(np.concatenate([L1_attn_bq.reshape(-1), L1_attn_bk.reshape(-1)])),
        "wv": rows_layout(head_cols(L1_attn_wv)), "bv": L1_attn_bv.reshape(1, -1),
        "woT": rows_layout(L1_attn_wo.T), "bo": L1_attn_bo.reshape(1, -1),
    }
    arrays = {n: np.ascontiguousarray(v) for n, v in arrays.items()}
    nc = bacc.Bacc("TRN2", target_bir_lowering=False, num_devices=1)
    aps = {n: nc.dram_tensor(f"in_{n}", v.shape, mybir.dt.from_np(v.dtype), kind="ExternalInput").ap()
           for n, v in arrays.items()}
    shape = L0_attn_x.shape
    out = nc.dram_tensor("out", shape, F32, kind="ExternalOutput").ap()
    tokens = shape[0] * shape[1]
    qk_dram = nc.dram_tensor("qk_scratch", (2, 3, tokens // SEQ * D, SEQ), BF16, kind="Internal").ap()
    max_dram = nc.dram_tensor("max_scratch", (3 * SEQ // P, P), BF16, kind="Internal").ap()
    yT_dram = nc.dram_tensor("yT_scratch", (tokens // P, P, D), F32, kind="Internal").ap()
    build(nc, aps, out, qk_dram, max_dram, yT_dram)
    r = run(nc, [{f"in_{n}": v for n, v in arrays.items()}], core_ids=[0])
    return r.results[0]["out"]
```

```python
from contextlib import ExitStack

import numpy as np

import concourse.bass as bass
from concourse import mybir

F32 = mybir.dt.float32
F16 = mybir.dt.float16
BF16 = mybir.dt.bfloat16
U32 = mybir.dt.uint32
ALU = mybir.AluOpType
ACT = mybir.ActivationFunctionType
AX_X = mybir.AxisListType.X

P = 128
D = 256
DH = D // P
LN_EPS = 1e-5


def static(v):
    return isinstance(v, int)


def wait_count(eng, sem, count):
    if static(count) and count <= 0:
        return
    eng.wait_ge(sem, count)


def one(i):
    return slice(i, i + 1) if static(i) else bass.ds(i, 1)


def tile_of(buf, i):
    if static(i):
        return buf[:, i, :]
    return buf[:, bass.ds(i, 1), :].rearrange("p a n -> p (a n)")


class Chip:

    def __init__(self, nc, name):
        self.nc, self.name, self.stack, self.sems = nc, name, ExitStack(), []

    def __enter__(self):
        self.stack.__enter__()
        return self

    def __exit__(self, *error):
        if error[0] is None and self.sems:
            self.nc.clear_and_free_semaphores(self.sems)
            self.nc.all_engine_barrier()
        return self.stack.__exit__(*error)

    def sb(self, name, shape, dt=F32):
        return self.stack.enter_context(self.nc.sbuf_tensor(f"{self.name}_{name}", shape, dt))

    def ps(self, name, shape, dt=F32):
        return self.stack.enter_context(self.nc.psum_tensor(f"{self.name}_{name}", shape, dt))

    def sem(self, name):
        self.sems.append(self.nc.alloc_semaphore(name=f"{self.name}_{name}"))
        return self.sems[-1]


def make_identities(nc, *idents):
    with Chip(nc, "ident") as c:
        zeroed = c.sem("zeroed")
        with nc.Block() as block:
            @block.gpsimd
            def _(pool):
                for m in idents:
                    pool.memset(m[:], 0.0).then_inc(zeroed, 1)
                pool.wait_ge(zeroed, len(idents))
                for m in idents:
                    pool.affine_select(out=m[:], in_=m[:], compare_op=ALU.not_equal, fill=1.0,
                                       base=0, pattern=[[-1, P]], channel_multiplier=1)


def row_statistics(nc, name, x, NT, mean, rstd, loads, var_eps=None, x_in=None):
    Q = NT // 4
    with Chip(nc, name + "_st") as c:
        st = c.sb("st", [P, NT, 6])
        w = [c.sb(f"w{i}", [P, NT]) for i in range(4)]
        var_ready, root_ready = c.sem("var_ready"), c.sem("root_ready")
        x_loaded = [c.sem(f"x_loaded{q}") for q in range(4 if x_in is not None else 0)]
        with nc.Block() as block:
            @block.sync
            def _(sp):
                if x_in is not None:
                    for q in range(4):
                        sp.dma_start(x[:, q * Q:(q + 1) * Q, :], x_in[:, q * Q:(q + 1) * Q, :]).then_inc(x_loaded[q], 16)
                loads(sp)

            @block.vector
            def _(dve):
                if x_in is not None:
                    for t in range(NT):
                        if t % Q == 0:
                            dve.wait_ge(x_loaded[t // Q], 16)
                        dve.bn_stats(st[:, t, :], x[:, t, :])
                else:
                    with dve.Fori(0, NT // 4) as i:
                        for k in range(4):
                            dve.bn_stats(tile_of(st, 4 * i + k), tile_of(x, 4 * i + k))
                dve.drain()
                m0, v0, m1, v1 = (st[:, :, k] for k in (1, 2, 4, 5))
                dve.tensor_tensor(w[0][:], m0, m1, ALU.add)
                dve.tensor_tensor(w[1][:], m0, m1, ALU.subtract)
                dve.tensor_tensor(w[2][:], v0, v1, ALU.add)
                dve.drain()
                dve.tensor_scalar(mean[:], w[0][:], 0.5, None, ALU.mult)
                dve.tensor_tensor(w[3][:], w[1][:], w[1][:], ALU.mult)
                dve.tensor_scalar(w[2][:], w[2][:], 1.0 / D, LN_EPS, ALU.mult, ALU.add)
                dve.drain()
                dve.scalar_tensor_tensor(out=w[1][:], in0=w[3][:], scalar=0.25, in1=w[2][:],
                                         op0=ALU.mult, op1=ALU.add).then_inc(var_ready, 1)
                dve.wait_ge(root_ready, 1)
                dve.reciprocal(rstd[:], w[0][:])
                if var_eps is not None:
                    dve.tensor_copy(var_eps[:], w[1][:])
                dve.drain()
                newton(dve, rstd[:], w[1][:], w[2][:])

            @block.scalar
            def _(act):
                act.wait_ge(var_ready, 1)
                act.activation(w[0][:], w[1][:], ACT.Sqrt).then_inc(root_ready, 1)


def newton(dve, r, v, tmp):
    dve.tensor_tensor(tmp, r, r, ALU.mult)
    dve.drain()
    dve.tensor_tensor(tmp, tmp, v, ALU.mult)
    dve.drain()
    dve.tensor_scalar(tmp, tmp, -0.5, 1.5, ALU.mult, ALU.add)
    dve.drain()
    dve.tensor_tensor(r, r, tmp, ALU.mult)
    dve.drain()



def peer_ffn(nc, name, x, ident, ident16, NT, w, yT_dram, x_in=None):
    gamma, beta, w_q, keysT, key_inT, key_out = w
    H, K, NK, KD = 8, 8, 64, 128
    NE = NK * NK
    NJ = NE // P
    JG = 4
    NG = NJ // JG
    HK = H * K
    S = 2 * H * NK
    HM = P // 4
    MQ = P // 2 // NG
    WS = 4096.0
    KS = 64.0
    PS = 16.0
    RING = 4
    LAG = 3
    with Chip(nc, name) as c:
        keyin = c.sb("keyin", [P, 2, DH * NE], F16)
        keyout = c.sb("keyout", [P, 2, NJ * D], F16)
        wc = c.sb("wc", [P, DH, S])
        xscale, xbias = c.sb("xscale", [P, DH]), c.sb("xbias", [P, DH])

        with Chip(nc, name + "a") as a:
            mean, rstd = a.sb("mean", [P, NT]), a.sb("rstd", [P, NT])
            wq = a.sb("wq", [P, 2 * H, D])
            kT = a.sb("kT", [P, 2 * H, NK])
            gb = a.sb("gb", [P, 2, DH])
            y = a.sb("y", [P, 2, 2, D])
            yT = a.sb("yT", [P, 2, DH, 2, P])
            bst = a.sb("bst", [P, DH, NT // 2, 6])
            mv = a.sb("mv", [P, DH, 2])
            rt, rv, rtmp = a.sb("rt", [P, DH]), a.sb("rv", [P, DH]), a.sb("rtmp", [P, DH])
            raw = a.sb("raw", [P, 2, 2, NJ * D // (NT // 2)])
            psT = a.ps("psT", [P, 2, 512])
            psW = a.ps("psW", [P, 2, 512])
            w_in, gb_in = a.sem("w_in"), a.sem("gb_in")
            keys_in = [a.sem("keys_in0"), a.sem("keys_in1")]
            key_high, key_low = a.sem("key_high"), a.sem("key_low")
            y_ready, yT_ready = a.sem("y_ready"), a.sem("yT_ready")
            transposed, stats_done = a.sem("transposed"), a.sem("stats_done")
            stored = [a.sem("stored0"), a.sem("stored1")]
            var_ready, root_ready = a.sem("bvar_ready"), a.sem("broot_ready")
            folded, fold_copied = a.sem("folded"), a.sem("fold_copied")
            PAIRS = NT // 2
            QUARTER = PAIRS // (2 * DH)
            PIECE = NJ * D // PAIRS
            assert DH * NE == NJ * D and PAIRS % (2 * DH) == 0 and QUARTER % 2 == 0

            def pairs_of(eng, lo, hi, step):
                if lo < hi:
                    with eng.Fori(lo // 2, hi // 2) as j:
                        for k in range(2):
                            step(2 * j + k, k)

            def piece_of(buf, n, i):
                return buf[:, n, i * PIECE:(i + 1) * PIECE] if static(i) else buf[:, n, bass.ds(i * PIECE, PIECE)]

            def load_keys(sp, i, k):
                wait_count(sp, key_low, 2 * (i - 1))
                for which, src in ((0, key_inT.rearrange("p h e -> p (h e)")),
                                   (1, key_out.rearrange("(c j) d -> c (j d)", j=NJ))):
                    cols = slice(i * PIECE, (i + 1) * PIECE) if static(i) else bass.ds(i * PIECE, PIECE)
                    sp.dma_start(raw[:, k, which, :], src[:, cols]).then_inc(keys_in[k], 16)

            def loads(sp):
                load_keys(sp, 0, 0)
                load_keys(sp, 1, 1)
                sp.dma_start(wq[:], w_q.rearrange("(r k) d -> k r d", k=KD)).then_inc(w_in, 16)
                sp.dma_start(kT[:], keysT).then_inc(w_in, 16)
                sp.dma_start(gb[:, 0, :], gamma).then_inc(gb_in, 16)
                sp.dma_start(gb[:, 1, :], beta).then_inc(gb_in, 16)

            row_statistics(nc, name, x, NT, mean, rstd, loads, x_in=x_in)
            with nc.Block() as block:
                @block.sync
                def _(sp):
                    pairs_of(sp, 2, PAIRS, lambda i, k: load_keys(sp, i, k))

                @block.gpsimd
                def _(pool):
                    def store(i, k):
                        pool.wait_ge(yT_ready, i + 1)
                        pool.dma_start(yT_dram[bass.ds(2 * i, 2), :, :].rearrange("a p (h n) -> p h a n", h=DH),
                                       yT[:, k, :, :, :]).then_inc(stored[k], 16)
                    pairs_of(pool, 0, PAIRS, store)
                    for k in range(2):
                        pool.wait_ge(stored[k], 16 * (PAIRS // 2))

                @block.vector
                def _(dve):
                    def y_pair(i, k):
                        wait_count(dve, transposed, i - 1)
                        for a in range(2):
                            t = 2 * i + a
                            ins = dve.tensor_scalar(y[:, k, a, :], tile_of(x, t), mean[:, one(t)], rstd[:, one(t)],
                                                    ALU.subtract, ALU.mult)
                        ins.then_inc(y_ready, 1)

                    def stats_pair(i, k):
                        dve.wait_ge(yT_ready, i + 1)
                        for h in range(DH):
                            st = bst[:, h, i, :] if static(i) else bst[:, h, bass.ds(i, 1), :].rearrange("p a n -> p (a n)")
                            ins = dve.bn_stats(st, yT[:, k, h, :, :].rearrange("p a n -> p (a n)"))
                        ins.then_inc(stats_done, 1)

                    def key_rest(i, k):
                        for which, keys in ((0, keyin), (1, keyout)):
                            dve.wait_ge(key_high, 2 * i + which + 1)
                            dve.scalar_tensor_tensor(out=piece_of(keys, 1, i), in0=raw[:, k, which, :],
                                                     scalar=KS, in1=piece_of(keys, 0, i),
                                                     op0=ALU.mult, op1=ALU.subtract).then_inc(key_low, 1)

                    def step(i, k):
                        stats_pair(i, k)
                        if not static(i) or i + 2 < PAIRS:
                            y_pair(i + 2, k)
                        key_rest(i, k)

                    y_pair(0, 0)
                    y_pair(1, 1)
                    pairs_of(dve, 0, PAIRS - 2, step)
                    step(PAIRS - 2, 0)
                    step(PAIRS - 1, 1)
                    dve.drain()
                    for h in range(DH):
                        dve.bn_aggr(mv[:, h, :], bst[:, h, :, :].rearrange("p t n -> p (t n)"))
                    dve.drain()
                    dve.tensor_scalar(rv[:], mv[:, :, 1], 1e-5, None, ALU.add).then_inc(var_ready, 1)
                    dve.wait_ge(root_ready, 1)
                    dve.reciprocal(xscale[:], rt[:])
                    dve.drain()
                    newton(dve, xscale[:], rv[:], rtmp[:])
                    dve.wait_ge(gb_in, 32)
                    dve.tensor_tensor(xscale[:], xscale[:], gb[:, 0, :], ALU.mult)
                    dve.drain()
                    dve.tensor_tensor(rt[:], mv[:, :, 0], xscale[:], ALU.mult)
                    dve.drain()
                    dve.tensor_tensor(xbias[:], gb[:, 1, :], rt[:], ALU.subtract)

                @block.tensor
                def _(pe):
                    def turn(i, k):
                        pe.wait_ge(y_ready, i + 1)
                        wait_count(pe, yT_ready, i - 1)
                        for a in range(2):
                            for h in range(DH):
                                mm = pe.transpose(psT[:, k, (h * 2 + a) * P:(h * 2 + a + 1) * P],
                                                  y[:, k, a, h * P:(h + 1) * P], ident[:])
                        mm.then_inc(transposed, 1)

                    def fold(n):
                        hd, half = n // 2, n % 2
                        if n == 0:
                            pe.wait_ge(w_in, 32)
                        if n >= 2:
                            pe.wait_ge(fold_copied, n - 1)
                        for r in range(H):
                            mm = pe.matmul(psW[:, n % 2, r * NK:(r + 1) * NK], wq[:, half * H + r, hd * P:(hd + 1) * P],
                                           kT[:, half * H + r, :], start=True, stop=True)
                        mm.then_inc(folded, 1)

                    turn(0, 0)
                    turn(1, 1)
                    for n in range(2 * DH):
                        pairs_of(pe, max(2, n * QUARTER), (n + 1) * QUARTER, turn)
                        fold(n)

                @block.scalar
                def _(act):
                    def yT_pair(i, k):
                        act.wait_ge(transposed, i + 1)
                        wait_count(act, stats_done, i - 1)
                        wait_count(act, stored[k], 16 * ((i - k) // 2) if static(i) else 8 * (i - k))
                        act.activation(yT[:, k, :, :, :].rearrange("p h a n -> p (h a n)"), psT[:, k, :], ACT.Copy
                                       ).then_inc(yT_ready, 1)

                        act.wait_ge(keys_in[k], 32 * ((i - k) // 2 + 1) if static(i) else 16 * (i - k) + 32)
                        for which, keys in ((0, keyin), (1, keyout)):
                            act.activation(piece_of(keys, 0, i), raw[:, k, which, :], ACT.Copy, scale=KS
                                           ).then_inc(key_high, 1)

                    yT_pair(0, 0)
                    yT_pair(1, 1)
                    for n in range(2 * DH):
                        pairs_of(act, max(2, n * QUARTER), (n + 1) * QUARTER, yT_pair)
                        act.wait_ge(folded, n + 1)
                        act.activation(wc[:, n // 2, (n % 2) * 512:(n % 2 + 1) * 512], psW[:, n % 2, :],
                                       ACT.Copy).then_inc(fold_copied, 1)
                    act.wait_ge(var_ready, 1)
                    act.activation(rt[:], rv[:], ACT.Sqrt).then_inc(root_ready, 1)

        with Chip(nc, name + "b") as b:
            yTd = b.sb("yTd", [P, DH, P])
            yTs = b.sb("yTs", [P, DH, P])
            xnT = b.sb("xnT", [P, DH, P])
            sim = b.sb("sim", [P, S])
            top = b.sb("top", [P, 2 * H, K])
            topi = b.sb("topi", [P, 2 * H, K], U32)
            topf = b.sb("topf", [P, 2 * H, K], F16)
            pairs = b.sb("pairs", [P, H * K * K])
            pair = pairs[:].rearrange("p (h a b) -> p h a b", h=H, a=K)
            hot = pairs[:].bitcast(F16).rearrange("p (a n k) -> p a n k", a=2, k=K)
            best = b.sb("best", [P, H, K])
            pick = b.sb("pick", [P, H, K], U32)
            rank = b.sb("rank", [P, 2, HK], U32)
            ixy = b.sb("ixy", [P, 2, HK])
            upper = b.sb("upper", [P, HK])
            hi = b.sb("hi", [P, HK])
            lo = b.sb("lo", [P, HK])
            expo = b.sb("expo", [P, H, K])
            ex = b.sb("ex", [P, H, K])
            total = b.sb("total", [P, H])
            inv = b.sb("inv", [P, H])
            wt = b.sb("wt", [P, HK])
            NC = 5
            cat = b.sb("cat", [P, NC, 2, HK], F16)
            catT = b.sb("catT", [P, 2, NC, P // 2], F16)
            iota8 = b.sb("iota8", [P, K], U32)
            iota64 = b.sb("iota64", [P, NK, HM], F16)
            left = b.sb("left", [P, 2, P, HM], F16)
            right = b.sb("right", [P, 2, 2, 2 * NJ, HM], F16)
            A = b.sb("A", [P, 2, NJ, P])
            G = b.sb("G", [P, RING, JG * P])
            GP = b.sb("GP", [P, RING, 2, JG * P], F16)
            yTp = b.sb("yTp", [P, 2, 2, DH, P], F16)
            psO = b.ps("psO", [P, 2, 512])
            psA = b.ps("psA", [P, 2, 512])
            psS = b.ps("psS", [P, 512])
            psX = b.ps("psX", [P, 2, 512])
            psI = b.ps("psI", [P, 1024], F16)

            experts_in = [b.sem("experts_in0"), b.sem("experts_in1")]
            simil_in = [b.sem("simil_in0"), b.sem("simil_in1")]
            xn_ready, sims_done, sim_ready, sim_used = (b.sem(n) for n in ("xn_ready", "sims_done", "sim_ready", "sim_used"))
            expo_ready, ex_ready, cat_ready, cat_turned, catT_ready = (
                b.sem(n) for n in ("expo_ready", "ex_ready", "cat_ready", "cat_turned", "catT_ready"))
            factors_ready, built, A_ready = b.sem("factors_ready"), b.sem("built"), b.sem("A_ready")
            hot_ready, rest_ready = b.sem("hot_ready"), b.sem("rest_ready")
            o_done, gelu_done, prod_ready, prod_used, x_added = (
                b.sem(n) for n in ("o_done", "gelu_done", "prod_ready", "prod_used", "x_added"))
            y_high, y_split, high_ready, parts_ready = (
                b.sem(n) for n in ("y_high", "y_split", "high_ready", "parts_ready"))
            consts = b.sem("consts")

            LEAD = 4

            def run(eng, step):
                for t in range(-LEAD, 2):
                    step(t, t // 2)
                with eng.Fori(1, (NT - LEAD) // 2) as i:
                    for k in range(2):
                        step(2 * i + k, i, k)
                for t in range(NT - LEAD, NT):
                    step(t, t // 2)

            def has(t):
                return not static(t) or 0 <= t < NT

            with nc.Block() as block:
                @block.gpsimd
                def _(pool):
                    pool.iota(iota8[:], [[1, K]], base=0, channel_multiplier=0)
                    pool.iota(iota64[:], [[1, NK], [0, HM]], base=0, channel_multiplier=0,
                              allow_small_or_imprecise_dtypes=True).then_inc(consts, 1)

                    def rest(u, h, n, k):
                        cols = slice(n * NJ, (n + 1) * NJ)
                        pool.wait_ge(hot_ready, 2 * u + h + 1)
                        pool.tensor_tensor(right[:, h, 1, cols, :], right[:, h, 0, cols, :],
                                           catT[:, k, 4, h * HM:(h + 1) * HM].unsqueeze(1).broadcast_to([P, NJ, HM]),
                                           ALU.mult).then_inc(rest_ready, 1)

                    def low(t, g):
                        pool.wait_ge(high_ready, NG * t + g + 1)
                        pool.tensor_tensor(GP[:, g % RING, 1, :], G[:, g % RING, :], GP[:, g % RING, 0, :], ALU.subtract
                                           ).then_inc(parts_ready, 1)

                    def step(t, i, k=None):
                        k = t % 2 if k is None else k
                        for g in range(NG):
                            for n in range(2):
                                if g == 0 and has(t + 1):
                                    rest(t + 1, 1, n, 1 - k)
                                if g == 4 and has(t + 2):
                                    rest(t + 2, 0, n, k)
                            if has(t):
                                low(t, g)
                            if g == 4 and has(t + 1):
                                pool.wait_ge(y_high, t + 2)
                                pool.tensor_tensor(yTp[:, 1 - k, 1, :, :], yTd[:], yTp[:, 1 - k, 0, :, :],
                                                   ALU.subtract).then_inc(y_split, 1)
                    run(pool, step)

                @block.sync
                def _(sp):
                    def step(t, i, k=None):
                        k = t % 2 if k is None else k
                        u = t + LEAD
                        if has(u):
                            wait_count(sp, xn_ready, u)
                            sp.dma_start(yTs[:].rearrange("p h n -> p (h n)"), dram_tile(yT_dram, u)
                                         ).then_inc(simil_in[k], 16)
                        v = t + 1
                        if has(v):
                            wait_count(sp, y_split, v)
                            sp.dma_start(yTd[:].rearrange("p h n -> p (h n)"), dram_tile(yT_dram, v)
                                         ).then_inc(experts_in[1 - k], 16)
                    run(sp, step)

                @block.tensor
                def _(pe):
                    PASSES = ((0, 0), (0, 1), (1, 0))

                    def experts(t, g, k, i):
                        if g == 0:
                            pe.wait_ge(y_split, t + 1)
                        wait_count(pe, gelu_done, NG * t + g - 1)
                        for j in range(JG):
                            for h in range(DH):
                                at = h * NE + (g * JG + j) * P
                                for n, (kp, yp) in enumerate(PASSES):
                                    mm = pe.matmul(psO[:, g % 2, j * P:(j + 1) * P], keyin[:, kp, at:at + P],
                                                   yTp[:, k, yp, h, :], start=(h == 0 and n == 0),
                                                   stop=(h == DH - 1 and n == 2))
                        mm.then_inc(o_done, 1)

                    def combine(t, g, k):
                        pe.wait_ge(parts_ready, NG * t + g + 1)
                        if g == 0:
                            wait_count(pe, x_added, t - 1)
                        for j in range(JG):
                            jj = g * JG + j
                            for n, (gp, kp) in enumerate(PASSES):
                                mm = pe.matmul(psX[:, k, 0:D], GP[:, g % RING, gp, j * P:(j + 1) * P],
                                               keyout[:, kp, jj * D:(jj + 1) * D],
                                               start=(jj == 0 and n == 0), stop=(jj == NJ - 1 and n == 2))
                        mm.then_inc(prod_used, 1)

                    def build(u, q):
                        h = q // (NG // 2)
                        pe.wait_ge(factors_ready, 2 * u + h + 1)
                        wait_count(pe, A_ready, NG * u + q - 1)
                        for n in range(MQ):
                            m = (q * MQ + n) % HM
                            for part in range(2):
                                mm = pe.matmul(psA[:, q % 2, n * 2 * NJ:(n + 1) * 2 * NJ], left[:, h, :, m],
                                               right[:, h, part, :, m], start=(part == 0), stop=(part == 1))
                        mm.then_inc(built, 1)

                    def similarities(u, s):
                        pe.wait_ge(xn_ready, u + 1)
                        wait_count(pe, sim_ready, 2 * u + s)
                        for h in range(DH):
                            mm = pe.matmul(psS[:], xnT[:, h, :], wc[:, h, s * 512:(s + 1) * 512],
                                           start=(h == 0), stop=(h == DH - 1))
                        mm.then_inc(sims_done, 1)

                    def turn(u):
                        pe.wait_ge(cat_ready, u + 1)
                        wait_count(pe, catT_ready, u)
                        for n in range(NC):
                            mm = pe.transpose(psI[:, n * P:(n + 1) * P], cat[:, n, :, :].rearrange("p s n -> p (s n)"),
                                              ident16[:])
                        mm.then_inc(cat_turned, 1)

                    def step(t, i, k=None):
                        k = t % 2 if k is None else k
                        for g in range(NG):
                            if has(t):
                                experts(t, g, k, i)
                            if g == 1 and has(t + 2):
                                turn(t + 2)
                            if has(t + 1):
                                build(t + 1, g)
                            if g >= LAG and has(t):
                                combine(t, g - LAG, k)
                            if g < LAG and has(t - 1) and not (static(t) and t == 0):
                                combine(t - 1, NG - LAG + g, 1 - k)
                            if g in (3, 5) and has(t + LEAD):
                                similarities(t + LEAD, g // 5)
                    run(pe, step)
                    for g in range(NG - LAG, NG):
                        combine(NT - 1, g, 1)

                @block.scalar
                def _(act):
                    def high(t, g):
                        act.wait_ge(prod_ready, NG * t + g + 1)
                        wait_count(act, prod_used, NG * t + g - RING + 1)
                        act.activation(GP[:, g % RING, 0, :], G[:, g % RING, :], ACT.Copy).then_inc(high_ready, 1)

                    def step(t, i, k=None):
                        k = t % 2 if k is None else k
                        u = t + LEAD
                        for g in range(NG):
                            if g == 0 and has(u):
                                act.wait_ge(simil_in[k], 16 * (i + LEAD // 2 + 1))
                                wait_count(act, sims_done, 2 * u)
                                for h in range(DH):
                                    ins = act.activation(xnT[:, h, :], yTs[:, h, :], ACT.Identity,
                                                         scale=xscale[:, h:h + 1], bias=xbias[:, h:h + 1])
                                ins.then_inc(xn_ready, 1)
                            if has(t):
                                act.wait_ge(o_done, NG * t + g + 1)
                                wait_count(act, parts_ready, NG * t + g - RING + 1)
                                act.activation(G[:, g % RING, :], psO[:, g % 2, :], ACT.Gelu, scale=1 / KS
                                               ).then_inc(gelu_done, 1)
                            if g == 2 and has(t + 2):
                                v = t + 2
                                act.wait_ge(cat_turned, v + 1)
                                wait_count(act, factors_ready, 2 * v - 2)
                                for s in range(2):
                                    src = psI[64 * s:64 * s + 64, 0:NC * P].rearrange("p (n s m) -> p n s m", n=NC, s=2)
                                    ins = act.activation(catT[64 * s:64 * s + 64, k, :, :], src[:, :, s, :], ACT.Copy)
                                ins.then_inc(catT_ready, 1)
                            if has(t + 1):
                                act.wait_ge(built, NG * (t + 1) + g + 1)
                                wait_count(act, prod_ready, NG * t)
                                dst = A[:, 1 - k, :, :].rearrange("p j (s m) -> p j s m", s=2)[:, :, :, g * MQ:(g + 1) * MQ]
                                src = psA[:, g % 2, :].rearrange("p (m s j) -> p j s m", s=2, j=NJ)
                                act.activation(dst, src, ACT.Copy, scale=PS / WS).then_inc(A_ready, 1)
                            if g > 0 and has(t):
                                high(t, g - 1)
                            if g == 0 and has(t - 1) and not (static(t) and t == 0):
                                high(t - 1, NG - 1)
                            if g == 6 and has(t + 3):
                                act.wait_ge(expo_ready, t + 4)
                                act.activation(ex[:], expo[:], ACT.Exp).then_inc(ex_ready, 1)
                            if g in (4, 6) and has(u):
                                half = g // 6
                                act.wait_ge(sims_done, 2 * u + half + 1)
                                wait_count(act, sim_used, u)
                                act.activation(sim[:, half * 512:(half + 1) * 512], psS[:], ACT.Copy).then_inc(sim_ready, 1)
                            if g == 3 and has(t + 1):
                                act.wait_ge(experts_in[1 - k], 16 * ((t + 1) // 2 + 1 if static(t) else i + k + 1))
                                wait_count(act, o_done, NG * t)
                                act.activation(yTp[:, 1 - k, 0, :, :], yTd[:], ACT.Copy).then_inc(y_high, 1)
                    run(act, step)
                    high(NT - 1, NG - 1)

                @block.vector
                def _(dve):
                    flat = lambda ap: ap.rearrange("p h k -> p (h k)")

                    def product(t, g, k):
                        dve.wait_ge(gelu_done, NG * t + g + 1)
                        if g == 0:
                            dve.wait_ge(A_ready, NG * t + NG)
                        dve.tensor_tensor(G[:, g % RING, :], G[:, g % RING, :],
                                          A[:, k, g * JG:(g + 1) * JG, :].rearrange("p j n -> p (j n)"),
                                          ALU.mult).then_inc(prod_ready, 1)

                    def factors(u, h, stage, k):
                        ms = slice(h * HM, (h + 1) * HM)
                        def row(n):
                            return catT[:, k, n, ms].unsqueeze(1).broadcast_to([P, NK, HM])
                        if stage == 0:
                            dve.wait_ge(catT_ready, u + 1)
                            wait_count(dve, built, NG * (u - 1) + (NG // 2) * (h + 1))
                            dve.tensor_tensor(left[:, h, 0:NK, :], iota64[:], row(0), ALU.is_equal)
                            dve.tensor_tensor(right[:, h, 0, :, :], iota64[:], row(2), ALU.is_equal).then_inc(hot_ready, 1)
                        elif stage == 1:
                            dve.tensor_tensor(left[:, h, NK:P, :], iota64[:], row(1), ALU.is_equal)
                        elif stage == 3:
                            dve.wait_ge(rest_ready, 4 * u + 2 * h + 2)
                            dve.tensor_tensor(right[:, h, 0, :, :], right[:, h, 0, :, :], row(3), ALU.mult
                                              ).then_inc(factors_ready, 1)

                    def picks(u, g):
                        if g == 0:
                            for r in range(2 * H):
                                dve.max(top[:, r, :], sim[:, r * NK:(r + 1) * NK])
                        elif g == 1:
                            dve.drain()
                            for r in range(2 * H):
                                ins = dve.max_index(topi[:, r, :], top[:, r, :], sim[:, r * NK:(r + 1) * NK])
                            ins.then_inc(sim_used, 1)
                            dve.tensor_tensor(pair, top[:, 0:H, :].unsqueeze(3).broadcast_to([P, H, K, K]),
                                              top[:, H:2 * H, :].unsqueeze(2).broadcast_to([P, H, K, K]), ALU.add)
                        elif g == 2:
                            dve.drain()
                            dve.tensor_copy(topf[:], topi[:])
                            for r in range(H):
                                dve.max(best[:, r, :], pair[:, r, :, :].rearrange("p a b -> p (a b)"))
                        elif g == 3:
                            dve.drain()
                            dve.tensor_tensor(expo[:], best[:], best[:, :, 0:1].broadcast_to([P, H, K]),
                                              ALU.subtract).then_inc(expo_ready, 1)
                            for r in range(H):
                                dve.max_index(pick[:, r, :], best[:, r, :], pair[:, r, :, :].rearrange("p a b -> p (a b)"))
                        elif g == 4:
                            dve.drain()
                            dve.tensor_scalar(rank[:, 0, :], flat(pick[:]), 3, None, ALU.logical_shift_right)
                            dve.tensor_scalar(rank[:, 1, :], flat(pick[:]), K - 1, None, ALU.bitwise_and)
                            dve.drain()
                            dve.tensor_tensor(hot.rearrange("p a n k -> p (a n) k"),
                                              rank[:].rearrange("p a n -> p (a n)").unsqueeze(2).broadcast_to([P, 2 * HK, K]),
                                              iota8[:].unsqueeze(1).broadcast_to([P, 2 * HK, K]), ALU.is_equal)
                        elif g == 5:
                            dve.drain()
                            hv = hot.rearrange("p a (h r) k -> p (a h) r k", h=H)
                            dve.tensor_tensor(hv, hv, topf[:].unsqueeze(2).broadcast_to([P, 2 * H, K, K]), ALU.mult)
                        elif g == 6:
                            dve.drain()
                            dve.tensor_reduce(ixy[:].rearrange("p a n -> p (a n)"),
                                              hot.rearrange("p a n k -> p (a n) k"), AX_X, ALU.add)
                            dve.drain()
                            dve.tensor_scalar(upper[:], ixy[:, 1, :], float(NJ), None, ALU.is_ge)
                            dve.drain()
                            dve.scalar_tensor_tensor(out=hi[:], in0=ixy[:, 0, :], scalar=2.0, in1=upper[:],
                                                     op0=ALU.mult, op1=ALU.add)
                            dve.scalar_tensor_tensor(out=lo[:], in0=upper[:], scalar=-float(NJ), in1=ixy[:, 1, :],
                                                     op0=ALU.mult, op1=ALU.add)
                        else:
                            dve.wait_ge(ex_ready, u + 1)
                            dve.tensor_reduce(total[:], ex[:], AX_X, ALU.add)
                            twice = lambda ap: ap.unsqueeze(1).broadcast_to([P, 2, HK])
                            dve.drain()
                            wait_count(dve, cat_turned, u)
                            dve.reciprocal(inv[:], total[:])
                            dve.tensor_scalar(cat[:, 0, :, :], twice(hi[:]), 1.0, None, ALU.mult)
                            dve.tensor_scalar(cat[:, 1, :, :], twice(hi[:]), -float(NK), None, ALU.add)
                            dve.tensor_scalar(cat[:, 2, 0, :], lo[:], 1.0, None, ALU.mult)
                            dve.tensor_scalar(cat[:, 2, 1, :], lo[:], float(NJ), None, ALU.add)
                            dve.drain()
                            dve.scalar_tensor_tensor(out=wt[:].rearrange("p (h k) -> p h k", h=H), in0=ex[:], scalar=WS,
                                                     in1=inv[:].unsqueeze(2).broadcast_to([P, H, K]),
                                                     op0=ALU.mult, op1=ALU.mult)
                            dve.drain()
                            dve.tensor_scalar(cat[:, 3, :, :], twice(wt[:]), 1.0, None, ALU.mult)
                            dve.drain()
                            dve.tensor_tensor(cat[:, 4, :, :], twice(wt[:]), cat[:, 3, :, :], ALU.subtract
                                              ).then_inc(cat_ready, 1)

                    def add_x(t, k):
                        dve.wait_ge(prod_used, NG * t + NG)
                        xt = tile_of(x, t)
                        dve.scalar_tensor_tensor(out=xt, in0=psX[:, k, 0:D], scalar=0.5 / (PS * KS), in1=xt,
                                                 op0=ALU.mult, op1=ALU.add).then_inc(x_added, 1)

                    def step(t, i, k=None):
                        k = t % 2 if k is None else k
                        for g in range(NG):
                            if g == LAG + 1 and has(t - 1) and not (static(t) and t == 0):
                                add_x(t - 1, 1 - k)
                            if g == 3 and has(t + 1):
                                factors(t + 1, 1, 3, 1 - k)
                            if g == 7 and has(t + 2):
                                factors(t + 2, 0, 3, k)
                            if has(t):
                                product(t, g, k)
                            if g == 0 and has(t + 3):
                                dve.wait_ge(sim_ready, 2 * (t + 4))
                            if g < 3 and has(t + 1):
                                factors(t + 1, 1, g, 1 - k)
                            if 4 <= g < 7 and has(t + 2):
                                factors(t + 2, 0, g - 4, k)
                            if has(t + 3):
                                picks(t + 3, g)

                    dve.wait_ge(consts, 1)
                    run(dve, step)
                    add_x(NT - 1, 1)



def moe_ffn(nc, name, x, ident, NT, w, tokens=None):
    gate_w, gate_b, expert_w, expert_b = w
    E, KTOP = 8, 2
    SCORE_EPS, W_MIN = 1e-4, 0.1
    KS = 512.0
    PASSES = ((0, 0), (0, 1), (1, 0))
    GT = 4
    NGR = NT // GT
    DUOS = 2 * E // 2
    with Chip(nc, name) as c:
        mean, rstd = c.sb("mean", [P, NT]), c.sb("rstd", [P, NT])
        ew = c.sb("ew", [P, DH, E * D])
        ewp = c.sb("ewp", [P, 2, DH, E * D], F16)
        eb = c.sb("eb", [E, D])
        gw = c.sb("gw", [P, DH, E])
        gb = c.sb("gb", [E, 1])
        lgT = c.sb("lgT", [E, GT * P])
        iota = c.sb("iota", [P, E], U32)
        y = c.sb("y", [P, GT, D])
        yT = c.sb("yT", [P, 2, GT, DH, P])
        yTp = c.sb("yTp", [P, 2, 2, GT, DH, P], F16)
        score = c.sb("score", [P, GT, E])
        big = c.sb("big", [P, GT])
        diff = c.sb("diff", [P, GT, E])
        ex = c.sb("ex", [P, GT, E])
        total = c.sb("total", [P, GT])
        prob = c.sb("prob", [P, GT, E])
        best = c.sb("best", [P, GT, 8])
        besti = c.sb("besti", [P, GT, 8], U32)
        chosen = c.sb("chosen", [P, 2, GT, E])
        two = c.sb("two", [P, GT, 2])
        comb = c.sb("comb", [P, 2, GT, E])
        combT = c.sb("combT", [E, GT, P])
        psY = c.ps("psY", [P, 2, 2, 512])
        psT = c.ps("psT", [P, 512])
        psL = c.ps("psL", [P, 512])
        psG = c.ps("psG", [P, 512])
        psB = c.ps("psB", [P, 512])
        w_in, consts = c.sem("w_in"), c.sem("consts")
        y_ready, turned, turn_copied = c.sem("y_ready"), c.sem("turned"), c.sem("turn_copied")
        w_high, w_split, parts_ready = c.sem("w_high"), c.sem("w_split"), c.sem("parts_ready")
        gate_done, gate_copied = c.sem("gate_done"), c.sem("gate_copied")
        group_done, x_stored = c.sem("group_done"), c.sem("x_stored")
        logits_done, diff_ready, ex_ready, comb_ready = (
            c.sem(n) for n in ("logits_done", "diff_ready", "ex_ready", "comb_ready"))
        duo_done, duo_used, bias_done, bias_added = (
            c.sem(n) for n in ("duo_done", "duo_used", "bias_done", "bias_added"))
        TURNS = 3

        def run(eng, step):
            for n in range(-1, min(2, NGR)):
                step(n, n % 2)
            if NGR > 4:
                with eng.Fori(1, (NGR - 2) // 2) as i:
                    for k in range(2):
                        step(2 * i + k, k)
            for n in range(max(NGR - 2, 2), NGR):
                step(n, n % 2)

        def has(n):
            return not static(n) or 0 <= n < NGR

        def turns_before(n):
            if static(n) and n == 0:
                return 0
            return TURNS * n - 1

        def turns_of_comb(n):
            return TURNS * n + (4 if not static(n) or n < NGR - 1 else 2)

        def loads(sp):
            sp.dma_start(gw[:], gate_w.rearrange("(h p) e -> p h e", p=P)).then_inc(w_in, 16)
            sp.dma_start(gb[:], gate_b.rearrange("(e a) -> e a", a=1)).then_inc(w_in, 16)
            sp.dma_start(eb[:], expert_b).then_inc(w_in, 16)
            for h in range(DH):
                sp.dma_start(ew[:, h, :].rearrange("p (e f) -> p e f", e=E),
                             expert_w.rearrange("e (h p) f -> h p e f", p=P)[h]).then_inc(w_in, 16)

        row_statistics(nc, name, x, NT, mean, rstd, loads)
        with nc.Block() as block:
            @block.gpsimd
            def _(pool):
                pool.iota(iota[:], [[1, E]], base=0, channel_multiplier=0).then_inc(consts, 1)

                def step(n, k):
                    for half in range(2 if has(n + 1) else 0):
                        pool.wait_ge(turn_copied, turns_before(n + 1) + half + 1)
                        tiles = slice(2 * half, 2 * half + 2)
                        pool.tensor_tensor(yTp[:, 1 - k, 1, tiles, :, :], yT[:, 1 - k, tiles, :, :],
                                           yTp[:, 1 - k, 0, tiles, :, :], ALU.subtract).then_inc(parts_ready, 1)
                run(pool, step)

            @block.sync
            def _(sp):
                def step(n, k):
                    if has(n):
                        sp.wait_ge(group_done, n + 1)
                        tiles = slice(GT * n, GT * (n + 1)) if static(n) else bass.ds(GT * n, GT)
                        sp.dma_start(tokens[:, tiles, :], x[:, tiles, :]).then_inc(x_stored, 16)
                if tokens is not None:
                    run(sp, step)
                    sp.wait_ge(x_stored, 16 * NGR)

            @block.tensor
            def _(pe):
                def turn_tiles(n, half):
                    if half == 0:
                        pe.wait_ge(y_ready, n + 1)
                    wait_count(pe, turn_copied, turns_before(n) + half)
                    for a in range(2):
                        for h in range(DH):
                            mm = pe.transpose(psT[:, (a * DH + h) * P:(a * DH + h + 1) * P],
                                              y[:, 2 * half + a, h * P:(h + 1) * P], ident[:])
                    mm.then_inc(turned, 1)

                def turn_comb(n, k):
                    pe.wait_ge(comb_ready, n + 1)
                    wait_count(pe, turn_copied, turns_of_comb(n))
                    for a in range(GT):
                        mm = pe.transpose(psT[0:E, a * P:(a + 1) * P], comb[:, k, a, :], ident[:])
                    mm.then_inc(turned, 1)

                def bias(n, half):
                    pe.wait_ge(turn_copied, turns_of_comb(n) + 1)
                    wait_count(pe, bias_added, 2 * n + half)
                    for a in range(2):
                        mm = pe.matmul(psB[:, a * D:(a + 1) * D], combT[:, 2 * half + a, :], eb[:],
                                       start=True, stop=True)
                    mm.then_inc(bias_done, 1)

                def logits(n, k):
                    if static(n) and n == 0:
                        pe.wait_ge(w_in, 16 * (3 + DH))
                    pe.wait_ge(turn_copied, turns_before(n) + 2)
                    wait_count(pe, gate_copied, n)
                    for h in range(DH):
                        mm = pe.matmul(psL[0:E, :], gw[:, h, :], yT[:, k, :, h, :], start=(h == 0), stop=(h == DH - 1))
                    mm.then_inc(gate_done, 1)

                def turn_logits(n):
                    pe.wait_ge(gate_copied, n + 1)
                    wait_count(pe, diff_ready, n)
                    for a in range(GT):
                        mm = pe.matmul(psG[:, a * E:(a + 1) * E], lgT[:, a * P:(a + 1) * P], ident[0:E, 0:E],
                                       start=True, stop=True)
                    mm.then_inc(logits_done, 1)

                def duo(n, u, k):
                    ep, tp = u % (E // 2), u // (E // 2)
                    if static(n) and n == 0 and u == 0:
                        pe.wait_ge(w_split, DH + 1)
                    if ep == 0:
                        pe.wait_ge(parts_ready, 2 * n + tp + 1)
                    wait_count(pe, duo_used, DUOS * n + u - 1)
                    for a in range(2):
                        for h in range(DH):
                            for q, (yp, wp) in enumerate(PASSES):
                                mm = pe.matmul(psY[:, u % 2, a, :], yTp[:, k, yp, 2 * tp + a, h, :],
                                               ewp[:, wp, h, ep * 2 * D:(ep + 1) * 2 * D],
                                               start=(h == 0 and q == 0), stop=(h == DH - 1 and q == 2))
                    mm.then_inc(duo_done, 1)

                def step(n, k):
                    for u in range(DUOS):
                        if has(n):
                            duo(n, u, k)
                        if u in (0, 1) and has(n + 1):
                            turn_tiles(n + 1, u)
                        if u == 2 and has(n):
                            turn_comb(n, k)
                        if u in (3, 5) and has(n):
                            bias(n, (u - 3) // 2)
                        if u == 3 and has(n + 1):
                            logits(n + 1, 1 - k)
                        if u == 4 and has(n + 1):
                            turn_logits(n + 1)
                run(pe, step)

            @block.scalar
            def _(act):
                def copy_tiles(n, half, k):
                    act.wait_ge(turned, turns_before(n) + half + 1)
                    tiles = slice(2 * half, 2 * half + 2)
                    act.activation(yT[:, k, tiles, :, :].rearrange("p a h n -> p (a h n)"), psT[:], ACT.Copy)
                    act.activation(yTp[:, k, 0, tiles, :, :].rearrange("p a h n -> p (a h n)"), psT[:], ACT.Copy
                                   ).then_inc(turn_copied, 1)

                def copy_comb(n):
                    act.wait_ge(turned, turns_of_comb(n) + 1)
                    wait_count(act, bias_done, 2 * n)
                    act.activation(combT[:].rearrange("e a n -> e (a n)"), psT[0:E, :], ACT.Copy
                                   ).then_inc(turn_copied, 1)

                def step(n, k):
                    if has(n + 1):
                        copy_tiles(n + 1, 0, 1 - k)
                        copy_tiles(n + 1, 1, 1 - k)
                    if static(n) and n == -1:
                        act.wait_ge(w_in, 16 * (3 + DH))
                        for h in range(DH):
                            act.activation(ewp[:, 0, h, :], ew[:, h, :], ACT.Copy, scale=KS).then_inc(w_high, 1)
                    if has(n):
                        copy_comb(n)
                    if has(n + 1):
                        act.wait_ge(gate_done, n + 2)
                        wait_count(act, logits_done, n + 1)
                        act.activation(lgT[:], psL[0:E, :], ACT.Identity, bias=gb[:]).then_inc(gate_copied, 1)
                        act.wait_ge(diff_ready, n + 2)
                        act.activation(ex[:], diff[:], ACT.Exp).then_inc(ex_ready, 1)
                run(act, step)

            @block.vector
            def _(dve):
                def normalise(n):
                    wait_count(dve, turned, turns_before(n - 1) + 2 if not static(n) or n > 0 else 0)
                    for a in range(GT):
                        t = GT * n + a
                        ins = dve.tensor_scalar(y[:, a, :], tile_of(x, t), mean[:, one(t)], rstd[:, one(t)],
                                                ALU.subtract, ALU.mult)
                    ins.then_inc(y_ready, 1)

                def route_scores(n):
                    dve.wait_ge(logits_done, n + 1)
                    dve.tensor_scalar(score[:].rearrange("p a e -> p (a e)"), psG[:, 0:GT * E], SCORE_EPS, None, ALU.max)
                    dve.drain()
                    dve.tensor_reduce(big[:], score[:], AX_X, ALU.max)
                    dve.drain()
                    dve.tensor_tensor(diff[:], score[:], big[:].unsqueeze(2).broadcast_to([P, GT, E]), ALU.subtract
                                      ).then_inc(diff_ready, 1)

                def route_weights(n, k, piece):
                    wide = lambda ap: ap.unsqueeze(2).broadcast_to([P, GT, E])
                    if piece == 0:
                        dve.wait_ge(ex_ready, n + 1)
                        dve.tensor_reduce(total[:], ex[:], AX_X, ALU.add)
                        dve.drain()
                        dve.reciprocal(total[:], total[:])
                        dve.drain()
                        dve.tensor_tensor(prob[:], ex[:], wide(total[:]), ALU.mult)
                    elif piece == 1:
                        dve.drain()
                        for a in range(GT):
                            dve.max(best[:, a, :], prob[:, a, :])
                        dve.drain()
                        for a in range(GT):
                            dve.max_index(besti[:, a, :], best[:, a, :], prob[:, a, :])
                        dve.tensor_scalar(two[:], best[:, :, 0:KTOP], W_MIN, None, ALU.max)
                    else:
                        dve.drain()
                        for q in range(KTOP):
                            dve.tensor_tensor(chosen[:, q, :, :], iota[:].unsqueeze(1).broadcast_to([P, GT, E]),
                                              besti[:, :, q:q + 1].broadcast_to([P, GT, E]), ALU.is_equal)
                        dve.tensor_reduce(total[:], two[:], AX_X, ALU.add)
                        dve.tensor_scalar(prob[:], prob[:], W_MIN, 0.5 / KTOP / KS, ALU.max, ALU.mult)
                        dve.drain()
                        dve.reciprocal(total[:], total[:])
                        dve.tensor_tensor(chosen[:, 0, :, :], chosen[:, 0, :, :], chosen[:, 1, :, :], ALU.add)
                        dve.drain()
                        dve.tensor_tensor(prob[:], prob[:], wide(total[:]), ALU.mult)
                        dve.drain()
                        dve.tensor_tensor(comb[:, k, :, :], prob[:], chosen[:, 0, :, :], ALU.mult).then_inc(comb_ready, 1)

                def combine(n, u, k):
                    ep, tp = u % (E // 2), u // (E // 2)
                    for q in range(2):
                        e = 2 * ep + q
                        dve.drain()
                        if q == 0:
                            dve.wait_ge(duo_done, DUOS * n + u + 1)
                        for a in range(2):
                            ta = 2 * tp + a
                            xt = tile_of(x, GT * n + ta)
                            ins = dve.scalar_tensor_tensor(out=xt, in0=psY[:, u % 2, a, q * D:(q + 1) * D],
                                                           scalar=comb[:, k, ta, e:e + 1], in1=xt,
                                                           op0=ALU.mult, op1=ALU.add)
                    ins.then_inc(duo_used, 1)

                def add_bias(n, half):
                    dve.drain()
                    dve.wait_ge(bias_done, 2 * n + half + 1)
                    t = GT * n + 2 * half
                    xt = (x[:, t:t + 2, :] if static(t) else x[:, bass.ds(t, 2), :]).rearrange("p a n -> p (a n)")
                    dve.tensor_tensor(xt, psB[:], xt, ALU.add).then_inc(bias_added, 1)

                dve.wait_ge(consts, 1)

                def step(n, k):
                    if static(n) and n == -1:
                        normalise(0)
                        for h in range(DH):
                            dve.wait_ge(w_high, h + 1)
                            dve.scalar_tensor_tensor(out=ewp[:, 1, h, :], in0=ew[:, h, :], scalar=KS, in1=ewp[:, 0, h, :],
                                                     op0=ALU.mult, op1=ALU.subtract).then_inc(w_split, 1)
                        dve.tensor_scalar(eb[:], eb[:], KS, None, ALU.mult).then_inc(w_split, 1)
                    for u in range(DUOS):
                        if has(n):
                            combine(n, u, k)
                        if u == 4 and has(n):
                            add_bias(n, 0)
                        if u == 3 and has(n + 2):
                            normalise(n + 2)
                        if u == 5 and has(n + 1):
                            route_scores(n + 1)
                        if u == 6 and has(n):
                            add_bias(n, 1)
                        if u == 6 and has(n + 1):
                            route_weights(n + 1, 1 - k, 0)
                        if u == DUOS - 1 and has(n):
                            dve.drain()
                            dve.memset(big[:, 0:1], 0.0).then_inc(group_done, 1)
                        if u == 7 and has(n + 1):
                            route_weights(n + 1, 1 - k, 1)
                            route_weights(n + 1, 1 - k, 2)
                run(dve, step)



def recurrent_block(nc, name, x, ident, NT, SEQ, w):
    norm1, norm2, in_projT, out_projT, fcT, projT = w
    HD = 16
    CH = 64
    GT = 4
    SEG = GT * P
    NS = NT // GT
    NC = SEG // CH
    PARTS = 5
    F = fcT.shape[2]
    MF = F // P
    KS = 512.0
    PASSES = ((0, 0), (0, 1), (1, 0))
    RES = float(1.0 / np.sqrt(2.0))
    QEPS = float(np.finfo(np.float32).eps)
    with Chip(nc, name) as c:
        mean, rstd, var_eps = c.sb("mean", [P, NT]), c.sb("rstd", [P, NT]), c.sb("var_eps", [P, NT])
        raw = c.sb("raw", [P, DH * (PARTS * D + 2 * F)])
        assert MF * D == DH * F and PARTS * SEG <= PARTS * D + 2 * F
        wi = raw[:, 0:DH * PARTS * D].rearrange("p (h n) -> p h n", h=DH)
        wf = raw[:, DH * PARTS * D:DH * (PARTS * D + F)].rearrange("p (h n) -> p h n", h=DH)
        wp = raw[:, DH * (PARTS * D + F):].rearrange("p (m n) -> p m n", m=MF)
        wo = c.sb("wo", [P, DH, D])
        wip = c.sb("wip", [P, 2, DH, PARTS * D], F16)
        wfp = c.sb("wfp", [P, 2, DH, F], F16)
        wpp = c.sb("wpp", [P, 2, MF, D], F16)
        n1, n2 = c.sb("n1", [P, DH]), c.sb("n2", [P, DH])
        scale1 = c.sb("scale1", [P, NT])
        t1, t2, t3 = c.sb("t1", [P, NT]), c.sb("t2", [P, NT]), c.sb("t3", [P, NT])
        heads = c.sb("heads", [P, P])
        goes_on = c.sb("goes_on", [P, NS])
        inside = c.sb("inside", [P, SEG])
        two_bias, q_eps, r_eps = c.sb("two_bias", [P, 1]), c.sb("q_eps", [P, 1]), c.sb("r_eps", [P, 1])
        y = c.sb("y", [P, GT, D])
        h1T = c.sb("h1T", [P, DH, SEG])
        h1p = c.sb("h1p", [P, 2, DH, SEG], F16)
        seg = lambda n: c.sb(n, [P, DH, SEG])
        five = c.sb("five", [P, PARTS, DH, SEG])
        FIVE = (five, raw[:, 0:PARTS * DH * SEG].rearrange("p (f h n) -> p f h n", f=PARTS, h=DH))
        qq, rq = seg("qq"), seg("rq")
        first, prefix, ratio, acc, mixed = (seg(n) for n in ("first", "prefix", "ratio", "acc", "mixed"))
        chunk_end = c.sb("chunk_end", [P, DH, NC])
        prefix_end = c.sb("prefix_end", [P, DH, NC])
        state = c.sb("state", [P, DH, NC + 1])
        x1 = c.sb("x1", [P, GT, D])
        sq = c.sb("sq", [P, D])
        ms, root2, r2, r2t = (c.sb(n, [P, GT]) for n in ("ms", "root2", "r2", "r2t"))
        h2 = c.sb("h2", [P, GT, D])
        h2T = c.sb("h2T", [P, DH, SEG])
        h2p = c.sb("h2p", [P, 2, DH, SEG], F16)
        hid = c.sb("hid", [P, MF, SEG])
        hidp = c.sb("hidp", [P, 2, MF, SEG], F16)
        psR = c.ps("psR", [P, 2, 512])
        psT = c.ps("psT", [P, 512])
        psX = c.ps("psX", [P, 2, 512])
        psM = c.ps("psM", [P, 2, 512])
        w_in, consts, sq1_ready, root1_ready, weights_ready = (
            c.sem(n) for n in ("w_in", "consts", "sq1_ready", "root1_ready", "weights_ready"))
        y_ready, turned, turn_copied, filled, emptied = (
            c.sem(n) for n in ("y_ready", "turned", "turn_copied", "filled", "emptied"))
        qq_ready, mixed_ready, attn_done, x1_ready, ms_ready, root2_ready, h2_ready = (
            c.sem(n) for n in ("qq_ready", "mixed_ready", "attn_done", "x1_ready", "ms_ready", "root2_ready", "h2_ready"))
        mlp_done, mlp_added = c.sem("mlp_done"), c.sem("mlp_added")
        w_scaled, w_high, hid_high, h1_parts, h2_parts, hid_parts = (
            c.sem(n) for n in ("w_scaled", "w_high", "hid_high", "h1_parts", "h2_parts", "hid_parts"))
        TILES_P = PARTS * DH
        USES = TILES_P + MF + DH

        def runs(n):
            return not static(n) or 0 <= n < NS

        LOOP = 2

        def run(eng, step):
            last = LOOP + (NS - 2 - LOOP) // 2 * 2 if NS - 2 > LOOP else LOOP
            for n in range(-2, LOOP):
                step(n, n % 2)
            if last > LOOP:
                with eng.Fori(LOOP // 2, last // 2) as i:
                    for k in range(2):
                        step(2 * i + k, k)
            for n in range(last, NS + 2):
                step(n, n % 2)

        def before(n, uses, per_step):
            if static(n):
                return sum(uses(e) for e in range(-2, n))
            return per_step * n + before(LOOP, uses, per_step) - per_step * LOOP

        def proj_base(n):
            return before(n, lambda e: TILES_P * runs(e + 1) + MF * runs(e - 1) + DH * runs(e), USES)

        def rms_base(n):
            return proj_base(n) + TILES_P * runs(n + 1)

        def fc_base(n):
            return rms_base(n) + DH * runs(n)

        def turns_h1(n):
            return before(n, lambda e: 2 * runs(e - 1) + 2 * runs(e + 2), 4)

        def turns_h2(n):
            return turns_h1(n) + 2 * runs(n + 2)

        SPLIT = ((wi, wip), (wf, wfp), (wp, wpp))

        def loads(sp):
            sp.dma_start(wi, in_projT).then_inc(w_in, 16)
            sp.dma_start(n1[:], norm1).then_inc(w_in, 16)
            sp.dma_start(n2[:], norm2).then_inc(w_in, 16)
            sp.dma_start(wf, fcT).then_inc(w_in, 16)
            sp.dma_start(wo[:], out_projT).then_inc(w_in, 16)
            sp.dma_start(wp, projT).then_inc(w_in, 16)

        row_statistics(nc, name, x, NT, mean, rstd, loads, var_eps)
        with nc.Block() as block:
            @block.gpsimd
            def _(pool):
                pool.memset(heads[:], 1.0 / HD).then_inc(consts, 1)
                pool.memset(goes_on[:], 1.0).then_inc(consts, 1)
                pool.memset(inside[:], 1.0).then_inc(consts, 1)
                pool.memset(first[:], 0.0)
                pool.memset(state[:], 0.0)
                pool.memset(two_bias[:], 2.0)
                pool.memset(q_eps[:], QEPS)
                pool.memset(r_eps[:], 1e-6)
                pool.wait_ge(consts, 3)
                hv = heads[:].rearrange("p (h d) -> p h d", d=HD)
                pool.affine_select(out=hv, in_=hv, compare_op=ALU.is_ge, fill=0.0, base=0,
                                   pattern=[[-HD, P // HD], [0, HD]], channel_multiplier=1).then_inc(consts, 1)
                pool.memset(goes_on[:].rearrange("p (b s) -> p b s", s=SEQ // SEG)[:, :, 0:1], 0.0)
                pool.memset(inside[:].rearrange("p (n c) -> p n c", c=CH)[:, :, 0:1], 0.0)
                pool.wait_ge(consts, 4)
                pool.affine_select(out=hv, in_=hv, compare_op=ALU.is_ge, fill=0.0, base=HD - 1,
                                   pattern=[[HD, P // HD], [0, HD]], channel_multiplier=-1).then_inc(consts, 1)

                def low_turned(src, parts, base, done):
                    for half in range(2):
                        cols = slice(2 * half * P, 2 * (half + 1) * P)
                        pool.wait_ge(turn_copied, base + half + 1)
                        pool.tensor_tensor(parts[:, 1, :, cols], src[:, :, cols], parts[:, 0, :, cols], ALU.subtract
                                           ).then_inc(done, 1)

                def step(n, k):
                    if runs(n + 2):
                        low_turned(h1T, h1p, turns_h1(n), h1_parts)
                    if runs(n - 1):
                        low_turned(h2T, h2p, turns_h2(n), h2_parts)
                        for m in range(MF):
                            pool.wait_ge(hid_high, MF * (n - 1) + m + 1)
                            pool.tensor_tensor(hidp[:, 1, m, :], hid[:, m, :], hidp[:, 0, m, :], ALU.subtract
                                               ).then_inc(hid_parts, 1)
                run(pool, step)

            @block.tensor
            def _(pe):
                pe.wait_ge(consts, 5)

                def turn(src, base, half):
                    wait_count(pe, turn_copied, base + half)
                    for hh in range(DH):
                        for b in range(2):
                            mm = pe.transpose(psT[:, (2 * hh + b) * P:(2 * hh + b + 1) * P],
                                              src[:, 2 * half + b, hh * P:(hh + 1) * P], ident[:])
                    mm.then_inc(turned, 1)

                def mlp(n, half):
                    if half == 0:
                        pe.wait_ge(hid_parts, MF * (n + 1))
                        wait_count(pe, mlp_added, n)
                    for t in (2 * half, 2 * half + 1):
                        for m in range(MF):
                            for e, (hpart, wpart) in enumerate(PASSES):
                                mm = pe.matmul(psM[:, t // 2, (t % 2) * D:(t % 2 + 1) * D],
                                               hidp[:, hpart, m, t * P:(t + 1) * P], wpp[:, wpart, m, :],
                                               start=(m == 0 and e == 0), stop=(m == MF - 1 and e == 2))
                    if half == 1:
                        mm.then_inc(mlp_done, 1)

                def step(n, k):
                    if runs(n - 1):
                        pe.wait_ge(mixed_ready, n)
                        wait_count(pe, x1_ready, n - 1)
                        for t in range(GT):
                            for hh in range(DH):
                                mm = pe.matmul(psX[:, t // 2, (t % 2) * D:(t % 2 + 1) * D],
                                               mixed[:, hh, t * P:(t + 1) * P], wo[:, hh, :],
                                               start=(hh == 0), stop=(hh == DH - 1))
                        mm.then_inc(attn_done, 1)
                    if runs(n + 1):
                        if static(n) and n == -1:
                            pe.wait_ge(weights_ready, 3)
                        pe.wait_ge(h1_parts, 2 * (n + 2))
                        for m in range(TILES_P):
                            wait_count(pe, emptied, proj_base(n) + m - 1)
                            for hh in range(DH):
                                for e, (wpart, hpart) in enumerate(PASSES):
                                    mm = pe.matmul(psR[:, m % 2, :], wip[:, wpart, hh, m * P:(m + 1) * P],
                                                   h1p[:, hpart, hh, :], start=(hh == 0 and e == 0),
                                                   stop=(hh == DH - 1 and e == 2))
                            mm.then_inc(filled, 1)
                    if runs(n + 2):
                        pe.wait_ge(y_ready, n + 3)
                        turn(y, turns_h1(n), 0)
                        turn(y, turns_h1(n), 1)
                    if runs(n):
                        pe.wait_ge(qq_ready, n + 1)
                        for hh in range(DH):
                            wait_count(pe, emptied, rms_base(n) + hh - 1)
                            pe.matmul(psR[:, hh % 2, :], heads[:], qq[:, hh, :], start=True, stop=True
                                      ).then_inc(filled, 1)
                    for half in range(2):
                        if runs(n - 1):
                            pe.wait_ge(h2_ready, n)
                            turn(h2, turns_h2(n), half)
                        if runs(n - 2):
                            mlp(n - 2, half)
                    if runs(n - 1):
                        pe.wait_ge(h2_parts, 2 * n)
                        for m in range(MF):
                            wait_count(pe, emptied, fc_base(n) + m - 1)
                            for hh in range(DH):
                                for e, (wpart, hpart) in enumerate(PASSES):
                                    mm = pe.matmul(psR[:, m % 2, :], wfp[:, wpart, hh, m * P:(m + 1) * P],
                                                   h2p[:, hpart, hh, :], start=(hh == 0 and e == 0),
                                                   stop=(hh == DH - 1 and e == 2))
                            mm.then_inc(filled, 1)
                run(pe, step)

            @block.scalar
            def _(act):
                act.wait_ge(sq1_ready, 1)
                act.activation(t2[:], t1[:], ACT.Sqrt).then_inc(root1_ready, 1)
                act.wait_ge(consts, 5)

                def copy_turned(dst, parts, base):
                    for half in range(2):
                        cols = slice(2 * half * P, 2 * (half + 1) * P)
                        src = psT[:].rearrange("p (h n) -> p h n", h=DH)
                        act.wait_ge(turned, base + half + 1)
                        act.activation(dst[:, :, cols], src, ACT.Copy)
                        act.activation(parts[:, 0, :, cols], src, ACT.Copy).then_inc(turn_copied, 1)

                def mean_square(n):
                    act.wait_ge(x1_ready, n + 1)
                    for t in range(GT):
                        if t:
                            act.drain()
                        act.activation(sq[:], x1[:, t, :], ACT.Square, accum_out=ms[:, t:t + 1])
                    act.drain()
                    act.activation(root2[:], ms[:], ACT.Sqrt, bias=r_eps[:], scale=1.0 / D).then_inc(root2_ready, 1)

                def hid_parts_high(n, m):
                    act.wait_ge(emptied, fc_base(n) + m + 1)
                    act.activation(hidp[:, 0, m, :], hid[:, m, :], ACT.Copy).then_inc(hid_high, 1)

                def step(n, k):
                    if runs(n + 1):
                        wait_count(act, mixed_ready, n)
                        for m in range(TILES_P):
                            if m == TILES_P // 2 and runs(n - 1):
                                mean_square(n - 1)
                            act.wait_ge(filled, proj_base(n) + m + 1)
                            dst = FIVE[1 - k][:, m // DH, m % DH, :]
                            src = psR[:, m % 2, :]
                            part = "qkvag"[m // DH]
                            if part in "qv":
                                ins = act.activation(dst, src, ACT.Copy, scale=1 / KS)
                            elif part == "k":
                                ins = act.activation(dst, src, ACT.Tanh, scale=1 / KS)
                            elif part == "a":
                                ins = act.activation(dst, src, ACT.Sigmoid, bias=two_bias[:], scale=1 / KS)
                            else:
                                ins = act.activation(dst, src, ACT.Sigmoid, scale=1 / KS)
                            ins.then_inc(emptied, 1)
                    elif runs(n - 1):
                        mean_square(n - 1)
                    if runs(n + 2):
                        wait_count(act, h1_parts, 2 * (n + 2))
                        copy_turned(h1T, h1p, turns_h1(n))
                    if runs(n):
                        wait_count(act, mixed_ready, n)
                        for hh in range(DH):
                            act.wait_ge(filled, rms_base(n) + hh + 1)
                            act.activation(rq[:, hh, :], psR[:, hh % 2, :], ACT.Sqrt, bias=q_eps[:]).then_inc(emptied, 1)
                    if runs(n - 1):
                        wait_count(act, h2_parts, 2 * (n - 1))
                        copy_turned(h2T, h2p, turns_h2(n))
                        wait_count(act, hid_parts, MF * (n - 1))
                        wait_count(act, mlp_done, n - 1)
                        for m in range(MF):
                            act.wait_ge(filled, fc_base(n) + m + 1)
                            act.activation(hid[:, m, :], psR[:, m % 2, :], ACT.Silu, scale=1 / KS).then_inc(emptied, 1)
                            if m > 0:
                                hid_parts_high(n, m - 1)
                        hid_parts_high(n, MF - 1)
                    if static(n) and n == -2:
                        act.wait_ge(w_scaled, 1)
                        for w, parts in SPLIT:
                            act.activation(parts[:, 0, :, :], w, ACT.Copy, scale=KS).then_inc(w_high, 1)
                run(act, step)

            @block.vector
            def _(dve):
                dve.tensor_scalar(t1[:], var_eps[:], -LN_EPS, None, ALU.add)
                dve.tensor_tensor(t2[:], rstd[:], rstd[:], ALU.mult)
                dve.drain()
                dve.tensor_tensor(t3[:], t1[:], t2[:], ALU.mult)
                dve.drain()
                dve.tensor_scalar(t1[:], t3[:], 1e-6, None, ALU.add).then_inc(sq1_ready, 1)
                dve.wait_ge(root1_ready, 1)
                dve.reciprocal(scale1[:], t2[:])
                dve.drain()
                newton(dve, scale1[:], t1[:], t3[:])
                dve.tensor_tensor(scale1[:], scale1[:], rstd[:], ALU.mult)
                dve.wait_ge(w_in, 96)
                for hh in range(DH):
                    dve.tensor_scalar(wi[:, hh, :], wi[:, hh, :], n1[:, hh:hh + 1], None, ALU.mult)
                    dve.tensor_scalar(wf[:, hh, :], wf[:, hh, :], n2[:, hh:hh + 1], None, ALU.mult)
                dve.drain()
                dve.memset(t3[:, 0:1], 0.0).then_inc(w_scaled, 1)
                dve.wait_ge(consts, 5)
                ends = lambda ap: ap.rearrange("p h (n c) -> p h n c", c=CH)[:, :, :, CH - 1]
                starts = lambda ap: ap.rearrange("p h (n c) -> p h n c", c=CH)[:, :, :, 0]

                def normalise(n):
                    wait_count(dve, turned, turns_h1(n - 3) + 2 if not static(n) or n > 0 else 0)
                    for b in range(GT):
                        t = GT * n + b
                        ins = dve.tensor_scalar(y[:, b, :], tile_of(x, t), mean[:, one(t)], scale1[:, one(t)],
                                                ALU.subtract, ALU.mult)
                    ins.then_inc(y_ready, 1)

                def second_norm(n):
                    dve.wait_ge(root2_ready, n + 1)
                    dve.reciprocal(r2[:], root2[:])
                    dve.tensor_scalar(r2t[:], ms[:], 1.0 / D, 1e-6, ALU.mult, ALU.add)
                    dve.drain()
                    newton(dve, r2[:], r2t[:], root2[:])
                    for b in range(GT):
                        ins = dve.tensor_scalar(h2[:, b, :], x1[:, b, :], r2[:, b:b + 1], None, ALU.mult)
                    ins.then_inc(h2_ready, 1)

                def middle_part(n):
                    if runs(n - 1):
                        first_residual(n - 1)

                def late_part(n):
                    if runs(n - 1):
                        second_norm(n - 1)

                def recurrence(n, parity):
                    five_of = FIVE[parity]
                    q, k, v, a, g = (five_of[:, part] for part in range(PARTS))
                    dve.wait_ge(emptied, proj_base(n - 1) + 2)
                    dve.tensor_tensor(qq[:], q, q, ALU.mult).then_inc(qq_ready, 1)
                    dve.wait_ge(emptied, proj_base(n - 1) + 8)
                    dve.tensor_tensor(k, k, v, ALU.mult)
                    dve.tensor_scalar(a, a, 0.6, 0.9995, ALU.max, ALU.min)
                    dve.tensor_scalar(state[:, :, 0], state[:, :, NC], goes_on[:, one(n)], None, ALU.mult)
                    dve.drain()
                    dve.tensor_copy(starts(first[:]), starts(a))
                    dve.drain()
                    dve.memset(starts(a), 0.0)
                    dve.drain()
                    for hh in range(DH):
                        dve.tensor_tensor_scan(prefix[:, hh, :], a[:, hh, :], first[:, hh, :], 0.0, ALU.mult, ALU.add)
                    dve.drain()
                    dve.tensor_scalar(ratio[:], prefix[:], 1e-6, None, ALU.max)
                    middle_part(n)
                    dve.drain()
                    dve.reciprocal(ratio[:], ratio[:])
                    late_part(n)
                    dve.drain()
                    dve.tensor_tensor(ratio[:], ratio[:], k, ALU.mult)
                    dve.drain()
                    for hh in range(DH):
                        dve.tensor_tensor_scan(acc[:, hh, :], inside[:], ratio[:, hh, :], 0.0, ALU.mult, ALU.add)
                    dve.tensor_copy(prefix_end[:], ends(prefix[:]))
                    dve.drain()
                    dve.tensor_tensor(chunk_end[:], prefix_end[:], ends(acc[:]), ALU.mult)
                    dve.drain()
                    for hh in range(DH):
                        dve.tensor_tensor_scan(state[:, hh, 1:NC + 1], prefix_end[:, hh, :], chunk_end[:, hh, :],
                                               state[:, hh, 0:1], ALU.mult, ALU.add)
                    dve.drain()
                    for hh in range(DH):
                        av = acc[:, hh, :].rearrange("p (n c) -> p n c", c=CH)
                        dve.tensor_tensor(av, av, state[:, hh, 0:NC].unsqueeze(2).broadcast_to([P, NC, CH]), ALU.add)
                    dve.drain()
                    dve.tensor_tensor(acc[:], acc[:], prefix[:], ALU.mult)
                    dve.drain()
                    dve.tensor_tensor(acc[:], acc[:], q, ALU.mult)
                    dve.wait_ge(emptied, rms_base(n) + 2)
                    dve.reciprocal(rq[:], rq[:])
                    dve.drain()
                    dve.tensor_tensor(acc[:], acc[:], rq[:], ALU.mult)
                    dve.drain()
                    dve.tensor_tensor(acc[:], acc[:], v, ALU.subtract)
                    dve.drain()
                    dve.tensor_tensor(acc[:], acc[:], g, ALU.mult)
                    dve.drain()
                    wait_count(dve, attn_done, n)
                    dve.tensor_tensor(mixed[:], acc[:], v, ALU.add).then_inc(mixed_ready, 1)

                def finish(n):
                    t = GT * n
                    xs = (x[:, t:t + GT, :] if static(t) else x[:, bass.ds(t, GT), :]).rearrange("p a n -> p (a n)")
                    dve.wait_ge(mlp_done, n + 1)
                    dve.scalar_tensor_tensor(out=xs, in0=psM[:].rearrange("p a n -> p (a n)"), scalar=RES / KS, in1=xs,
                                             op0=ALU.mult, op1=ALU.add).then_inc(mlp_added, 1)

                def first_residual(n):
                    for b in range(GT):
                        t = GT * n + b
                        dve.tensor_scalar(x1[:, b, :], tile_of(x, t), mean[:, one(t)], rstd[:, one(t)],
                                          ALU.subtract, ALU.mult)
                    dve.drain()
                    dve.wait_ge(attn_done, n + 1)
                    x1f = x1[:].rearrange("p a n -> p (a n)")
                    dve.scalar_tensor_tensor(out=x1f, in0=psX[:].rearrange("p a n -> p (a n)"), scalar=RES, in1=x1f,
                                             op0=ALU.mult, op1=ALU.add).then_inc(x1_ready, 1)
                    dve.drain()
                    t = GT * n
                    xs = (x[:, t:t + GT, :] if static(t) else x[:, bass.ds(t, GT), :]).rearrange("p a n -> p (a n)")
                    dve.tensor_tensor(xs, xs, x1f, ALU.add)

                def step(n, k):
                    if runs(n + 2):
                        normalise(n + 2)
                    if static(n) and n == -2:
                        for e, (w, parts) in enumerate(SPLIT):
                            dve.wait_ge(w_high, e + 1)
                            dve.scalar_tensor_tensor(out=parts[:, 1, :, :], in0=w, scalar=KS, in1=parts[:, 0, :, :],
                                                     op0=ALU.mult, op1=ALU.subtract).then_inc(weights_ready, 1)
                    if runs(n):
                        recurrence(n, k)
                    else:
                        middle_part(n)
                        late_part(n)
                    if runs(n - 2):
                        dve.drain()
                        finish(n - 2)
                run(dve, step)



def attention(nc, name, x, ident, identb, NT, SEQ, w, qk_dram, max_dram):
    wqk, bqk, wv, bv, woT, bo = w
    NH, HD = 16, 16
    B = NT * P // SEQ
    ST = SEQ // P
    NU = B * NH
    QPART = (0, 0, 0, 1, 2, 1)
    KPART = (0, 1, 2, 0, 0, 1)
    NP = len(QPART)
    ROWS = NP * HD
    MROW = ROWS
    ALLR = ROWS + 3
    SCALE = float(1.0 / np.sqrt(HD))
    KB = SEQ // 512
    VC = 32
    GT = 4
    GB = SEQ // (GT * P)
    with Chip(nc, name) as c:
        vaug = c.sb("vaug", [P, NU, ST, HD + 1])
        att = c.sb("att", [P, NU, ST, HD])
        with Chip(nc, name + "a") as a:
            mean, rstd = a.sb("mean", [P, NT]), a.sb("rstd", [P, NT])
            wqk_sb = a.sb("wqk", [P, DH, 2 * D])
            bqk_sb = a.sb("bqk", [P, 2 * DH])
            wv_sb = a.sb("wv", [P, DH, D])
            bv_sb = a.sb("bv", [1, D])
            ones = a.sb("ones", [1, P])
            y = a.sb("y", [P, GT, D])
            yT = a.sb("yT", [P, 2, DH, GT * P])
            qf = a.sb("qf", [P, 2 * DH, 512])
            rest = a.sb("rest", [P, 2, 512])
            parts = a.sb("parts", [P, 2 * DH, 3, 512], BF16)
            psT, psR, psV = a.ps("psT", [P, 512]), a.ps("psR", [P, 2 * DH, 512]), a.ps("psV", [P, 2, 512])
            w_in, consts, y_ready, turned, turn_copied, qk_done, qk_copied, split_ready, v_done, v_copied = (
                a.sem(n) for n in ("w_in", "consts", "y_ready", "turned", "turn_copied", "qk_done", "qk_copied",
                                   "split_ready", "v_done", "v_copied"))
            stored = [a.sem(f"stored{m}") for m in range(2 * DH)]

            def loads(sp):
                sp.dma_start(wqk_sb[:], wqk).then_inc(w_in, 16)
                sp.dma_start(bqk_sb[:], bqk).then_inc(w_in, 16)
                sp.dma_start(wv_sb[:], wv).then_inc(w_in, 16)
                sp.dma_start(bv_sb[:], bv).then_inc(w_in, 16)

            row_statistics(nc, name, x, NT, mean, rstd, loads)
            with nc.Block() as block:
                @block.gpsimd
                def _(pool):
                    pool.memset(ones[:], 1.0).then_inc(consts, 1)
                    pool.memset(vaug[:, :, :, HD:HD + 1], 1.0)

                @block.sync
                def _(sp):
                    with sp.Fori(0, B) as b:
                        for k in range(GB):
                            for m in range(2 * DH):
                                sp.wait_ge(split_ready, 2 * DH * (GB * b + k) + m + 1)
                                for part in range(3):
                                    sp.dma_start(qk_dram[m // DH, part, bass.ds(b * D + (m % DH) * P, P),
                                                         k * 512:(k + 1) * 512],
                                                 parts[:, m, part, :]).then_inc(stored[m], 16)
                    for m in range(2 * DH):
                        sp.wait_ge(stored[m], 16 * 3 * GB * B)

                @block.vector
                def _(dve):
                    with dve.Fori(0, B) as b:
                        for k in range(GB):
                            g = GB * b + k
                            for kk in ([0, 1] if k == 0 else [k + 1] if k + 1 < GB else []):
                                dve.wait_ge(turned, 2 * (GB * b + kk))
                                for q in range(GT):
                                    ins = dve.tensor_scalar(y[:, q, :], tile_of(x, (GB * b + kk) * GT + q),
                                                            mean[:, one((GB * b + kk) * GT + q)],
                                                            rstd[:, one((GB * b + kk) * GT + q)], ALU.subtract, ALU.mult)
                                ins.then_inc(y_ready, 1)
                            for m in range(0, 2 * DH, 2):
                                pair = slice(m, m + 2)
                                dve.wait_ge(qk_copied, 2 * DH * g + m + 2)
                                dve.tensor_tensor(rest[:], qf[:, pair, :], parts[:, pair, 0, :], ALU.subtract)
                                dve.drain()
                                dve.tensor_copy(parts[:, pair, 1, :], rest[:])
                                dve.drain()
                                dve.tensor_tensor(parts[:, pair, 2, :], rest[:], parts[:, pair, 1, :], ALU.subtract
                                                  ).then_inc(split_ready, 2)
                                dve.drain()

                @block.tensor
                def _(pe):
                    pe.wait_ge(w_in, 64)
                    pe.wait_ge(consts, 1)

                    def turn(g):
                        pe.wait_ge(y_ready, g + 1)
                        for half in range(2):
                            pe.wait_ge(turn_copied, 2 * g + half)
                            for hh in range(DH):
                                for q in range(2):
                                    mm = pe.transpose(psT[:, (2 * hh + q) * P:(2 * hh + q + 1) * P],
                                                      y[:, 2 * half + q, hh * P:(hh + 1) * P], ident[:])
                            mm.then_inc(turned, 1)

                    with pe.Fori(0, B) as b:
                        turn(GB * b)
                        for k in range(GB):
                            g = GB * b + k
                            pe.wait_ge(turn_copied, 2 * g + 2)
                            pe.wait_ge(qk_copied, 2 * DH * g)
                            for m in range(2 * DH):
                                for hh in range(DH):
                                    mm = pe.matmul(psR[:, m, :], wqk_sb[:, hh, m * P:(m + 1) * P], yT[:, k % 2, hh, :],
                                                   start=(hh == 0), stop=(hh == DH - 1))
                                mm.then_inc(qk_done, 1)
                            if k + 1 < GB:
                                turn(g + 1)
                            pe.wait_ge(v_copied, g)
                            for q in range(GT):
                                out = psV[:, q // 2, (q % 2) * D:(q % 2 + 1) * D]
                                for hh in range(DH):
                                    pe.matmul(out, yT[:, k % 2, hh, q * P:(q + 1) * P], wv_sb[:, hh, :],
                                              start=(hh == 0), stop=False)
                                mm = pe.matmul(out, ones[:], bv_sb[:], start=False, stop=True)
                            mm.then_inc(v_done, 1)

                @block.scalar
                def _(act):
                    def copy_turned(g, k):
                        for half in range(2):
                            act.wait_ge(turned, 2 * g + half + 1)
                            act.activation(yT[:, k % 2, :, 2 * half * P:2 * (half + 1) * P],
                                           psT[:].rearrange("p (h n) -> p h n", h=DH), ACT.Copy).then_inc(turn_copied, 1)

                    act.wait_ge(w_in, 64)
                    with act.Fori(0, B) as b:
                        copy_turned(GB * b, 0)
                        for k in range(GB):
                            g = GB * b + k
                            for m in range(2 * DH):
                                act.wait_ge(stored[m], 48 * g)
                                act.wait_ge(qk_done, 2 * DH * g + m + 1)
                                act.activation(qf[:, m, :], psR[:, m, :], ACT.Identity, bias=bqk_sb[:, m:m + 1])
                                act.activation(parts[:, m, 0, :], psR[:, m, :], ACT.Identity,
                                               bias=bqk_sb[:, m:m + 1]).then_inc(qk_copied, 1)
                            if k + 1 < GB:
                                copy_turned(g + 1, k + 1)
                            act.wait_ge(v_done, g + 1)
                            act.activation(vaug[:, bass.ds(NH * b, NH), GT * k:GT * (k + 1), 0:HD].rearrange("p n t e -> p t n e"),
                                           psV[:].rearrange("p a (t n e) -> p (a t) n e", n=NH, e=HD), ACT.Copy
                                           ).then_inc(v_copied, 1)

        RQ = 4
        RP = 4
        with Chip(nc, name + "b") as u_:
            qa = u_.sb("qa", [P, RQ, SEQ], BF16)
            ka = u_.sb("ka", [P, RQ, SEQ], BF16)
            vh = u_.sb("vh", [P, RQ, ST, VC])
            pt = u_.sb("pt", [P, RP, KB, 512])
            mx = u_.sb("mx", [P, ST, KB // 2])
            m = u_.sb("m", [P, ST])
            mr = u_.sb("mr", [P, ST])
            mcat = u_.sb("mcat", [P, P], BF16)
            mT = u_.sb("mT", [3 * ST, P], BF16)
            oS = u_.sb("oS", [P, 512])
            inv = u_.sb("inv", [P, KB, ST // KB])
            psA = u_.ps("psA", [P, 2, 1024])
            psE = u_.ps("psE", [P, 3, 512])
            psO = u_.ps("psO", [P, 512])
            rows_in = [u_.sem(f"rows_in{r}") for r in range(RQ)]
            (consts, scores_done, slot_read, m_ready, m_turned, m_stored, m_in, keys_done, exp_ready, pv_done,
             vh_ready, o_ready, o_copied, o_turned) = (
                u_.sem(n) for n in ("consts", "scores_done", "slot_read", "m_ready", "m_turned", "m_stored",
                                    "m_in", "keys_done", "exp_ready", "pv_done", "vh_ready", "o_ready", "o_copied",
                                    "o_turned"))
            LAG = 2
            HC = KB // 2

            AHEAD = 5
            T_MAX, T_OUT = ST - AHEAD + 2, 5

            def run(eng, step):
                for n in range(-2, RQ):
                    step(n, n // RQ, n % RQ)
                with eng.Fori(1, NU // RQ - 1) as i:
                    for r in range(RQ):
                        step(RQ * i + r, i, r)
                for n in range(NU - RQ, NU + 1):
                    step(n, n // RQ, n % RQ)

            def runs(n):
                return not static(n) or 0 <= n < NU

            def asked(n, t):
                return (1 if t < ST - AHEAD else 2), (t + AHEAD) % ST

            def asks(n, t):
                return runs(n + asked(n, t)[0])

            PER_STEP = HC * ST + 2

            def uses_before(n):
                if not static(n):
                    return PER_STEP * n + uses_before(RQ) - PER_STEP * RQ
                return sum(HC * sum(asks(e, t) for t in range(ST)) + runs(e + 1) + runs(e - 1) for e in range(-2, n))

            def use(n, t, k):
                inside = k + HC * sum(asks(n, e) for e in range(t)) + (runs(n + 1) if t > T_MAX else 0) + (runs(n - 1) if t > T_OUT else 0)
                slot = (uses_before(n if static(n) else RQ) + inside) % 2
                return uses_before(n) + inside, slot

            def turn_use(n, t):
                return use(n, t, HC if asks(n, t) else 0)

            def exp_slot(t, kb):
                return 1 if KB * t + kb == KB * ST - 1 else (KB * t + kb) % 3

            def exp_before(t, kb):
                j = KB * t + kb
                return {0: -3, 1: 0, 2: -1, KB * ST - 1: j - 1}.get(j, j - 2)

            assert KB * ST % 3 == 1

            with nc.Block() as block:
                @block.gpsimd
                def _(pool):
                    pool.memset(vh[:], 0.0).then_inc(consts, 1)
                    pool.wait_ge(consts, 1)
                    pool.memset(ka[MROW:ALLR, :, :], 1.0).then_inc(consts, 1)
                    pool.wait_ge(consts, 2)
                    pool.memset(mcat[:], 0.0).then_inc(consts, 1)
                    pool.wait_ge(consts, 3)

                    def step(n, i, r):
                        if runs(n + 1):
                            wait_count(pool, o_ready, n - 2)
                            src = vaug[:, n + 1, :, :] if static(n) else \
                                vaug[:, bass.ds(n + 1, 1), :, :].rearrange("p a t e -> p (a t) e")
                            pool.tensor_copy(vh[:, (r + 1) % RQ, :, 0:HD + 1], src).then_inc(vh_ready, 1)
                    run(pool, step)

                @block.sync
                def _(sp):
                    def step(n, i, r):
                        v = n + 3
                        rv = (r + 3) % RQ
                        for v, rv in ([(n + 2, (r + 2) % RQ), (v, rv)] if static(n) and n == -2 else [(v, rv)]):
                            if runs(v):
                                wait_count(sp, keys_done, KB * ST * (v - RQ + 1))
                                for which, dst, pick in ((0, qa, QPART), (1, ka, KPART)):
                                    for j, part in enumerate(pick):
                                        rows = slice(HD * v, HD * (v + 1)) if static(v) else bass.ds(HD * v, HD)
                                        sp.dma_start(dst[HD * j:HD * (j + 1), rv, :], qk_dram[which, part, rows, :]
                                                     ).then_inc(rows_in[rv], 16)
                        if runs(n + 1):
                            sp.wait_ge(slot_read, turn_use(n, T_MAX)[0] + 1)
                            wait_count(sp, m_in, 16 * (n + 1))
                            sp.dma_start(max_dram, mT[:]).then_inc(m_stored, 16)
                            sp.wait_ge(m_stored, 16 * (n + 2))
                            sp.dma_start(qa[MROW:ALLR, (r + 1) % RQ, :],
                                         max_dram.rearrange("(a t) s -> a (t s)", a=3)).then_inc(m_in, 16)
                    run(sp, step)

                @block.tensor
                def _(pe):
                    pe.wait_ge(consts, 3)

                    def by_query(n, t, r, i, hc):
                        after, st = asked(n, t)
                        i, r = i + (r + after) // RQ, (r + after) % RQ
                        if st == 0 and hc == 0:
                            pe.wait_ge(rows_in[r], 16 * 2 * NP * (i + 1))
                        before, slot = use(n, t, hc)
                        wait_count(pe, slot_read, before - 1)
                        for q in range(2):
                            kb = 2 * hc + q
                            mm = pe.matmul(psA[:, slot, q * 512:(q + 1) * 512],
                                           qa[0:ROWS, r, st * P:(st + 1) * P],
                                           ka[0:ROWS, r, kb * 512:(kb + 1) * 512], start=True, stop=True)
                        mm.then_inc(scores_done, 1)

                    def by_key(n, tt, r, kb):
                        if tt == 0 and kb == 0:
                            pe.wait_ge(m_in, 16 * (n + 1))
                        wait_count(pe, exp_ready, KB * ST * n + exp_before(tt, kb))
                        pe.matmul(psE[:, exp_slot(tt, kb), :], ka[0:ALLR, r, tt * P:(tt + 1) * P],
                                  qa[0:ALLR, r, kb * 512:(kb + 1) * 512], start=True, stop=True
                                  ).then_inc(keys_done, 1)

                    def values(n, tt, r):
                        if tt == 0:
                            pe.wait_ge(vh_ready, n + 1)
                            wait_count(pe, o_copied, n)
                        pe.wait_ge(exp_ready, KB * (ST * n + tt) + KB)
                        for kb in range(KB):
                            mm = pe.matmul(psO[VC * kb:VC * (kb + 1), :], vh[:, r, tt, :], pt[:, tt % RP, kb, :],
                                           start=(tt == 0), stop=(tt == ST - 1), tile_position=(0, VC * kb))
                        mm.then_inc(pv_done if tt < ST - 1 else o_ready, 1)

                    def turn_max(n):
                        pe.wait_ge(m_ready, n + 2)
                        before, slot = turn_use(n, T_MAX)
                        wait_count(pe, slot_read, before - 1)
                        pe.transpose(psA[:, slot, 0:P // 2].bitcast(BF16), mcat[:], identb[:]).then_inc(m_turned, 1)

                    def turn_out(n):
                        pe.wait_ge(o_copied, n)
                        before, slot = turn_use(n, T_OUT)
                        wait_count(pe, slot_read, before - 1)
                        for q in range(512 // P):
                            mm = pe.transpose(psA[:, slot, q * P:(q + 1) * P], oS[:, q * P:(q + 1) * P], ident[:])
                        mm.then_inc(o_turned, 1)

                    def step(n, i, r):
                        def keys(t, blocks):
                            if runs(n):
                                for kb in blocks:
                                    by_key(n, t, r, kb)

                        def queries(t, hc):
                            if asks(n, t):
                                by_query(n, t, r, i, hc)

                        for t in range(ST):
                            keys(t, (0, 1))
                            queries(t, 0)
                            keys(t, range(2, KB - 1))
                            if t < LAG and runs(n - 1):
                                values(n - 1, ST - LAG + t, (r - 1) % RQ)
                            if t >= LAG and runs(n):
                                values(n, t - LAG, r)
                            keys(t, (KB - 1,))
                            queries(t, 1)
                            if t == T_MAX and runs(n + 1):
                                turn_max(n)
                            if t == T_OUT and runs(n - 1):
                                turn_out(n)
                    run(pe, step)

                @block.scalar
                def _(act):
                    act.wait_ge(consts, 3)

                    def step(n, i, r):
                        for t in range(ST):
                            if runs(n):
                                if t >= RP:
                                    wait_count(act, pv_done, (ST - 1) * n + t - RP + 1)
                                elif t == RP - 1:
                                    wait_count(act, o_ready, n)
                                else:
                                    wait_count(act, pv_done, (ST - 1) * (n - 1) + ST - RP + t + 1)
                                for kb in range(KB):
                                    act.wait_ge(keys_done, KB * (ST * n + t) + kb + 1)
                                    act.activation(pt[:, t % RP, kb, :], psE[:, exp_slot(t, kb), :], ACT.Exp, scale=SCALE
                                                   ).then_inc(exp_ready, 1)
                            if t == 1 and runs(n - 1):
                                act.wait_ge(o_ready, n)
                                wait_count(act, o_turned, n - 1)
                                act.activation(oS[:], psO[:], ACT.Copy).then_inc(o_copied, 1)
                    run(act, step)

                @block.vector
                def _(dve):
                    dve.wait_ge(consts, 3)
                    part_of = lambda j: mcat[:, j * ST:(j + 1) * ST]

                    def maxima(v, piece):
                        if piece in range(5):
                            dve.drain()
                        if piece == 0:
                            dve.tensor_reduce(m[:], mx[:], AX_X, ALU.max)
                            dve.drain()
                        elif piece == 1:
                            wait_count(dve, m_turned, v)
                            dve.tensor_scalar(part_of(0), m[:], -1.0, None, ALU.mult)
                        elif piece == 2:
                            dve.scalar_tensor_tensor(out=mr[:], in0=m[:], scalar=-1.0, in1=part_of(0),
                                                     op0=ALU.mult, op1=ALU.subtract)
                        elif piece == 3:
                            dve.tensor_copy(part_of(1), mr[:])
                        elif piece == 4:
                            dve.tensor_tensor(part_of(2), mr[:], part_of(1), ALU.subtract).then_inc(m_ready, 1)

                    def step(n, i, r):
                        for t in range(ST):
                            if asks(n, t):
                                after, st = asked(n, t)
                            for hc in range(HC):
                                if asks(n, t):
                                    dve.wait_ge(scores_done, HC * (ST * (n + after) + st) + hc + 1)
                                    dve.tensor_reduce(mx[:, st, hc:hc + 1], psA[:, use(n, t, hc)[1], :], AX_X, ALU.max
                                                      ).then_inc(slot_read, 1)
                                if runs(n + 1):
                                    maxima(n + 1, HC * (t - ST + AHEAD) + hc + 1)
                            if t == T_MAX and runs(n + 1):
                                wait_count(dve, m_stored, 16 * (n + 1))
                                dve.wait_ge(m_turned, n + 2)
                                dve.tensor_copy(mT[:], psA[0:3 * ST, turn_use(n, t)[1], 0:P // 2].bitcast(BF16)
                                                ).then_inc(slot_read, 1)
                            if t == T_OUT and runs(n - 1):
                                dve.drain()
                                dve.wait_ge(o_turned, n)
                                ov = psA[:, turn_use(n, t)[1], 0:512].rearrange(
                                    "p (q j e) -> p j q e", j=KB, e=VC)
                                dve.reciprocal(inv[:], ov[:, :, :, HD])
                                dve.drain()
                                dst = (att[:, n - 1, :, :] if static(n) else
                                       att[:, bass.ds(n - 1, 1), :, :].rearrange("p a t e -> p (a t) e"))
                                dve.tensor_tensor(dst.rearrange("p (j q) e -> p j q e", j=KB), ov[:, :, :, 0:HD],
                                                  inv[:].unsqueeze(3).broadcast_to([P, KB, ST // KB, HD]), ALU.mult
                                                  ).then_inc(slot_read, 1)
                    run(dve, step)

        with Chip(nc, name + "c") as o:
            wo_sb = o.sb("wo", [P, DH, D])
            bo_sb = o.sb("bo", [1, D])
            ones = o.sb("ones", [1, P])
            ag = o.sb("ag", [P, 2, D])
            aT = o.sb("aT", [P, 2, DH, P])
            psT, psY = o.ps("psT", [P, 2, 512]), o.ps("psY", [P, 2, 512])
            w_in, consts, gathered, turned, turn_copied, projected, added = (
                o.sem(n) for n in ("w_in", "consts", "gathered", "turned", "turn_copied", "projected", "added"))
            with nc.Block() as block:
                @block.gpsimd
                def _(pool):
                    pool.memset(ones[:], 1.0).then_inc(consts, 1)

                @block.sync
                def _(sp):
                    sp.dma_start(wo_sb[:], woT).then_inc(w_in, 16)
                    sp.dma_start(bo_sb[:], bo).then_inc(w_in, 16)

                def run(eng, step):
                    for b in range(B):
                        if b == 0:
                            step(0, 0, 0, 0)
                            step(1, 1, 0, 1)
                        with eng.Fori(1 if b == 0 else 0, ST // 2) as i:
                            for k in range(2):
                                step(b * ST + 2 * i + k, k, b, 2 * i + k)

                @block.vector
                def _(dve):
                    def gather(t, k, b, st):
                        src = att[:, b * NH:(b + 1) * NH, one(st), :].rearrange("p n t e -> p n (t e)")
                        wait_count(dve, turned, t - 1)
                        dve.tensor_copy(ag[:, k, :].rearrange("p (n e) -> p n e", n=NH), src).then_inc(gathered, 1)

                    def add(t, k, b, st):
                        dve.wait_ge(projected, t + 1)
                        xt = tile_of(x, t)
                        dve.tensor_tensor(xt, psY[:, k, 0:D], xt, ALU.add).then_inc(added, 1)

                    def both(t, k, b, st):
                        gather(t, k, b, st)
                        if not static(t) or t > 1:
                            add(t - 2, k, b, st)
                    run(dve, both)
                    add(NT - 2, 0, 0, 0)
                    add(NT - 1, 1, 0, 0)

                @block.tensor
                def _(pe):
                    pe.wait_ge(w_in, 32)
                    pe.wait_ge(consts, 1)

                    def turn(t, k, b, st):
                        pe.wait_ge(gathered, t + 1)
                        wait_count(pe, turn_copied, t - 1)
                        for hh in range(DH):
                            mm = pe.transpose(psT[:, k, hh * P:(hh + 1) * P], ag[:, k, hh * P:(hh + 1) * P], ident[:])
                        mm.then_inc(turned, 1)

                    def project(t, k, b, st):
                        pe.wait_ge(turn_copied, t + 1)
                        wait_count(pe, added, t - 1)
                        for hh in range(DH):
                            pe.matmul(psY[:, k, 0:D], aT[:, k, hh, :], wo_sb[:, hh, :], start=(hh == 0), stop=False)
                        pe.matmul(psY[:, k, 0:D], ones[:], bo_sb[:], start=False, stop=True).then_inc(projected, 1)

                    def step(t, k, b, st):
                        turn(t, k, b, st)
                        if not static(t) or t > 0:
                            project(t - 1, 1 - k, b, st)
                    run(pe, step)
                    project(NT - 1, 1, 0, 0)

                @block.scalar
                def _(act):
                    def step(t, k, b, st):
                        act.wait_ge(turned, t + 1)
                        wait_count(act, projected, t - 1)
                        act.activation(aT[:, k, :, :].rearrange("p h n -> p (h n)"), psT[:, k, 0:D], ACT.Copy
                                       ).then_inc(turn_copied, 1)
                    run(act, step)


def dram_tile(d, t):
    return d[t, :, :] if static(t) else d[bass.ds(t, 1), :, :].rearrange("a p n -> (a p) n")


def keys_layout(keys):
    h, nk, p, kd = keys.shape
    return np.ascontiguousarray(keys.transpose(3, 2, 0, 1).reshape(kd, p * h, nk))


def halves_layout(v):
    return np.ascontiguousarray(v.reshape(-1, P).T)


def key_in_layout(key_in):
    ne, d = key_in.shape
    return np.ascontiguousarray(key_in.reshape(P, ne // P, d // P, P).transpose(3, 2, 1, 0).reshape(P, d // P, ne))


def rows_layout(w):
    return np.ascontiguousarray(w.reshape(-1, P, w.shape[1]).transpose(1, 0, 2))


def head_cols(w):
    return w.transpose(1, 0, 2).reshape(w.shape[1], -1)


SEQ = 2048


def build(nc, a, out, qk_dram, max_dram, yT_dram):
    tokens = out.rearrange("b s d -> (b s) d").rearrange("(t p) d -> p t d", p=P)
    x_in = a["x"].rearrange("b s d -> (b s) d").rearrange("(t p) d -> p t d", p=P)
    NT = tokens.shape[1]
    peer = tuple(a[n] for n in ("gamma", "beta", "w_q", "keysT", "key_inT", "key_out"))
    mix = tuple(a[n] for n in ("norm1", "norm2", "in_projT", "out_projT", "fcT", "projT"))
    moe = tuple(a[n] for n in ("gate_W", "gate_b", "expert_W", "expert_b"))
    att = tuple(a[n] for n in ("wqk", "bqk", "wv", "bv", "woT", "bo"))
    with Chip(nc, "all") as c:
        x = c.sb("x", [P, NT, D])
        ident, ident16, identb = c.sb("ident", [P, P]), c.sb("ident16", [P, P], F16), c.sb("identb", [P, P], BF16)
        make_identities(nc, ident, ident16, identb)
        peer_ffn(nc, "peer0", x, ident, ident16, NT, peer, yT_dram, x_in)
        recurrent_block(nc, "mix", x, ident, NT, SEQ, mix)
        peer_ffn(nc, "peer1", x, ident, ident16, NT, peer, yT_dram)
        moe_ffn(nc, "moe0", x, ident, NT, moe)
        attention(nc, "att", x, ident, identb, NT, SEQ, att, qk_dram, max_dram)
        moe_ffn(nc, "moe1", x, ident, NT, moe, tokens)


def kernel(L0_attn_x, L0_attn_norm1_w, L0_attn_norm2_w, L0_attn_in_proj_w, L0_attn_out_proj_w, L0_attn_fc_w,
           L0_attn_proj_w, L0_ffn_gamma, L0_ffn_beta, L0_ffn_w_q, L0_ffn_keys, L0_ffn_key_in, L0_ffn_key_out,
           L1_attn_wq, L1_attn_bq, L1_attn_wk, L1_attn_bk, L1_attn_wv, L1_attn_bv, L1_attn_wo, L1_attn_bo,
           L1_ffn_gate_W, L1_ffn_gate_b, L1_ffn_expert_W, L1_ffn_expert_b):
    import concourse.bacc as bacc
    from concourse.bass_utils import run_bass_kernel_spmd as run

    arrays = {
        "x": L0_attn_x,
        "gamma": halves_layout(L0_ffn_gamma), "beta": halves_layout(L0_ffn_beta), "w_q": L0_ffn_w_q,
        "keysT": keys_layout(L0_ffn_keys), "key_inT": key_in_layout(L0_ffn_key_in), "key_out": L0_ffn_key_out,
        "norm1": halves_layout(L0_attn_norm1_w), "norm2": halves_layout(L0_attn_norm2_w),
        "in_projT": rows_layout(L0_attn_in_proj_w.T), "out_projT": rows_layout(L0_attn_out_proj_w.T),
        "fcT": rows_layout(L0_attn_fc_w.T), "projT": rows_layout(L0_attn_proj_w.T),
        "gate_W": L1_ffn_gate_W, "gate_b": L1_ffn_gate_b, "expert_W": L1_ffn_expert_W, "expert_b": L1_ffn_expert_b,
        "wqk": rows_layout(np.concatenate([head_cols(L1_attn_wq), head_cols(L1_attn_wk)], axis=1)),
        "bqk": halves_layout(np.concatenate([L1_attn_bq.reshape(-1), L1_attn_bk.reshape(-1)])),
        "wv": rows_layout(head_cols(L1_attn_wv)), "bv": L1_attn_bv.reshape(1, -1),
        "woT": rows_layout(L1_attn_wo.T), "bo": L1_attn_bo.reshape(1, -1),
    }
    arrays = {n: np.ascontiguousarray(v) for n, v in arrays.items()}
    nc = bacc.Bacc("TRN2", target_bir_lowering=False, num_devices=1)
    aps = {n: nc.dram_tensor(f"in_{n}", v.shape, mybir.dt.from_np(v.dtype), kind="ExternalInput").ap()
           for n, v in arrays.items()}
    shape = L0_attn_x.shape
    out = nc.dram_tensor("out", shape, F32, kind="ExternalOutput").ap()
    tokens = shape[0] * shape[1]
    qk_dram = nc.dram_tensor("qk_scratch", (2, 3, tokens // SEQ * D, SEQ), BF16, kind="Internal").ap()
    max_dram = nc.dram_tensor("max_scratch", (3 * SEQ // P, P), BF16, kind="Internal").ap()
    yT_dram = nc.dram_tensor("yT_scratch", (tokens // P, P, D), F32, kind="Internal").ap()
    build(nc, aps, out, qk_dram, max_dram, yT_dram)
    r = run(nc, [{f"in_{n}": v for n, v in arrays.items()}], core_ids=[0])
    return r.results[0]["out"]
```
